# Optimizing a Trainium2 kernel written in Bass

```python
import numpy as np
import jax
import jax.numpy as jnp

def _softmax(x, axis=-1):
    return jax.nn.softmax(x, axis=axis)

def _gelu(x):
    return jax.nn.gelu(x, approximate=True)

def _silu(x):
    return jax.nn.silu(x)

def _sigmoid(x):
    return jax.nn.sigmoid(x)

def _layernorm(x, axis=-1, eps=1e-05):
    m = jnp.mean(x, axis=axis, keepdims=True)
    v = jnp.var(x, axis=axis, keepdims=True)
    return (x - m) / jnp.sqrt(v + eps)

def _scatter_add(tgt, idx, src, axis=0):
    return tgt.at[idx].add(src)

def _segment_sum(src, seg, n):
    return jax.ops.segment_sum(src, seg, n)
kernel_name = 'mk_gnn_ffn_d2_gnn_r32_da4e1a'

def setup_inputs(seed: int=0):
    np.random.seed(seed)
    _w = jnp.asarray

    def _rec_inputs():
        import jax
        import jax.numpy as jnp
        _gk = jax.random.key(seed)
        x = -0.0005963 + 1.001 * jax.random.normal(jax.random.fold_in(_gk, 1), (96, 1024), jnp.float32)
        _s = jax.random.randint(jax.random.fold_in(_gk, 2), (768,), 0, 96, jnp.int32)
        _d = jax.random.randint(jax.random.fold_in(_gk, 3), (768,), 0, 96, jnp.int32)
        _loop = jnp.arange(96, dtype=jnp.int32)
        src = jnp.concatenate([_s, _d, _loop])
        dst = jnp.concatenate([_d, _s, _loop])
        _o = jnp.argsort(dst, stable=True)
        src = src[_o]
        dst = dst[_o]
        edge_type_5 = jax.random.randint(jax.random.fold_in(_gk, 12), (1632,), 0, 5, jnp.int32)
        return (x, src, dst, edge_type_5)
    x, src, dst, edge_type_5 = _rec_inputs()

    def _L0_gnn_setup():
        import jax, jax.numpy as jnp
        import numpy as np
        N = 96
        E = 3072
        IN_F = 1024
        OUT_F = 1024
        H = 16
        D = OUT_F // H
        NUM_ETYPES = 4

        def _build_mask(edge_index, edge_type, edge_type_weights, dtype):
            src, dst = (edge_index[0], edge_index[1])
            w = jax.nn.softplus(edge_type_weights)
            mask = jnp.full((N, N), -jnp.inf, dtype=dtype)
            mask = mask.at[src, dst].set(w[edge_type - 1])
            diag = jnp.diagonal(mask)
            idx = jnp.arange(N)
            mask = mask.at[idx, idx].set(jnp.where(jnp.isneginf(diag), w[3], diag))
            return mask
        key = jax.random.key(seed)
        ks = jax.random.split(key, 20)
        p = lambda k, shape: jax.random.normal(k, shape, dtype=jnp.float32) * 0.02
        return {'x': jax.random.normal(ks[0], (N, IN_F), dtype=jnp.float32), 'edge_index': jax.random.randint(ks[1], (2, E), 0, N), 'edge_type': jax.random.randint(ks[2], (E,), 1, NUM_ETYPES + 1), 'edge_type_weights': jnp.ones((NUM_ETYPES,), jnp.float32) + 0.1 * jax.random.normal(ks[3], (NUM_ETYPES,), dtype=jnp.float32), 'wq': p(ks[4], (OUT_F, IN_F)), 'bq': p(ks[5], (OUT_F,)), 'wk': p(ks[6], (OUT_F, IN_F)), 'bk': p(ks[7], (OUT_F,)), 'wv': p(ks[8], (OUT_F, IN_F)), 'bv': p(ks[9], (OUT_F,)), 'wiq': p(ks[10], (OUT_F, OUT_F)), 'biq': p(ks[11], (OUT_F,)), 'wik': p(ks[12], (OUT_F, OUT_F)), 'bik': p(ks[13], (OUT_F,)), 'wiv': p(ks[14], (OUT_F, OUT_F)), 'biv': p(ks[15], (OUT_F,)), 'wo': p(ks[16], (OUT_F, OUT_F)), 'bo': p(ks[17], (OUT_F,))}
    _L0_gnn_all = _L0_gnn_setup()
    _L0_gnn_in = {k: v for k, v in _L0_gnn_all.items() if k in ('edge_type_weights', 'wq', 'bq', 'wk', 'bk', 'wv', 'bv', 'wiq', 'biq', 'wik', 'bik', 'wiv', 'biv', 'wo', 'bo')}
    del _L0_gnn_all

    def _L0_ffn_setup():
        import jax, jax.numpy as jnp
        import numpy as np
        D_MODEL = 1024
        EXPANSION = 4
        D_HIDDEN = D_MODEL * EXPANSION
        NUM_STAGES = int(np.log2(D_HIDDEN))

        def butterfly(y, weights, dim):
            lead = y.shape[:-1]
            for stage in range(weights.shape[0]):
                s = 2 ** stage
                nb = dim // (2 * s)
                yr = y.reshape(*lead, nb, 2, s)
                a = yr[..., 0, :]
                b = yr[..., 1, :]
                w = weights[stage].reshape(nb, s, 2, 2)
                na = w[..., 0, 0] * a + w[..., 0, 1] * b
                nb2 = w[..., 1, 0] * a + w[..., 1, 1] * b
                y = jnp.stack([na, nb2], axis=-2).reshape(*lead, dim)
            return y
        key = jax.random.key(seed)
        ks = jax.random.split(key, 6)
        B, S = (4, 64)
        x = jax.random.normal(ks[0], (B, S, D_MODEL), jnp.float32)
        W_exp = jax.random.normal(ks[1], (D_MODEL, D_HIDDEN), jnp.float32) * 0.02
        b_exp = jnp.zeros((D_HIDDEN,), jnp.float32)
        up_weights = jax.random.normal(ks[2], (NUM_STAGES, D_HIDDEN // 2, 2, 2), jnp.float32) * 0.02
        up_bias = jnp.zeros((D_HIDDEN,), jnp.float32)
        down_weights = jax.random.normal(ks[3], (NUM_STAGES, D_HIDDEN // 2, 2, 2), jnp.float32) * 0.02
        W_con = jax.random.normal(ks[4], (D_HIDDEN, D_MODEL), jnp.float32) * 0.02
        b_con = jnp.zeros((D_MODEL,), jnp.float32)
        down_bias = jnp.zeros((D_MODEL,), jnp.float32)
        return dict(x=x, W_exp=W_exp, b_exp=b_exp, up_weights=up_weights, up_bias=up_bias, down_weights=down_weights, W_con=W_con, b_con=b_con, down_bias=down_bias)
    _L0_ffn_all = _L0_ffn_setup()
    _L0_ffn_in = {k: v for k, v in _L0_ffn_all.items() if k in ('W_exp', 'b_exp', 'up_weights', 'up_bias', 'down_weights', 'W_con', 'b_con', 'down_bias')}
    del _L0_ffn_all

    def _L1_gnn_setup():
        import jax, jax.numpy as jnp
        import numpy as np
        N = 625
        E = 10000
        IN = 1024
        HID = 256
        H = 4
        D = HID // H
        OUT = 1024
        EPS = 1e-06
        NEG_SLOPE = 0.2
        key = jax.random.key(seed)
        ks = jax.random.split(key, 8)
        x = jax.random.normal(ks[0], (N, IN), dtype=jnp.float32)
        edge_index = jax.random.randint(ks[1], (2, E), 0, N, dtype=jnp.int64)
        s = 0.02
        return {'x': x, 'edge_index': edge_index, 'rms_w': jnp.ones((IN,), dtype=jnp.float32), 'W_down': jax.random.normal(ks[2], (IN, HID), dtype=jnp.float32) * s, 'Wl': jax.random.normal(ks[3], (HID, HID), dtype=jnp.float32) * s, 'Wr': jax.random.normal(ks[4], (HID, HID), dtype=jnp.float32) * s, 'att': jax.random.normal(ks[5], (H, D), dtype=jnp.float32) * s, 'W_up': jax.random.normal(ks[6], (HID, OUT), dtype=jnp.float32) * s}
    _L1_gnn_all = _L1_gnn_setup()
    _L1_gnn_in = {k: v for k, v in _L1_gnn_all.items() if k in ('rms_w', 'W_down', 'Wl', 'Wr', 'att', 'W_up')}
    del _L1_gnn_all

    def _L1_ffn_setup():
        import jax, jax.numpy as jnp
        import numpy as np
        R = 64
        key = jax.random.key(seed)
        k1, k2, k3 = jax.random.split(key, 3)
        B, S, D_IN, D_OUT = (8, 128, 1024, 1024)
        x = jax.random.normal(k1, (B, S, D_IN), dtype=jnp.float32)
        weight = jax.random.normal(k2, (D_OUT, D_IN), dtype=jnp.float32) * (1.0 / np.sqrt(D_IN))
        disha = jax.random.normal(k3, (R, D_OUT), dtype=jnp.float32) * 0.01
        return {'x': x, 'weight': weight, 'disha': disha}
    _L1_ffn_all = _L1_ffn_setup()
    _L1_ffn_in = {k: v for k, v in _L1_ffn_all.items() if k in ('weight', 'disha')}
    del _L1_ffn_all
    return {'x': x, 'src': src, 'dst': dst, 'edge_type_5': edge_type_5, 'L0_gnn_edge_type_weights': _L0_gnn_in['edge_type_weights'], 'L0_gnn_wq': _L0_gnn_in['wq'], 'L0_gnn_bq': _L0_gnn_in['bq'], 'L0_gnn_wk': _L0_gnn_in['wk'], 'L0_gnn_bk': _L0_gnn_in['bk'], 'L0_gnn_wv': _L0_gnn_in['wv'], 'L0_gnn_bv': _L0_gnn_in['bv'], 'L0_gnn_wiq': _L0_gnn_in['wiq'], 'L0_gnn_biq': _L0_gnn_in['biq'], 'L0_gnn_wik': _L0_gnn_in['wik'], 'L0_gnn_bik': _L0_gnn_in['bik'], 'L0_gnn_wiv': _L0_gnn_in['wiv'], 'L0_gnn_biv': _L0_gnn_in['biv'], 'L0_gnn_wo': _L0_gnn_in['wo'], 'L0_gnn_bo': _L0_gnn_in['bo'], 'L0_ffn_W_exp': _L0_ffn_in['W_exp'], 'L0_ffn_b_exp': _L0_ffn_in['b_exp'], 'L0_ffn_up_weights': _L0_ffn_in['up_weights'], 'L0_ffn_up_bias': _L0_ffn_in['up_bias'], 'L0_ffn_down_weights': _L0_ffn_in['down_weights'], 'L0_ffn_W_con': _L0_ffn_in['W_con'], 'L0_ffn_b_con': _L0_ffn_in['b_con'], 'L0_ffn_down_bias': _L0_ffn_in['down_bias'], 'L1_gnn_rms_w': _L1_gnn_in['rms_w'], 'L1_gnn_W_down': _L1_gnn_in['W_down'], 'L1_gnn_Wl': _L1_gnn_in['Wl'], 'L1_gnn_Wr': _L1_gnn_in['Wr'], 'L1_gnn_att': _L1_gnn_in['att'], 'L1_gnn_W_up': _L1_gnn_in['W_up'], 'L1_ffn_weight': _L1_ffn_in['weight'], 'L1_ffn_disha': _L1_ffn_in['disha']}

def reference(x, src, dst, edge_type_5, L0_gnn_edge_type_weights, L0_gnn_wq, L0_gnn_bq, L0_gnn_wk, L0_gnn_bk, L0_gnn_wv, L0_gnn_bv, L0_gnn_wiq, L0_gnn_biq, L0_gnn_wik, L0_gnn_bik, L0_gnn_wiv, L0_gnn_biv, L0_gnn_wo, L0_gnn_bo, L0_ffn_W_exp, L0_ffn_b_exp, L0_ffn_up_weights, L0_ffn_up_bias, L0_ffn_down_weights, L0_ffn_W_con, L0_ffn_b_con, L0_ffn_down_bias, L1_gnn_rms_w, L1_gnn_W_down, L1_gnn_Wl, L1_gnn_Wr, L1_gnn_att, L1_gnn_W_up, L1_ffn_weight, L1_ffn_disha):
    import jax
    import jax.numpy as jnp

    def _L0_gnn_ref(x, edge_index, edge_type, edge_type_weights, wq, bq, wk, bk, wv, bv, wiq, biq, wik, bik, wiv, biv, wo, bo):
        import jax, jax.numpy as jnp
        import numpy as np
        N = 96
        E = 3072
        IN_F = 1024
        OUT_F = 1024
        H = 16
        D = OUT_F // H
        NUM_ETYPES = 4

        def _build_mask(edge_index, edge_type, edge_type_weights, dtype):
            src, dst = (edge_index[0], edge_index[1])
            w = jax.nn.softplus(edge_type_weights)
            mask = jnp.full((N, N), -jnp.inf, dtype=dtype)
            mask = mask.at[src, dst].set(w[edge_type - 1])
            diag = jnp.diagonal(mask)
            idx = jnp.arange(N)
            mask = mask.at[idx, idx].set(jnp.where(jnp.isneginf(diag), w[3], diag))
            return mask
        q = x @ wq.T + bq
        k = x @ wk.T + bk
        v = x @ wv.T + bv
        q2 = (q @ wiq.T + biq).reshape(N, H, D).transpose(1, 0, 2)
        k2 = (k @ wik.T + bik).reshape(N, H, D).transpose(1, 0, 2)
        v2 = (v @ wiv.T + biv).reshape(N, H, D).transpose(1, 0, 2)
        mask = _build_mask(edge_index, edge_type, edge_type_weights, x.dtype)
        scale = 1.0 / np.sqrt(D).astype(np.float32)
        scores = jnp.einsum('hnd,hmd->hnm', q2, k2) * scale + mask[None]
        attn = jax.nn.softmax(scores, axis=-1)
        out = jnp.einsum('hnm,hmd->hnd', attn, v2)
        out = out.transpose(1, 0, 2).reshape(N, OUT_F)
        return out @ wo.T + bo

    def _L0_ffn_ref(x, W_exp, b_exp, up_weights, up_bias, down_weights, W_con, b_con, down_bias):
        import jax, jax.numpy as jnp
        import numpy as np
        D_MODEL = 1024
        EXPANSION = 4
        D_HIDDEN = D_MODEL * EXPANSION
        NUM_STAGES = int(np.log2(D_HIDDEN))

        def butterfly(y, weights, dim):
            lead = y.shape[:-1]
            for stage in range(weights.shape[0]):
                s = 2 ** stage
                nb = dim // (2 * s)
                yr = y.reshape(*lead, nb, 2, s)
                a = yr[..., 0, :]
                b = yr[..., 1, :]
                w = weights[stage].reshape(nb, s, 2, 2)
                na = w[..., 0, 0] * a + w[..., 0, 1] * b
                nb2 = w[..., 1, 0] * a + w[..., 1, 1] * b
                y = jnp.stack([na, nb2], axis=-2).reshape(*lead, dim)
            return y
        h = jnp.einsum('bsd,dh->bsh', x, W_exp) + b_exp
        h = butterfly(h, up_weights, D_HIDDEN)
        h = jax.nn.gelu(h + up_bias, approximate=False)
        h = butterfly(h, down_weights, D_HIDDEN)
        y = jnp.einsum('bsh,hd->bsd', h, W_con) + b_con
        return y + down_bias

    def _L1_gnn_ref(x, edge_index, rms_w, W_down, Wl, Wr, att, W_up):
        import jax, jax.numpy as jnp
        import numpy as np
        N = 625
        E = 10000
        IN = 1024
        HID = 256
        H = 4
        D = HID // H
        OUT = 1024
        EPS = 1e-06
        NEG_SLOPE = 0.2
        n = x.shape[0]
        ms = jnp.mean(jnp.square(x), axis=-1, keepdims=True)
        x = x * jax.lax.rsqrt(ms + EPS) * rms_w
        x = x @ W_down
        loop = jnp.arange(n, dtype=edge_index.dtype)
        src = jnp.concatenate([edge_index[0], loop])
        dst = jnp.concatenate([edge_index[1], loop])
        xl = (x @ Wl).reshape(n, H, D)
        xr = (x @ Wr).reshape(n, H, D)
        msg = xl[src] + xr[dst]
        act = jnp.where(msg > 0, msg, NEG_SLOPE * msg)
        e = jnp.einsum('ehd,hd->eh', act, att)
        m = jax.ops.segment_max(e, dst, num_segments=n)
        p = jnp.exp(e - m[dst])
        denom = jax.ops.segment_sum(p, dst, num_segments=n)
        alpha = p / (denom[dst] + 1e-16)
        out = jax.ops.segment_sum(alpha[..., None] * xl[src], dst, num_segments=n)
        out = out.reshape(n, HID)
        return out @ W_up

    def _L1_ffn_ref(x, weight, disha):
        import jax, jax.numpy as jnp
        import numpy as np
        R = 64
        result = jnp.einsum('bsd,od->bso', x, weight)
        r = disha.shape[0]
        pooled = x.reshape(*x.shape[:-1], x.shape[-1] // r, r).sum(axis=-2)
        return result + pooled @ disha
    edge_index = jnp.stack([src, dst])
    x = x + _L0_gnn_ref(_layernorm(x, axis=-1), edge_index, edge_type_5, L0_gnn_edge_type_weights, L0_gnn_wq, L0_gnn_bq, L0_gnn_wk, L0_gnn_bk, L0_gnn_wv, L0_gnn_bv, L0_gnn_wiq, L0_gnn_biq, L0_gnn_wik, L0_gnn_bik, L0_gnn_wiv, L0_gnn_biv, L0_gnn_wo, L0_gnn_bo)
    x = x + _L0_ffn_ref(_layernorm(x, axis=-1)[None], L0_ffn_W_exp, L0_ffn_b_exp, L0_ffn_up_weights, L0_ffn_up_bias, L0_ffn_down_weights, L0_ffn_W_con, L0_ffn_b_con, L0_ffn_down_bias)[0]
    x = x + _L1_gnn_ref(_layernorm(x, axis=-1), edge_index, L1_gnn_rms_w, L1_gnn_W_down, L1_gnn_Wl, L1_gnn_Wr, L1_gnn_att, L1_gnn_W_up)
    x = x + _L1_ffn_ref(_layernorm(x, axis=-1)[None], L1_ffn_weight, L1_ffn_disha)[0]
    return x

_drawn_inputs = setup_inputs


def setup_inputs(seed=0):
    import zlib

    import numpy as np

    out = dict(_drawn_inputs(seed))
    spreads = {'L0_ffn_b_exp': (0.0, 0.1),
     'L0_ffn_up_bias': (0.0, 0.1),
     'L0_ffn_b_con': (0.0, 0.1),
     'L0_ffn_down_bias': (0.0, 0.1),
     'L1_gnn_rms_w': (1.0, 0.6)}
    factors = {'L0_gnn_edge_type_weights': 38.616,
     'L0_gnn_wq': 6.198,
     'L0_gnn_bq': 8.0,
     'L0_gnn_wk': 6.215,
     'L0_gnn_bk': 64.0,
     'L0_gnn_bv': 8.0,
     'L0_gnn_wiq': 6.235,
     'L0_gnn_biq': 8.0,
     'L0_gnn_wik': 6.186,
     'L0_gnn_bik': 64.0,
     'L0_gnn_biv': 5.357,
     'L0_gnn_bo': 3.449,
     'L1_gnn_W_down': 3.291,
     'L1_gnn_Wl': 3.211,
     'L1_gnn_Wr': 8.0,
     'L1_gnn_att': 8.0,
     'L1_gnn_W_up': 3.228}
    for name, (base, spread) in spreads.items():
        noise = np.random.default_rng([zlib.crc32(name.encode()), seed]).standard_normal(out[name].shape)
        drawn = base * np.exp(spread * noise) if base else spread * noise
        out[name] = jnp.asarray(drawn.astype(out[name].dtype))
    for name, factor in factors.items():
        out[name] = (out[name] * factor).astype(out[name].dtype)
    return out
```

```python
from contextlib import ExitStack

import concourse.bass as bass
from concourse import mybir

F32 = mybir.dt.float32
I32 = mybir.dt.int32
BF16 = mybir.dt.bfloat16
ALU = mybir.AluOpType
ACT = mybir.ActivationFunctionType
AX = mybir.AxisListType

P = 128
BANK = 512
T = 96
D = 1024
KD = D // P
HID = 4096
HEADS, HD = 16, 64
E = 1632
ET = (E + P - 1) // P
EP = ET * P
EL = EP + T
LT = ET + 1
G1 = 256
H1 = 4
SLOTS = 4
SLAB = 4096
STAGES = 6
GRP = 64
NT = HID // P
COEF = GRP * 2 * GRP
BIG = 1.0e30
LN_EPS, RMS_EPS = 1e-5, 1e-6
GNN = ["q", "k", "iq", "ik", "v", "iv", "o"]
GNN_SLABS = 2 * len(GNN)
EXP_SLABS = 8
CON_SLABS = 8
STREAM = GNN_SLABS + EXP_SLABS + CON_SLABS


def program(nc, A, out):
    with ExitStack() as ctx:
        def sb(name, shape, dt=F32):
            return ctx.enter_context(nc.sbuf_tensor(name, shape, dt))

        def sem(name):
            return ctx.enter_context(nc.semaphore(name))

        ring = sb("ring", [P, SLOTS, SLAB])
        mix = sb("mix", [P, 4, NT * GRP])
        UV = sb("UV", [P, 2, HID])
        B = sb("B", [P, 2, NT * T])
        Bf = B[:, :, :].rearrange("p a b -> p (a b)")
        cur_odd = sb("cur_odd", [P, NT * 16])
        x = sb("x", [T, D])
        xn = sb("xn", [T, D])
        bcs = sb("bcs", [T, D])
        xT = sb("xT", [P, KD, T])
        fm = sb("fm", [P, 3, KD * T])
        tok = sb("tok", [T, 2, D])
        dst_hot = sb("dst_hot", [P, ET, T])
        src_live = sb("src_live", [P, ET, T])
        src_col = sb("src_col", [P, ET], I32)
        dst_col = sb("dst_col", [P, ET], I32)
        type_col = sb("type_col", [P, ET], I32)
        key_col = sb("key_col", [P, ET])
        code = sb("code", [P, ET])
        later = sb("later", [P, ET])
        live = sb("live", [P, ET])
        stands = sb("stands", [P, ET])
        live_code = sb("live_code", [P, ET])
        node_row = sb("node_row", [P, T])
        node_col = sb("node_col", [P, 1])
        ident = sb("ident", [P, P])
        ones = sb("ones", [1, T])
        bias_fm = sb("bias_fm", [P, 6, KD])
        bexp = sb("bexp", [P, NT])
        upb = sb("upb", [P, NT])
        rmsw = sb("rmsw", [P, KD])
        att = sb("att", [P, 2, H1])
        etw = sb("etw", [T, 4])
        sp_t = sb("sp_t", [T, 4, 4])
        mask = sb("mask", [T, T])
        mtmp = sb("mtmp", [T, 3, T])
        count = sb("count", [T, T])
        absent = sb("absent", [T, T])
        stats = sb("stats", [T, 2, 6])
        mv = sb("mv", [T, 2])
        rstd = sb("rstd", [T, 1])
        minus_half = sb("minus_half", [T, 1])
        ms = sb("ms", [T, 1])
        rms = sb("rms", [T, 1])
        mx = sb("mx", [T, HEADS])
        den = sb("den", [T, HEADS])
        e_sb = sb("e_sb", [P, LT, H1])
        pooled = sb("pooled", [P, T])

        bank = [ctx.enter_context(nc.psum_tensor(f"bank{i}", [P, BANK], F32)) for i in range(8)]

        brow = mix[0:1, 2:4, :].rearrange("p a n -> p (a n)")[:, 0:3 * D].rearrange("p (a n) -> p a n", a=3)
        U, V = UV[:, 0, :], UV[:, 1, :]
        by_group = U.rearrange("p (c g x) -> p g x c", g=NT, x=2)
        B0 = B[:, 0, :].rearrange("p (n t) -> p n t", t=T)
        B1 = B[:, 1, :].rearrange("p (n t) -> p n t", t=T)
        keys = Bf[:, 0:EP]
        dst_bc = Bf[:, EP:2 * EP]
        after = Bf[:, 2 * EP:2 * EP + EP // 2].bitcast(BF16)
        junk = Bf[:, 2 * EP + EP // 2:3 * EP].bitcast(BF16)
        cur_even = Bf[:, 5120:6144]
        src_hot = Bf[:, 0:ET * T].rearrange("p (n t) -> p n t", t=T)
        dst_code = Bf[:, ET * T:2 * ET * T].rearrange("p (n t) -> p n t", t=T)
        S = Bf[0:T, 2 * ET * T:2 * ET * T + HEADS * T]
        S3 = S.rearrange("p (h t) -> p h t", t=T)
        PT = Bf[0:T, 0:HEADS * T].rearrange("p (h t) -> p h t", t=T)
        fmv = [fm[:, i, :].rearrange("p (k t) -> p k t", t=T) for i in range(3)]
        src_by_node = UV[0:T, 1, 0:EL]
        dst_by_node = UV[0:T, 1, EL:2 * EL]
        msg = UV[:, 0, 0:2 * EL].rearrange("p (f e) -> p f e", f=2)
        edge_rhs = Bf[:, 0:LT * H1 * T].rearrange("p (n h t) -> p n h t", h=H1, t=T)

        x_in = sem("x_in")
        rows_in = sem("rows_in")
        edge_in = sem("edge_in")
        small_in = sem("small_in")
        idx_set = sem("idx_set")
        slab_in = [sem(f"slab_in{i}") for i in range(SLOTS)]
        down_in, up_in = sem("down_in"), sem("up_in")
        slab_used = sem("slab_used")
        coef_in = [sem(f"coef_in{i}") for i in range(4)]
        consts = sem("consts")
        hot_made, pool_hot = sem("hot_made"), sem("pool_hot")
        composed = sem("composed")
        bc_done, bc_read = sem("bc_done"), sem("bc_read")
        bcs_ready = sem("bcs_ready")
        xn_ready = sem("xn_ready")
        var_ready, rstd_ready = sem("var_ready"), sem("rstd_ready")
        ms_ready, rms_ready = sem("ms_ready"), sem("rms_ready")
        xT_turned, xT_ready = sem("xT_turned"), sem("xT_ready")
        acc_ready = [sem(f"acc_ready_{n}") for n in GNN]
        tok_ready = [sem(f"tok_ready_{n}") for n in GNN]
        turned = [sem(f"turned_{n}") for n in GNN]
        fm_ready = [sem(f"fm_ready_{n}") for n in GNN]
        live_ready = sem("live_ready")
        counts_done, counts_read = sem("counts_done"), sem("counts_read")
        soft_ready = sem("soft_ready")
        scores_done, scores_read = sem("scores_done"), sem("scores_read")
        shifted, exped = sem("shifted"), sem("exped")
        probs_ready = sem("probs_ready")
        probs_turned, probsT_ready = sem("probs_turned"), sem("probsT_ready")
        attended, attended_read = sem("attended"), sem("attended_read")
        x1_ready = sem("x1_ready")
        exp_acc, exp_tok = sem("exp_acc"), sem("exp_tok")
        exp_turned, exp_fm = sem("exp_turned"), sem("exp_fm")
        up1_done, up1_read = sem("up1_done"), sem("up1_read")
        up2_turned, up2_fm = sem("up2_turned"), sem("up2_fm")
        up2_done, up2_read0, up2_read1 = sem("up2_done"), sem("up2_read0"), sem("up2_read1")
        act_turned, act_biased, act_fm = sem("act_turned"), sem("act_biased"), sem("act_fm")
        dn1_done, dn1_read0, dn1_read1 = sem("dn1_done"), sem("dn1_read0"), sem("dn1_read1")
        dn2_turned, dn2_fm = sem("dn2_turned"), sem("dn2_fm")
        dn2_done, dn2_read0, dn2_read1 = sem("dn2_done"), sem("dn2_read0"), sem("dn2_read1")
        con_done = sem("con_done")
        x2_ready = sem("x2_ready")
        idx_in, hot_ready = sem("idx_in"), sem("hot_ready")
        wd_done, wd_tok, wd_turned, wd_fm = sem("wd_done"), sem("wd_tok"), sem("wd_turned"), sem("wd_fm")
        lr_done, lr_ready = sem("lr_done"), sem("lr_ready")
        z_done, z_scaled, msg_ready = sem("z_done"), sem("z_scaled"), sem("msg_ready")
        e_done, rhs_ready = sem("e_done"), sem("rhs_ready")
        pair_done, pair_shift, pair_exp, alpha_ready = (
            sem("pair_done"), sem("pair_shift"), sem("pair_exp"), sem("alpha_ready"))
        alpha_turned, alphaT_ready = sem("alpha_turned"), sem("alphaT_ready")
        agg_done, agg_ready = sem("agg_done"), sem("agg_ready")
        up_done = sem("up_done")
        fin_done, fin_ready = sem("fin_done"), sem("fin_ready")
        out_done = sem("out_done")
        dve_step, act_step, pool_step = sem("dve_step"), sem("act_step"), sem("pool_step")

        block = ctx.enter_context(nc.Block())

        @block.sync
        def _(sp):
            for s in range(SLOTS):
                sp.dma_start(ring[:, s, :], A["stream"][s]).then_inc(slab_in[s], 16)
            rounds = (STREAM - SLOTS) // SLOTS
            with sp.Fori(1, rounds + 1) as r:
                for s in range(SLOTS):
                    sp.wait_ge(slab_used, r * SLOTS + (s - SLOTS + 1))
                    sp.dma_start(ring[:, s, :],
                                 A["stream"][bass.ds(r * SLOTS + s, 1)].rearrange("o p n -> (o p) n")
                                 ).then_inc(slab_in[s], 16)
            for i in range(SLOTS * (rounds + 1), STREAM):
                sp.wait_ge(slab_used, i - SLOTS + 1)
                sp.dma_start(ring[:, i % SLOTS, :], A["stream"][i]).then_inc(slab_in[i % SLOTS], 16)
            sp.wait_ge(slab_used, STREAM - SLOTS + 1)
            s = STREAM % SLOTS
            sp.dma_start(ring[:, s, 0:2048], A["w_down"]).then_inc(down_in, 16)
            sp.dma_start(ring[:, s, 2048:3072].rearrange("p (k n) -> p k n", k=2)[:, :, 0:G1], A["w_l"]).then_inc(down_in, 16)
            sp.dma_start(ring[:, s, 2048:3072].rearrange("p (k n) -> p k n", k=2)[:, :, G1:], A["w_r"]).then_inc(down_in, 16)
            sp.wait_ge(slab_used, STREAM - SLOTS + 2)
            s = (STREAM + 1) % SLOTS
            sp.dma_start(ring[:, s, 0:2048], A["w_up"]).then_inc(up_in, 16)
            sp.dma_start(ring[0:64, s, 2048:3072], A["disha"]).then_inc(up_in, 16)
            sp.dma_start(ring[64:128, s, 2048:3072], A["disha"]).then_inc(up_in, 16)
            for n in range(2):
                i = STREAM + 2 + n
                sp.wait_ge(slab_used, i - SLOTS + 1)
                sp.dma_start(ring[:, i % SLOTS, :], A["stream"][STREAM + n]).then_inc(slab_in[i % SLOTS], 16)
            for n in range(2):
                sp.wait_ge(fin_ready, n + 1)
                sp.dma_start(out[:, n * BANK:(n + 1) * BANK], xn[:, n * BANK:(n + 1) * BANK]).then_inc(out_done, 16)
            sp.wait_ge(out_done, 32)

        @block.gpsimd
        def _(pool):
            def coefs(k):
                src = A["coef"][k]
                for s in range(STAGES):
                    rows = 2 ** (STAGES + 1 - s)
                    width = NT * 2 ** (s + 1)
                    at = NT * (2 ** (s + 1) - 2)
                    row_src = src[s].rearrange("(r f) -> r f", r=rows)
                    pool.dma_start(UV[:, k % 2, at:at + width],
                                   row_src[:, None, :].broadcast_to([rows, 2 ** s, width])
                                   ).then_inc(coef_in[k], 16)

            nc.gpsimd.memset(ident[:], 0.0).then_inc(pool_step, 1)
            nc.gpsimd.memset(ones[:], 1.0).then_inc(consts, 1)
            nc.gpsimd.memset(minus_half[:], -0.5).then_inc(pool_step, 1)
            pool.wait_ge(pool_step, 2)
            nc.gpsimd.affine_select(out=ident[:], in_=ident[:], compare_op=ALU.not_equal, fill=1.0, base=0,
                                    pattern=[[-1, P]], channel_multiplier=1).then_inc(consts, 1)
            def root(n):
                pool.wait_ge(var_ready, n)
                nc.gpsimd.tensor_tensor(rstd[:], mv[:, 1:2], minus_half[:], ALU.pow).then_inc(rstd_ready, 1)

            coefs(0)
            coefs(1)
            root(1)
            nc.gpsimd.iota(node_row[:], pattern=[[1, T]], base=0, channel_multiplier=0,
                           allow_small_or_imprecise_dtypes=True).then_inc(consts, 1)
            nc.gpsimd.iota(node_col[:], pattern=[[0, 1]], base=0, channel_multiplier=1,
                           allow_small_or_imprecise_dtypes=True).then_inc(consts, 1)
            nc.gpsimd.memset(after, 1.0).then_inc(pool_step, 1)
            pool.wait_ge(pool_step, 3)
            nc.gpsimd.affine_select(out=after, in_=after, compare_op=ALU.is_gt, fill=0.0, base=0,
                                    pattern=[[1, EP]], channel_multiplier=-1).then_inc(consts, 1)
            pool.wait_ge(hot_made, 2)
            pool.wait_ge(live_ready, 1)
            nc.gpsimd.tensor_tensor(src_live[:], src_hot, stands[:, :, None].broadcast_to([P, ET, T]),
                                    ALU.mult).then_inc(pool_hot, 1)
            nc.gpsimd.tensor_tensor(dst_code, dst_hot[:], live_code[:, :, None].broadcast_to([P, ET, T]),
                                    ALU.mult).then_inc(pool_hot, 1)
            done = 3
            for k in range(4):
                pool.wait_ge(coef_in[k], 16 * STAGES)
                if k == 2:
                    pool.wait_ge(bc_done, 2)
                cur = UV[:, k % 2, 0:NT * 2].rearrange("p (g n) -> p g n", g=NT)
                for s in range(1, STAGES):
                    n = 2 ** s
                    at = NT * (2 * n - 2)
                    coef = UV[:, k % 2, at:at + NT * 2 * n].rearrange("p (g b n) -> p g b n", g=NT, b=2)
                    if s == STAGES - 1:
                        dst = mix[:, k, :]
                    elif s % 2:
                        dst = cur_odd[:, 0:NT * 2 * n]
                    else:
                        dst = cur_even[:, 0:NT * 2 * n]
                    new = dst.rearrange("p (g b n) -> p g b n", g=NT, b=2)
                    ins = nc.gpsimd.tensor_tensor(new, cur[:, :, None, :].broadcast_to([P, NT, 2, n]), coef, ALU.mult)
                    if s == STAGES - 1:
                        ins.then_inc(composed, 1)
                    else:
                        ins.then_inc(pool_step, 1)
                        done += 1
                        pool.wait_ge(pool_step, done)
                    cur = dst.rearrange("p (g n) -> p g n", g=NT)
                if k < 2:
                    pool.wait_ge(composed, k + 1)
                    coefs(k + 2)
            root(2)
            root(3)
            pool.wait_ge(ms_ready, 2)
            nc.gpsimd.tensor_tensor(rms[:], ms[:], minus_half[:], ALU.pow).then_inc(rms_ready, 1)
            root(4)

        @block.scalar
        def _(act):
            act.dma_start(x[:], A["x"]).then_inc(x_in, 16)
            for i, n in enumerate(["bo", "b_con", "down_bias"]):
                act.dma_start(brow[:, i, :], A[n]).then_inc(rows_in, 16)
            full = (ET - 1) * P
            act.wait_ge(idx_set, 6)
            for col, n in ((src_col, "src"), (dst_col, "dst"), (type_col, "etype")):
                act.dma_start(col[:, 0:ET - 1], A[n + "_cols"]).then_inc(edge_in, 16)
                act.dma_start(col[0:E - full, ET - 1:ET], A[n + "_tail"]).then_inc(edge_in, 16)
            for row, n in ((keys, "src"), (dst_bc, "dst")):
                act.dma_start(row.bitcast(I32)[:, 0:E], A[n].broadcast_to([P, E])).then_inc(edge_in, 16)
            act.dma_start(etw[:], A["etw"].broadcast_to([T, 4])).then_inc(small_in, 16)
            for i in range(6):
                act.dma_start(bias_fm[:, i, :], A["bias_fm"][i]).then_inc(small_in, 16)
            act.dma_start(bexp[:], A["b_exp"]).then_inc(small_in, 16)
            act.dma_start(upb[:], A["up_bias"]).then_inc(small_in, 16)
            act.dma_start(rmsw[:], A["rms_w"]).then_inc(small_in, 16)
            for h in range(H1):
                p0 = 64 * (h % 2)
                act.dma_start(att[p0:p0 + 64, h // 2, h:h + 1], A["att"][h]).then_inc(small_in, 16)
            act.wait_ge(bc_done, 2)
            for n in range(2):
                nc.scalar.copy(bcs[:, n * BANK:(n + 1) * BANK], bank[2 + n][0:T, :]).then_inc(bcs_ready, 1)
            act.wait_ge(small_in, 16 * 14)
            nc.scalar.activation(sp_t[:, 0, :], etw[:], ACT.Abs).then_inc(act_step, 1)
            act.wait_ge(act_step, 1)
            nc.scalar.activation(sp_t[:, 1, :], sp_t[:, 0, :], ACT.Exp, scale=-1.0).then_inc(act_step, 1)
            act.wait_ge(act_step, 2)
            nc.scalar.activation(sp_t[:, 2, :], sp_t[:, 1, :], ACT.Ln, bias=1.0).then_inc(soft_ready, 1)

            def evac_tok(j):
                for n in range(2):
                    act.wait_ge(acc_ready[j], n + 1)
                    if j >= 2:
                        act.wait_ge(turned[j - 2], 2)
                    nc.scalar.copy(tok[:, j % 2, n * BANK:(n + 1) * BANK],
                                   bank[2 * (j % 2) + n][0:T, :]).then_inc(tok_ready[j], 1)

            for j in range(6):
                evac_tok(j)
                if j == 4:
                    for g in range(2):
                        act.wait_ge(shifted, g + 1)
                        nc.scalar.activation(S[:, g * 768:(g + 1) * 768], S[:, g * 768:(g + 1) * 768],
                                             ACT.Exp).then_inc(exped, 1)
            for c in (1, 3):
                act.wait_ge(probs_turned, c + 1)
                nc.scalar.copy(PT[:, 4 * c:4 * c + 4, :], bank[4 + c][0:T, 0:4 * T].rearrange("p (h t) -> p h t", t=T)
                               ).then_inc(probsT_ready, 1)

            def evac_up1(m):
                act.wait_ge(up1_done, m + 1)
                if m == 0:
                    act.wait_ge(composed, 4)
                for h in range(2):
                    dst = by_group[0:T, 8 * m:8 * m + 8, h, :]
                    nc.scalar.copy(dst, bank[6 + h][0:T, :].rearrange("p (g c) -> p g c", c=GRP)).then_inc(up1_read, 1)

            for n in range(EXP_SLABS):
                act.wait_ge(exp_acc, n + 1)
                if n >= 2:
                    act.wait_ge(exp_turned, n - 1)
                nc.scalar.copy(tok[:, n % 2, 0:BANK], bank[n % 4][0:T, :]).then_inc(exp_tok, 1)
                if n >= 3 and n % 2:
                    evac_up1((n - 3) // 2)
            evac_up1(3)
            for m in range(4):
                act.wait_ge(up2_done, m + 1)
                dst = V.rearrange("p (g r x) -> p r x g", r=NT, x=2)[0:T, 8 * m:8 * m + 8, 0, :]
                nc.scalar.copy(dst, bank[(6, 2)[m % 2]][0:T, :].rearrange("p (r g) -> p r g", g=GRP)).then_inc(up2_read0, 1)

            def gelu(c):
                act.wait_ge(act_biased, c + 1)
                g = B1[:, 4 * c:4 * c + 4, :]
                nc.scalar.activation(g, g, ACT.Gelu).then_inc(act_fm, 1)

            def evac_dn1(m):
                act.wait_ge(dn1_done, m + 1)
                dst = by_group[0:T, 8 * m:8 * m + 8, 0, :]
                nc.scalar.copy(dst, bank[(6, 2)[m % 2]][0:T, :].rearrange("p (g c) -> p g c", c=GRP)).then_inc(dn1_read0, 1)

            for c in range(8):
                gelu(c)
                if c >= 3 and c % 2:
                    evac_dn1((c - 3) // 2)
            evac_dn1(3)
            act.wait_ge(act_turned, 8)
            for view, n in ((src_by_node, "src"), (dst_by_node, "dst")):
                act.dma_start(view.bitcast(I32)[:, 0:E], A[n].broadcast_to([T, E])).then_inc(idx_in, 16)
            for c in range(8):
                act.wait_ge(dn2_done, c + 1)
                nc.scalar.copy(B0[0:64, 4 * c:4 * c + 4, :],
                               bank[(6, 2)[c % 2]][0:64, 0:4 * T].rearrange("p (r t) -> p r t", t=T)).then_inc(dn2_read0, 1)
            act.wait_ge(lr_done, 1)
            nc.scalar.copy(tok[:, 1, 0:BANK], bank[7][0:T, :]).then_inc(lr_ready, 1)
            for i in range(8):
                c, f = i // 2, i % 2
                w = min(BANK, EL - c * BANK)
                act.wait_ge(z_done, i + 1)
                if i >= 2:
                    act.wait_ge(msg_ready, i - 1)
                nc.scalar.mul(fm[:, i % 2, 0:w], bank[i % 4][:, 0:w], 0.2).then_inc(z_scaled, 1)
            act.wait_ge(pair_shift, 1)
            nc.scalar.activation(S[:, 0:H1 * T], S[:, 0:H1 * T], ACT.Exp).then_inc(pair_exp, 1)

        @block.tensor
        def _(pe):
            def slab(i):
                pe.wait_ge(slab_in[i % SLOTS], 16 * (i // SLOTS + 1))
                return ring[:, i % SLOTS, :]

            def slab4(i):
                pe.wait_ge(slab_in[i % SLOTS], 16 * ((STREAM + SLOTS - 1 - i % SLOTS) // SLOTS + 1))
                return ring[:, i % SLOTS, :]

            def turn8(src, done):
                for c in range(2):
                    for k in range(4):
                        mm = nc.tensor.transpose(bank[4 + c][:, k * T:(k + 1) * T],
                                                 src[:, (4 * c + k) * P:(4 * c + k + 1) * P], ident[0:T, 0:T])
                    mm.then_inc(done, 1)

            pe.wait_ge(rows_in, 48)
            pe.wait_ge(consts, 2)
            for n in range(2):
                cols = slice(n * BANK, (n + 1) * BANK)
                nc.tensor.matmul(bank[6 + n][0:T, :], ones[:], brow[:, 0, cols], start=True, stop=True)
                nc.tensor.matmul(bank[2 + n][0:T, :], ones[:], brow[:, 1, cols], start=True, stop=False)
                mm = nc.tensor.matmul(bank[2 + n][0:T, :], ones[:], brow[:, 2, cols], start=False, stop=True)
                mm.then_inc(bc_done, 1)
            pe.wait_ge(xn_ready, 1)
            turn8(xn, xT_turned)

            def half(j, n, act_in):
                w = slab(2 * j + n).rearrange("p (k n) -> p k n", k=KD)
                b = bank[2 * (j % 2) + n]
                for k in range(KD):
                    mm = nc.tensor.matmul(b[0:T, :], act_in[:, k, :], w[:, k, :], start=(k == 0), stop=(k == KD - 1))
                mm.then_inc(acc_ready[j], 1)
                pe.wait_ge(acc_ready[j], n + 1)
                pe.sem_inc(slab_used, 1)

            def turn(j):
                pe.wait_ge(tok_ready[j], 2)
                if j >= 1:
                    pe.wait_ge(fm_ready[j - 1], 2)
                else:
                    pe.wait_ge(xT_ready, 2)
                turn8(tok[:, j % 2, :], turned[j])

            inputs = [xT, xT, fmv[0], fmv[1], xT, fmv[1], fmv[2]]
            for j in range(6):
                if j >= 2:
                    pe.wait_ge(tok_ready[j - 2], 2)
                if j == 0:
                    pe.wait_ge(xT_ready, 2)
                if j == 1:
                    pe.wait_ge(bcs_ready, 2)
                if j in (2, 3):
                    pe.wait_ge(fm_ready[j - 2], 2)
                if j == 5:
                    pe.wait_ge(fm_ready[4], 2)
                half(j, 0, inputs[j])
                if 1 <= j <= 4:
                    turn(j - 1)
                half(j, 1, inputs[j])
                if j == 2:
                    pe.wait_ge(hot_made, 2)
                    pe.wait_ge(pool_hot, 2)
                    pe.wait_ge(bc_read, 2)
                    for t in range(ET):
                        nc.tensor.matmul(bank[6][0:T, 0:T], src_hot[:, t, :], dst_code[:, t, :],
                                         start=(t == 0), stop=(t == ET - 1))
                    for t in range(ET):
                        mm = nc.tensor.matmul(bank[7][0:T, 0:T], dst_hot[:, t, :], src_hot[:, t, :],
                                              start=(t == 0), stop=(t == ET - 1))
                    mm.then_inc(counts_done, 1)
                if j == 4:
                    pe.wait_ge(fm_ready[3], 2)
                    pe.wait_ge(counts_read, 1)
                    for c in range(2):
                        for par in range(2):
                            for i in range(4):
                                k = 4 * c + i
                                mm = nc.tensor.matmul(bank[4 + 2 * par + c][0:T, i * T:(i + 1) * T],
                                                      fmv[2][64 * par:64 * par + 64, k, :],
                                                      fmv[0][64 * par:64 * par + 64, k, :], start=True, stop=True)
                            mm.then_inc(scores_done, 1)
                    pe.wait_ge(scores_read, 4)
                    turn(4)
            pe.wait_ge(fm_ready[4], 2)
            for c in range(4):
                pe.wait_ge(probs_ready, c // 2 + 1)
                for i in range(4):
                    mm = nc.tensor.transpose(bank[4 + c][0:T, i * T:(i + 1) * T], S3[:, 4 * c + i, :], ident[0:T, 0:T])
                mm.then_inc(probs_turned, 1)
            pe.wait_ge(tok_ready[5], 2)
            pe.wait_ge(probsT_ready, 4)
            for c in range(2):
                for k in range(4 * c, 4 * c + 4):
                    for par in range(2):
                        h = 2 * k + par
                        mm = nc.tensor.matmul(bank[2 + c][64 * par:64 * par + 64, (k - 4 * c) * T:(k - 4 * c + 1) * T],
                                              tok[:, 1, h * HD:(h + 1) * HD], PT[:, par * 8 + k, :],
                                              start=True, stop=True)
                mm.then_inc(attended, 1)
            pe.wait_ge(attended_read, 2)
            half(6, 0, inputs[6])
            half(6, 1, inputs[6])

            pe.wait_ge(xn_ready, 2)
            turn8(xn, xT_turned)
            lo, hi = (mix[:, k, :].rearrange("p (n c) -> p n c", c=GRP) for k in (0, 1))
            dlo, dhi = (mix[:, k, :].rearrange("p (n c) -> p n c", c=GRP) for k in (2, 3))

            def expand(n):
                if n >= 4:
                    pe.wait_ge(exp_tok, n - 3)
                w = slab(GNN_SLABS + n).rearrange("p (k n) -> p k n", k=KD)
                for k in range(KD):
                    mm = nc.tensor.matmul(bank[n % 4][0:T, :], xT[:, k, :], w[:, k, :],
                                          start=(k == 0), stop=(k == KD - 1))
                mm.then_inc(exp_acc, 1)
                pe.wait_ge(exp_acc, n + 1)
                pe.sem_inc(slab_used, 1)

            def exp_turn(n):
                pe.wait_ge(exp_tok, n + 1)
                if n >= 2:
                    pe.wait_ge(exp_fm, n - 1)
                for k in range(4):
                    mm = nc.tensor.transpose(bank[4 + n % 2][:, k * T:(k + 1) * T],
                                             tok[:, n % 2, k * P:(k + 1) * P], ident[0:T, 0:T])
                mm.then_inc(exp_turned, 1)

            def first_step(m, fm_in, matrix, pair):
                for g in range(8):
                    for h in range(2):
                        mm = nc.tensor.matmul(bank[pair + h][0:T, g * GRP:(g + 1) * GRP],
                                              fm_in[64 * h:64 * h + 64, 8 * m + g, :],
                                              matrix[64 * h:64 * h + 64, 8 * m + g, :], start=True, stop=True)
                return mm

            def up1(m):
                pe.wait_ge(exp_fm, 2 * m + 2)
                if m == 0:
                    pe.wait_ge(composed, 1)
                else:
                    pe.wait_ge(up1_read, 2 * m)
                first_step(m, B1, lo, 6).then_inc(up1_done, 1)

            pe.wait_ge(xT_ready, 4)
            pe.wait_ge(x1_ready, 2)
            for n in range(EXP_SLABS):
                expand(n)
                if n >= 1:
                    exp_turn(n - 1)
                if n >= 3 and n % 2:
                    up1((n - 3) // 2)
            exp_turn(7)
            up1(3)

            def turn4(c, src, b, done):
                for i in range(4 * c, 4 * c + 4):
                    mm = nc.tensor.transpose(b[:, (i - 4 * c) * T:(i - 4 * c + 1) * T], src[0:T, i * P:(i + 1) * P],
                                             ident[0:T, 0:T])
                mm.then_inc(done, 1)

            UPT = (4, 5, 0, 1)
            pe.wait_ge(up1_read, 8)
            pe.wait_ge(composed, 2)

            def up2(m):
                pe.wait_ge(up2_fm, 2 * m + 2)
                if m >= 2:
                    pe.wait_ge(up2_read0, m - 1)
                    pe.wait_ge(up2_read1, m - 1)
                first_step(m, B0, hi, (6, 2)[m % 2]).then_inc(up2_done, 1)

            for c in range(8):
                if c < 2:
                    pe.wait_ge(exp_fm, 8)
                if c >= 4:
                    pe.wait_ge(up2_fm, c - 3)
                turn4(c, U, bank[UPT[c % 4]], up2_turned)
                if c >= 3 and c % 2:
                    up2((c - 3) // 2)
            up2(3)
            pe.wait_ge(up2_read0, 4)
            pe.wait_ge(up2_read1, 4)

            def dn1(m):
                pe.wait_ge(act_fm, 2 * m + 2)
                if m >= 2:
                    pe.wait_ge(dn1_read0, m - 1)
                    pe.wait_ge(dn1_read1, m - 1)
                first_step(m, B1, dlo, (6, 2)[m % 2]).then_inc(dn1_done, 1)

            pe.wait_ge(composed, 4)
            for c in range(8):
                pe.wait_ge(up2_fm, 8)
                if c >= 4:
                    pe.wait_ge(act_biased, c - 3)
                turn4(c, V, bank[UPT[c % 4]], act_turned)
                if c >= 3 and c % 2:
                    dn1((c - 3) // 2)
            dn1(3)
            pe.wait_ge(dn1_read0, 4)
            pe.wait_ge(dn1_read1, 4)

            def dn2(c):
                pe.wait_ge(dn2_fm, c + 1)
                if c >= 2:
                    pe.wait_ge(dn2_read0, c - 1)
                    pe.wait_ge(dn2_read1, c - 1)
                for i in range(4):
                    for h in range(2):
                        hs = slice(64 * h, 64 * h + 64)
                        mm = nc.tensor.matmul(bank[(6, 2)[c % 2] + h][hs, i * T:(i + 1) * T],
                                              dhi[hs, 4 * c + i, :], B1[hs, 4 * c + i, :], start=True, stop=True)
                mm.then_inc(dn2_done, 1)

            def contract(s):
                pe.wait_ge(dn2_read0, s + 1)
                pe.wait_ge(dn2_read1, s + 1)
                w = slab(GNN_SLABS + EXP_SLABS + s).rearrange("p (k n) -> p k n", k=4)
                for i in range(4):
                    for n in range(2):
                        mm = nc.tensor.matmul(bank[n][0:T, :], B0[:, 4 * s + i, :], w[:, i, n * BANK:(n + 1) * BANK],
                                              start=(s == 0 and i == 0), stop=(s == 7 and i == 3))
                mm.then_inc(con_done, 1)
                pe.wait_ge(con_done, s + 1)
                pe.sem_inc(slab_used, 1)

            for c in range(8):
                if c < 2:
                    pe.wait_ge(act_biased, 8)
                else:
                    pe.wait_ge(dn2_fm, c - 1)
                turn4(c, U, bank[4 + c % 2], dn2_turned)
                if c >= 1:
                    dn2(c - 1)
                if c >= 3:
                    contract(c - 3)
            dn2(7)
            for s in range(5, 8):
                contract(s)

            pe.wait_ge(xn_ready, 3)
            turn8(xn, xT_turned)
            small = ring[:, STREAM % SLOTS, :]
            big = ring[:, (STREAM + 1) % SLOTS, :]
            pe.wait_ge(down_in, 48)
            pe.wait_ge(xT_ready, 6)
            for k in range(KD):
                mm = nc.tensor.matmul(bank[6][0:T, 0:G1], xT[:, k, :], small[:, k * G1:(k + 1) * G1],
                                      start=(k == 0), stop=(k == KD - 1))
            mm.then_inc(wd_done, 1)
            pe.wait_ge(wd_tok, 1)
            for k in range(2):
                mm = nc.tensor.transpose(bank[4][:, k * T:(k + 1) * T], tok[:, 0, k * P:(k + 1) * P], ident[0:T, 0:T])
            mm.then_inc(wd_turned, 1)
            pe.wait_ge(wd_fm, 1)
            for k in range(2):
                mm = nc.tensor.matmul(bank[7][0:T, :], fmv[2][:, k, :], small[:, 2048 + k * 512:2048 + (k + 1) * 512],
                                      start=(k == 0), stop=(k == 1))
            mm.then_inc(lr_done, 1)
            pe.wait_ge(lr_ready, 1)
            pe.wait_ge(hot_ready, 4)

            def messages(c):
                w = min(BANK, EL - c * BANK)
                for f in range(2):
                    i = 2 * c + f
                    if i >= 4:
                        pe.wait_ge(msg_ready, i - 3)
                    nc.tensor.matmul(bank[i % 4][:, 0:w], tok[:, 1, f * P:(f + 1) * P],
                                     src_by_node[:, c * BANK:c * BANK + w], start=True, stop=False)
                    nc.tensor.matmul(bank[i % 4][:, 0:w], tok[:, 1, G1 + f * P:G1 + (f + 1) * P],
                                     dst_by_node[:, c * BANK:c * BANK + w], start=False, stop=True).then_inc(z_done, 1)

            def logits(c):
                pe.wait_ge(msg_ready, 2 * c + 2)
                if c >= 2:
                    pe.wait_ge(rhs_ready, c - 1)
                for t in range(4 * c, min(4 * c + 4, LT)):
                    w = P if t < ET else T
                    for f in range(2):
                        mm = nc.tensor.matmul(bank[(5, 7)[c % 2]][0:w, t * H1:(t + 1) * H1],
                                              msg[:, f, t * P:t * P + w],
                                              att[:, f, :], start=(f == 0), stop=(f == 1))
                mm.then_inc(e_done, 1)

            def spread(c):
                pe.wait_ge(rhs_ready, c + 1 if c < 3 else 5)
                for t in range(4 * c, min(4 * c + 4, LT)):
                    w, dst = (P, dst_hot[:, t, :]) if t < ET else (T, ident[0:T, 0:T])
                    mm = nc.tensor.matmul(bank[6][0:T, 0:H1 * T], dst,
                                          edge_rhs[0:w, t, :, :].rearrange("p h t -> p (h t)"),
                                          start=(t == 0), stop=(t == LT - 1))
                return mm

            messages(0)
            messages(1)
            logits(0)
            messages(2)
            logits(1)
            spread(0)
            messages(3)
            logits(2)
            spread(1)
            logits(3)
            spread(2)
            spread(3).then_inc(pair_done, 1)
            pe.wait_ge(alpha_ready, 1)
            for h in range(H1):
                mm = nc.tensor.transpose(bank[4][0:T, h * T:(h + 1) * T], S3[:, h, :], ident[0:T, 0:T])
            mm.then_inc(alpha_turned, 1)
            pe.wait_ge(alphaT_ready, 1)
            for h in range(H1):
                p0 = 64 * (h % 2)
                mm = nc.tensor.matmul(bank[5][p0:p0 + 64, (h // 2) * T:(h // 2 + 1) * T],
                                      tok[:, 1, h * 64:(h + 1) * 64], S3[:, 4 + h, :], start=True, stop=True)
            mm.then_inc(agg_done, 1)
            pe.wait_ge(agg_ready, 1)
            pe.wait_ge(up_in, 48)
            for n in range(2):
                for k in range(2):
                    mm = nc.tensor.matmul(bank[n][0:T, :], fmv[2][:, k, :], big[:, k * D + n * BANK:k * D + (n + 1) * BANK],
                                          start=(k == 0), stop=(k == 1))
                mm.then_inc(up_done, 1)

            pe.wait_ge(xn_ready, 4)
            turn8(xn, xT_turned)
            pe.wait_ge(xT_ready, 9)
            for n in range(2):
                w = slab4(STREAM + 2 + n).rearrange("p (k n) -> p k n", k=KD)
                for k in range(KD):
                    nc.tensor.matmul(bank[2 + n][0:T, :], xT[:, k, :], w[:, k, :], start=(k == 0), stop=False)
                nc.tensor.matmul(bank[2 + n][0:T, :], pooled[:], big[:, 2048 + n * BANK:2048 + (n + 1) * BANK],
                                 start=False, stop=True).then_inc(fin_done, 1)

        @block.vector
        def _(dve):
            steps, norms = [0], [0]

            def step(ins):
                steps[0] += 1
                ins.then_inc(dve_step, 1)
                dve.wait_ge(dve_step, steps[0])

            def layer_norm():
                for n in range(2):
                    st = nc.vector.bn_stats(stats[:, n, :], x[:, n * BANK:(n + 1) * BANK])
                step(st)
                step(nc.vector.bn_aggr(mv[:], stats[:]))
                nc.vector.tensor_scalar(mv[:, 1:2], mv[:, 1:2], LN_EPS, None, ALU.add).then_inc(var_ready, 1)
                norms[0] += 1
                dve.wait_ge(var_ready, norms[0])
                dve.wait_ge(rstd_ready, norms[0])
                nc.vector.tensor_scalar(xn[:], x[:], mv[:, 0:1], rstd[:], ALU.subtract, ALU.mult
                                        ).then_inc(xn_ready, 1)

            def take_xT(t0, scale=None):
                for c in range(2):
                    dve.wait_ge(xT_turned, t0 + c + 1)
                    src = bank[4 + c][:, 0:4 * T].rearrange("p (k t) -> p k t", t=T)
                    if scale is None:
                        nc.vector.tensor_copy(xT[:, 4 * c:4 * c + 4, :], src).then_inc(xT_ready, 1)
                    else:
                        nc.vector.tensor_tensor(xT[:, 4 * c:4 * c + 4, :], src,
                                                scale[:, 4 * c:4 * c + 4, None].broadcast_to([P, 4, T]),
                                                ALU.mult).then_inc(xT_ready, 1)

            full = (ET - 1) * P
            for col in (src_col, dst_col, type_col):
                nc.vector.memset(col[:, ET - 1:ET], -1).then_inc(idx_set, 1)
            for row in (keys, dst_bc):
                nc.vector.memset(row.bitcast(I32)[:, E:EP], -1).then_inc(idx_set, 1)
            nc.vector.memset(att[:], 0.0).then_inc(idx_set, 1)
            dve.wait_ge(x_in, 16)
            layer_norm()
            take_xT(0)
            dve.wait_ge(bc_done, 2)
            for n in range(2):
                cols = slice(n * BANK, (n + 1) * BANK)
                nc.vector.tensor_tensor(x[:, cols], x[:, cols], bank[6 + n][0:T, :], ALU.add).then_inc(bc_read, 1)
            dve.wait_ge(edge_in, 16 * 8)
            dve.wait_ge(consts, 5)
            dve.wait_ge(idx_set, 6)
            step(nc.vector.scalar_tensor_tensor(out=keys, in0=keys.bitcast(I32), scalar=float(T),
                                                in1=dst_bc.bitcast(I32), op0=ALU.mult, op1=ALU.add))
            step(nc.vector.scalar_tensor_tensor(out=key_col[:], in0=src_col[:], scalar=float(T), in1=dst_col[:],
                                                op0=ALU.mult, op1=ALU.add))
            nodes = node_row[:, None, :].broadcast_to([P, ET, T])
            nc.vector.tensor_tensor(dst_hot[:], dst_col[:, :, None].broadcast_to([P, ET, T]), nodes,
                                    ALU.is_equal).then_inc(hot_made, 1)
            for t in range(ET):
                w = EP - t * P
                step(nc.vector.scalar_tensor_tensor(out=junk[:, 0:w], in0=keys[:, t * P:EP], scalar=key_col[:, t:t + 1],
                                                    in1=after[:, 0:w], op0=ALU.is_equal, op1=ALU.mult,
                                                    accum_out=later[:, t:t + 1]))
            nc.vector.tensor_tensor(src_hot, src_col[:, :, None].broadcast_to([P, ET, T]), nodes,
                                    ALU.is_equal).then_inc(hot_made, 1)
            step(nc.vector.tensor_scalar(live[:], later[:], 0.0, None, ALU.is_equal))
            step(nc.vector.tensor_scalar(code[:], type_col[:], 0.0, 4.0, ALU.is_equal, ALU.mult))
            step(nc.vector.tensor_tensor(code[:], code[:], type_col[:], ALU.add))
            step(nc.vector.tensor_tensor(stands[:], src_col[:], dst_col[:], ALU.not_equal))
            step(nc.vector.tensor_tensor(stands[:], stands[:], live[:], ALU.mult))
            nc.vector.tensor_tensor(live_code[:], live[:], code[:], ALU.mult).then_inc(live_ready, 1)

            def take_turn(j, dst):
                for c in range(2):
                    dve.wait_ge(turned[j], c + 1)
                    src = bank[4 + c][:, 0:4 * T].rearrange("p (k t) -> p k t", t=T)
                    b = bias_fm[:, BIAS[j], 4 * c:4 * c + 4, None].broadcast_to([P, 4, T])
                    nc.vector.tensor_tensor(dst[:, 4 * c:4 * c + 4, :], src, b, ALU.add).then_inc(fm_ready[j], 1)

            BIAS = [0, 1, 2, 3, 4, 5]
            dve.wait_ge(small_in, 16 * 14)
            take_turn(0, fmv[0])
            take_turn(1, fmv[1])
            dve.wait_ge(counts_done, 1)
            dve.wait_ge(soft_ready, 1)
            step(nc.vector.scalar_tensor_tensor(out=sp_t[:, 3, :], in0=etw[:], scalar=0.0, in1=sp_t[:, 2, :],
                                                op0=ALU.max, op1=ALU.add))
            step(nc.vector.tensor_copy(mtmp[:, 0, :], bank[6][0:T, 0:T]))
            step(nc.vector.tensor_scalar(mtmp[:, 1, :], mtmp[:, 0, :], 0.0, 4.0, ALU.is_equal, ALU.mult))
            step(nc.vector.tensor_tensor(mtmp[:, 1, :], mtmp[:, 1, :], ident[0:T, 0:T], ALU.mult))
            step(nc.vector.tensor_tensor(mtmp[:, 0, :], mtmp[:, 0, :], mtmp[:, 1, :], ALU.add))
            step(nc.vector.tensor_scalar(mask[:], mtmp[:, 0, :], 0.0, -BIG, ALU.is_equal, ALU.mult))
            for c in range(4):
                step(nc.vector.tensor_scalar(mtmp[:, 1, :], mtmp[:, 0, :], float(c + 1), sp_t[:, 3, c:c + 1],
                                             ALU.is_equal, ALU.mult))
                step(nc.vector.tensor_tensor(mask[:], mask[:], mtmp[:, 1, :], ALU.add))
            step(nc.vector.tensor_tensor(count[:], ident[0:T, 0:T], bank[7][0:T, 0:T], ALU.add))
            nc.vector.tensor_scalar(absent[:], count[:], 0.0, -BIG, ALU.is_equal, ALU.mult).then_inc(counts_read, 1)
            take_turn(2, fmv[2])
            dve.wait_ge(acc_ready[2], 2)
            take_turn(3, fmv[0])
            for n, (c, par) in enumerate(((0, 0), (0, 1), (1, 0), (1, 1))):
                dve.wait_ge(scores_done, n + 1)
                at = (par * 8 + c * 4) * T
                nc.vector.scalar_tensor_tensor(out=S[:, at:at + 4 * T].rearrange("p (h t) -> p h t", t=T),
                                               in0=bank[4 + 2 * par + c][0:T, 0:4 * T].rearrange("p (h t) -> p h t", t=T),
                                               scalar=float(HD) ** -0.5,
                                               in1=mask[:, None, :].broadcast_to([T, 4, T]),
                                               op0=ALU.mult, op1=ALU.add).then_inc(scores_read, 1)
            dve.wait_ge(scores_read, 4)
            dve.wait_ge(acc_ready[3], 2)
            for g in range(2):
                sl = S3[:, 8 * g:8 * g + 8, :]
                step(nc.vector.tensor_reduce(mx[:, 8 * g:8 * g + 8], sl, AX.X, ALU.max))
                nc.vector.tensor_tensor(sl, sl, mx[:, 8 * g:8 * g + 8, None].broadcast_to([T, 8, T]),
                                        ALU.subtract).then_inc(shifted, 1)
                if g == 0:
                    take_turn(4, fmv[1])
            for g in range(2):
                sl = S3[:, 8 * g:8 * g + 8, :]
                dve.wait_ge(exped, g + 1)
                step(nc.vector.tensor_reduce(den[:, 8 * g:8 * g + 8], sl, AX.X, ALU.add))
                step(nc.vector.reciprocal(den[:, 8 * g:8 * g + 8], den[:, 8 * g:8 * g + 8]))
                nc.vector.tensor_tensor(sl, sl, den[:, 8 * g:8 * g + 8, None].broadcast_to([T, 8, T]),
                                        ALU.mult).then_inc(probs_ready, 1)
            for c in (0, 2):
                dve.wait_ge(probs_turned, c + 1)
                nc.vector.tensor_copy(PT[:, 4 * c:4 * c + 4, :],
                                      bank[4 + c][0:T, 0:4 * T].rearrange("p (h t) -> p h t", t=T)).then_inc(probsT_ready, 1)
            for c in range(2):
                dve.wait_ge(attended, c + 1)
                nc.vector.tensor_tensor(fmv[2][:, 4 * c:4 * c + 4, :],
                                        bank[2 + c][:, 0:4 * T].rearrange("p (k t) -> p k t", t=T),
                                        bias_fm[:, 5, 4 * c:4 * c + 4, None].broadcast_to([P, 4, T]),
                                        ALU.add).then_inc(attended_read, 1)

            def add_halves(ready, banks, done):
                for n in range(2):
                    cols = slice(n * BANK, (n + 1) * BANK)
                    dve.wait_ge(ready, n + 1)
                    nc.vector.tensor_tensor(x[:, cols], x[:, cols], bank[banks[n]][0:T, :], ALU.add).then_inc(done, 1)
                dve.wait_ge(done, 2)

            add_halves(acc_ready[6], (0, 1), x1_ready)
            layer_norm()
            take_xT(2)
            dve.wait_ge(bcs_ready, 2)
            step(nc.vector.tensor_tensor(x[:], x[:], bcs[:], ALU.add))
            dve.wait_ge(composed, 4)
            for n in range(EXP_SLABS):
                dve.wait_ge(exp_turned, n + 1)
                nc.vector.tensor_tensor(B1[:, 4 * n:4 * n + 4, :],
                                        bank[4 + n % 2][:, 0:4 * T].rearrange("p (k t) -> p k t", t=T),
                                        bexp[:, 4 * n:4 * n + 4, None].broadcast_to([P, 4, T]), ALU.add).then_inc(exp_fm, 1)

            UPT = (4, 5, 0, 1)

            def evac_up2(m):
                dve.wait_ge(up2_done, m + 1)
                dst = V.rearrange("p (g r x) -> p r x g", r=NT, x=2)[0:T, 8 * m:8 * m + 8, 1, :]
                nc.vector.tensor_copy(dst, bank[(6, 2)[m % 2] + 1][0:T, :].rearrange("p (r g) -> p r g", g=GRP)
                                      ).then_inc(up2_read1, 1)

            for c in range(8):
                dve.wait_ge(up2_turned, c + 1)
                nc.vector.tensor_copy(B0[:, 4 * c:4 * c + 4, :],
                                      bank[UPT[c % 4]][:, 0:4 * T].rearrange("p (k t) -> p k t", t=T)).then_inc(up2_fm, 1)
                if c >= 3 and c % 2:
                    evac_up2((c - 3) // 2)
            evac_up2(3)

            def evac_dn1(m):
                dve.wait_ge(dn1_done, m + 1)
                dst = by_group[0:T, 8 * m:8 * m + 8, 1, :]
                nc.vector.tensor_copy(dst, bank[(6, 2)[m % 2] + 1][0:T, :].rearrange("p (g c) -> p g c", c=GRP)
                                      ).then_inc(dn1_read1, 1)

            for c in range(8):
                dve.wait_ge(act_turned, c + 1)
                nc.vector.tensor_tensor(B1[:, 4 * c:4 * c + 4, :],
                                        bank[UPT[c % 4]][:, 0:4 * T].rearrange("p (k t) -> p k t", t=T),
                                        upb[:, 4 * c:4 * c + 4, None].broadcast_to([P, 4, T]), ALU.add).then_inc(act_biased, 1)
                if c >= 3 and c % 2:
                    evac_dn1((c - 3) // 2)
            evac_dn1(3)
            for view in (src_by_node, dst_by_node):
                nc.vector.memset(view.bitcast(I32)[:, E:EP], -1).then_inc(idx_set, 1)
                nc.vector.tensor_copy(view[:, EP:EL], ident[0:T, 0:T]).then_inc(hot_ready, 1)

            def evac_dn2(c):
                dve.wait_ge(dn2_done, c + 1)
                nc.vector.tensor_copy(B0[64:128, 4 * c:4 * c + 4, :],
                                      bank[(6, 2)[c % 2] + 1][64:128, 0:4 * T].rearrange("p (r t) -> p r t", t=T)
                                      ).then_inc(dn2_read1, 1)

            for c in range(8):
                dve.wait_ge(dn2_turned, c + 1)
                if c == 0:
                    dve.wait_ge(dn1_done, 4)
                nc.vector.tensor_copy(B1[:, 4 * c:4 * c + 4, :],
                                      bank[4 + c % 2][:, 0:4 * T].rearrange("p (k t) -> p k t", t=T)).then_inc(dn2_fm, 1)
                if c >= 1:
                    evac_dn2(c - 1)
            evac_dn2(7)
            dve.wait_ge(idx_in, 32)
            dve.wait_ge(idx_set, 8)
            for view in (src_by_node, dst_by_node):
                nc.vector.tensor_scalar(view[:, 0:EP], view[:, 0:EP].bitcast(I32), node_col[0:T, 0:1], None, ALU.is_equal
                                        ).then_inc(hot_ready, 1)
            dve.wait_ge(con_done, 8)
            for n in range(2):
                cols = slice(n * BANK, (n + 1) * BANK)
                nc.vector.tensor_tensor(x[:, cols], x[:, cols], bank[n][0:T, :], ALU.add).then_inc(x2_ready, 1)
            dve.wait_ge(x2_ready, 2)
            layer_norm()
            dve.wait_ge(xn_ready, 3)
            take_xT(4, rmsw)
            nc.vector.scalar_tensor_tensor(out=tok[:, 1, :], in0=xn[:], scalar=1.0 / D, in1=xn[:],
                                           op0=ALU.mult, op1=ALU.mult, accum_out=ms[:]).then_inc(ms_ready, 1)
            dve.wait_ge(ms_ready, 1)
            nc.vector.tensor_scalar(ms[:], ms[:], RMS_EPS, None, ALU.add).then_inc(ms_ready, 1)
            dve.wait_ge(rms_ready, 1)
            dve.wait_ge(wd_done, 1)
            nc.vector.tensor_scalar(tok[:, 0, 0:G1], bank[6][0:T, 0:G1], rms[:], None, ALU.mult).then_inc(wd_tok, 1)
            dve.wait_ge(wd_turned, 1)
            nc.vector.tensor_copy(fmv[2][:, 0:2, :], bank[4][:, 0:2 * T].rearrange("p (k t) -> p k t", t=T)
                                  ).then_inc(wd_fm, 1)

            def leaky(c):
                w = min(BANK, EL - c * BANK)
                for f in range(2):
                    i = 2 * c + f
                    dve.wait_ge(z_scaled, i + 1)
                    nc.vector.tensor_tensor(msg[:, f, c * BANK:c * BANK + w], fm[:, i % 2, 0:w], bank[i % 4][:, 0:w],
                                            ALU.max).then_inc(msg_ready, 1)

            def weigh(c):
                dve.wait_ge(e_done, c + 1)
                for t0, n, w, hot in (((4 * c, 4, P, src_live[:, 4 * c:4 * c + 4, :]),) if c < 3 else
                                      ((ET - 1, 1, P, src_live[:, ET - 1:ET, :]), (ET, 1, T, ident[0:T, None, 0:T]))):
                    step(nc.vector.tensor_copy(e_sb[0:w, t0:t0 + n, :].rearrange("p t h -> p (t h)"),
                                               bank[(5, 7)[c % 2]][0:w, t0 * H1:(t0 + n) * H1]))
                    nc.vector.tensor_tensor(edge_rhs[0:w, t0:t0 + n, :, :],
                                            hot[:, :, None, :].broadcast_to([w, n, H1, T]),
                                            e_sb[0:w, t0:t0 + n, :, None].broadcast_to([w, n, H1, T]),
                                            ALU.mult).then_inc(rhs_ready, 1)

            leaky(0)
            leaky(1)
            weigh(0)
            leaky(2)
            weigh(1)
            leaky(3)
            weigh(2)
            weigh(3)
            dve.wait_ge(pair_done, 1)
            pr = S3[:, 0:H1, :]
            step(nc.vector.tensor_tensor(pr, bank[6][0:T, 0:H1 * T].rearrange("p (h t) -> p h t", t=T),
                                         absent[:, None, :].broadcast_to([T, H1, T]), ALU.add))
            step(nc.vector.tensor_reduce(mx[:, 0:H1], pr, AX.X, ALU.max))
            nc.vector.tensor_tensor(pr, pr, mx[:, 0:H1, None].broadcast_to([T, H1, T]), ALU.subtract).then_inc(pair_shift, 1)
            dve.wait_ge(pair_exp, 1)
            step(nc.vector.tensor_tensor(pr, pr, count[:, None, :].broadcast_to([T, H1, T]), ALU.mult))
            step(nc.vector.tensor_reduce(den[:, 0:H1], pr, AX.X, ALU.add))
            step(nc.vector.tensor_scalar(den[:, 0:H1], den[:, 0:H1], 1e-16, None, ALU.add))
            step(nc.vector.reciprocal(den[:, 0:H1], den[:, 0:H1]))
            nc.vector.tensor_tensor(pr, pr, den[:, 0:H1, None].broadcast_to([T, H1, T]), ALU.mult).then_inc(alpha_ready, 1)
            dve.wait_ge(alpha_turned, 1)
            nc.vector.tensor_copy(S3[:, H1:2 * H1, :], bank[4][0:T, 0:H1 * T].rearrange("p (h t) -> p h t", t=T)
                                  ).then_inc(alphaT_ready, 1)
            dve.wait_ge(agg_done, 1)
            nc.vector.tensor_copy(fmv[2][:, 0:2, :], bank[5][:, 0:2 * T].rearrange("p (k t) -> p k t", t=T)
                                  ).then_inc(agg_ready, 1)
            for n in range(2):
                cols = slice(n * BANK, (n + 1) * BANK)
                dve.wait_ge(up_done, n + 1)
                nc.vector.tensor_tensor(x[:, cols], x[:, cols], bank[n][0:T, :], ALU.add).then_inc(x2_ready, 1)
            dve.wait_ge(x2_ready, 4)
            layer_norm()
            take_xT(6)
            dve.wait_ge(xT_ready, 8)
            nc.vector.tensor_reduce(pooled[:], xT[:, :, :].rearrange("p k t -> p t k"), AX.X, ALU.add).then_inc(xT_ready, 1)
            for n in range(2):
                cols = slice(n * BANK, (n + 1) * BANK)
                dve.wait_ge(fin_done, n + 1)
                nc.vector.tensor_tensor(xn[:, cols], x[:, cols], bank[2 + n][0:T, :], ALU.add).then_inc(fin_ready, 1)


def lay_out(i):
    import numpy as np

    a = {k: np.asarray(v) for k, v in i.items()}

    def tiles(w):
        return w.reshape(-1, P, w.shape[1]).transpose(1, 0, 2).reshape(P, -1)

    def halves(w):
        return [tiles(w[:, n * BANK:(n + 1) * BANK]) for n in range(w.shape[1] // BANK)]

    slabs = []
    for n in GNN:
        slabs += halves(a["L0_gnn_w" + n].T)
    slabs += halves(a["L0_ffn_W_exp"])
    con = a["L0_ffn_W_con"].reshape(GRP, NT, 2, D).transpose(2, 0, 1, 3).reshape(P, NT, D)
    slabs += [con[:, 4 * s:4 * s + 4].reshape(P, SLAB) for s in range(CON_SLABS)]
    slabs += halves(a["L1_ffn_weight"].T)

    def coefs(w):
        low, high = [], []
        for s in range(STAGES):
            v = w[s].reshape(NT, 2, 2 ** (5 - s), 2 ** s, 2, 2)
            low.append(v.transpose(1, 2, 5, 0, 4, 3).reshape(-1))
            v = w[s + 6].reshape(2 ** (5 - s), 2 ** s, NT, 2, 2, 2)
            high.append(v.transpose(3, 0, 5, 2, 4, 1).reshape(-1))
        return [np.stack(low), np.stack(high)]

    full = (ET - 1) * P
    r = {
        "x": a["x"],
        "stream": np.stack(slabs),
        "coef": np.stack(coefs(a["L0_ffn_up_weights"]) + coefs(a["L0_ffn_down_weights"])),
        "bo": a["L0_gnn_bo"].reshape(1, D),
        "b_con": a["L0_ffn_b_con"].reshape(1, D),
        "down_bias": a["L0_ffn_down_bias"].reshape(1, D),
        "bias_fm": np.stack([a["L0_gnn_b" + n].reshape(KD, P).T for n in ("q", "k", "iq", "ik", "v", "iv")]),
        "b_exp": a["L0_ffn_b_exp"].reshape(NT, P).T,
        "up_bias": a["L0_ffn_up_bias"].reshape(NT, P).T,
        "rms_w": a["L1_gnn_rms_w"].reshape(KD, P).T,
        "att": a["L1_gnn_att"].reshape(H1, 64, 1),
        "etw": a["L0_gnn_edge_type_weights"].reshape(1, 4),
        "w_down": tiles(a["L1_gnn_W_down"]),
        "w_l": a["L1_gnn_Wl"].reshape(2, P, G1).transpose(1, 0, 2),
        "w_r": a["L1_gnn_Wr"].reshape(2, P, G1).transpose(1, 0, 2),
        "w_up": tiles(a["L1_gnn_W_up"]),
        "disha": a["L1_ffn_disha"],
    }
    for name, key in (("src", "src"), ("dst", "dst"), ("etype", "edge_type_5")):
        v = a[key]
        r[name] = v.reshape(1, E)
        r[name + "_cols"] = v[:full].reshape(ET - 1, P).T
        r[name + "_tail"] = v[full:].reshape(E - full, 1)
    return {k: np.ascontiguousarray(v) for k, v in r.items()}


def kernel(**inputs):
    import concourse.bacc as bacc
    from concourse.bass_utils import run_bass_kernel_spmd

    nc = bacc.Bacc("TRN2", target_bir_lowering=False, num_devices=1)
    arrays = lay_out(inputs)
    A = {k: nc.dram_tensor(f"in_{k}", v.shape, mybir.dt.from_np(v.dtype), kind="ExternalInput").ap()
         for k, v in arrays.items()}
    out = nc.dram_tensor("out", (T, D), F32, kind="ExternalOutput").ap()
    program(nc, A, out)
    r = run_bass_kernel_spmd(nc, [{f"in_{k}": v for k, v in arrays.items()}], core_ids=[0])
    return r.results[0]["out"]
```

```python
from contextlib import ExitStack

import concourse.bass as bass
from concourse import mybir

F32 = mybir.dt.float32
F32R = mybir.dt.float32r
I32 = mybir.dt.int32
BF16 = mybir.dt.bfloat16
ALU = mybir.AluOpType
ACT = mybir.ActivationFunctionType
AX = mybir.AxisListType

P = 128
BANK = 512
T = 96
D = 1024
KD = D // P
HID = 4096
HEADS, HD = 16, 64
E = 1632
ET = (E + P - 1) // P
EP = ET * P
EL = EP + T
LT = ET + 1
G1 = 256
H1 = 4
SLOTS = 3
SLAB = 4096
STAGES = 6
GRP = 64
NT = HID // P
COEF = GRP * 2 * GRP
BIG = 1.0e30
LN_EPS, RMS_EPS = 1e-5, 1e-6
GNN = ["q", "k", "iq", "ik", "v", "iv", "o"]
GNN_SLABS = 2 * len(GNN)
EXP_SLABS = 8
CON_SLABS = 8
STAGED = 24
FEATS = 7 * KD + 2 * NT + 2 * H1
PARTS = 4
PART = SLAB // PARTS
NSPLIT = 3
EDGE_SLABS = 8
STREAM = GNN_SLABS + EXP_SLABS + CON_SLABS


def slot_of(slab):
    return slab % SLOTS if slab < STREAM else (2, 0)[slab - STREAM]


def split_parts(slab):
    if slab < EDGE_SLABS:
        return 0 if slab == 0 else 2 if slab < EDGE_SLABS // 2 else 1
    return 3 if slab < GNN_SLABS else PARTS


def split_no(slab, part):
    return sum(split_parts(i) for i in range(slab)) + min(part, split_parts(slab) if slab < STREAM + 2 else 0)


def part_of_split(n):
    slab = 0
    while n >= split_parts(slab):
        n -= split_parts(slab)
        slab += 1
    return slab, n


def program(nc, A, out):
    with ExitStack() as ctx:
        def sb(name, shape, dt=F32):
            return ctx.enter_context(nc.sbuf_tensor(name, shape, dt))

        def sem(name):
            return ctx.enter_context(nc.semaphore(name))

        ring = sb("ring", [P, SLOTS, SLAB])
        part_hi = sb("part_hi", [P, NSPLIT, PART], F32R)
        part_lo = sb("part_lo", [P, NSPLIT, PART], F32R)
        x = sb("x", [T, D])
        bcs = sb("bcs", [T, D])
        xT = sb("xT", [P, KD, T])
        xT_hi = sb("xT_hi", [P, KD, T], F32R)
        xT_lo = sb("xT_lo", [P, KD, T], F32R)
        tok = sb("tok", [T, 2, D])
        xn = tok[:, 0, :]
        dst_hot = sb("dst_hot", [P, ET, T])
        src_live = sb("src_live", [P, ET, T])
        edge_cols = sb("edge_cols", [P, 3, ET], I32)
        src_col, dst_col, type_col = (edge_cols[:, i, :] for i in range(3))
        key_col = sb("key_col", [P, ET])
        code = sb("code", [P, ET])
        later = sb("later", [P, ET])
        live = sb("live", [P, ET])
        stands = sb("stands", [P, ET])
        live_code = sb("live_code", [P, ET])
        node_row = sb("node_row", [P, T])
        node_col = sb("node_col", [P, 1])
        ident = sb("ident", [P, P])
        ones = sb("ones", [1, T])
        by_feature = sb("by_feature", [P, FEATS])
        bias_fm = by_feature[:, 0:6 * KD].rearrange("p (i k) -> p i k", i=6)
        bexp = by_feature[:, 6 * KD:6 * KD + NT]
        upb = by_feature[:, 6 * KD + NT:6 * KD + 2 * NT]
        rmsw = by_feature[:, 6 * KD + 2 * NT:7 * KD + 2 * NT]
        att = by_feature[:, 7 * KD + 2 * NT:FEATS].rearrange("p (f h) -> p f h", f=2)
        etw = sb("etw", [T, 4])
        sp_t = sb("sp_t", [T, 4, 4])
        mask = sb("mask", [T, T])
        mtmp = sb("mtmp", [T, 3, T])
        count = sb("count", [T, T])
        absent = sb("absent", [T, T])
        stats = sb("stats", [T, 2, 6])
        mv = sb("mv", [T, 2])
        rstd = sb("rstd", [T, 1])
        minus_half = sb("minus_half", [T, 1])
        ms = sb("ms", [T, 1])
        rms = sb("rms", [T, 1])
        mx = sb("mx", [T, HEADS])
        den = sb("den", [T, HEADS])
        e_sb = sb("e_sb", [P, LT, H1])
        pooled = sb("pooled", [P, T])

        def phase(*tensors):
            with ExitStack() as space:
                return [space.enter_context(nc.sbuf_tensor(name, shape, dt)) for name, shape, dt in tensors]

        MIX = (("low{}", [P, NT, P], F32), ("high{}", [P, NT, P], F32))

        def mixes(n):
            return [(name.format(n), shape, dt) for name, shape, dt in MIX]

        mix_low, mix_high, stage, ends, after, fm, fm_hi, fm_lo = phase(
            *mixes(1),
            ("stage", [P, HID], F32),
            ("ends", [P, 2, EP], F32),
            ("after", [P, EP], BF16),
            ("fm", [P, 3, KD * T], F32),
            ("fm_hi", [P, 2, KD * T], F32R),
            ("fm_lo", [P, 2, KD * T], F32R))
        keys, dst_bc = ends[:, 0, :], ends[:, 1, :]
        junk = dst_bc.bitcast(BF16)[:, 0:EP]
        _, _, _, src_hot, dst_code, S3 = phase(
            *mixes("_1b"),
            ("stage_1b", [P, HID], F32),
            ("src_hot", [P, ET, T], F32),
            ("dst_code", [P, ET, T], F32),
            ("scores", [T, HEADS, T], F32))
        _, _, _, PT = phase(
            *mixes("_1c"),
            ("stage_1c", [P, HID], F32),
            ("probs_by_source", [T, HEADS, T], F32))
        _, _, V, B0, B1, U, cur_even, cur_odd = phase(
            *mixes("_2"),
            ("V", [P, HID], F32),
            ("B0", [P, NT, T], F32),
            ("B1", [P, NT, T], F32),
            ("U", [P, HID], F32),
            ("cur_even", [P, NT * 32], F32),
            ("cur_odd", [P, NT * 16], F32))
        by_node, _, z_lo, z_hi = phase(
            ("by_node", [P, 2, NT * GRP], F32),
            ("high_2b", [P, NT, P], F32),
            ("z_lo", [P, HID], F32R),
            ("z_hi", [P, NT, T], F32R))
        z_lo = z_lo[:, 0:NT * T].rearrange("p (n t) -> p n t", t=T)
        _, hot_by_node, edge_rhs, lr_hi, lr_lo, alpha, small_fm, msg = phase(
            ("by_node_3", [P, 2, NT * GRP], F32),
            ("hot_by_node", [P, 2, NT * GRP], F32R),
            ("edge_rhs", [P, LT, H1, T], F32),
            ("lr_hi", [T, 2 * G1], F32R),
            ("lr_lo", [T, 2 * G1], F32R),
            ("alpha", [T, 2 * H1, T], F32),
            ("small_fm", [P, 3, KD * T], F32),
            ("msg", [P, 2, EL], F32))

        bank = [ctx.enter_context(nc.psum_tensor(f"bank{i}", [P, BANK], F32)) for i in range(8)]

        rows = mix_high[0:T, :, :].rearrange("p a n -> p (a n)")[:, 0:3 * D].rearrange("p (a n) -> p a n", a=3)
        by_group = U[:, :].rearrange("p (c g x) -> p g x c", g=NT, x=2)
        by_place = V[:, :].rearrange("p (g r x) -> p r x g", r=NT, x=2)
        S = S3[:, :, :].rearrange("p h t -> p (h t)")
        fmv, fm_hiv, fm_lov = ([f[:, i, :].rearrange("p (k t) -> p k t", t=T) for i in range(n)]
                               for f, n in ((fm, 3), (fm_hi, 2), (fm_lo, 2)))
        sfm = [small_fm[:, i, :].rearrange("p (k t) -> p k t", t=T) for i in range(3)]
        src_by_node = hot_by_node[0:T, 0, 0:EL]
        dst_by_node = hot_by_node[0:T, 1, 0:EL]

        x_in = sem("x_in")
        rows_in = sem("rows_in")
        edge_in, ends_in = sem("edge_in"), sem("ends_in")
        small_in = sem("small_in")
        slab_in = [sem(f"slab_in{i}") for i in range(SLOTS)]
        down_in, up_in = sem("down_in"), sem("up_in")
        hi_ready, lo_ready = sem("hi_ready"), sem("lo_ready")
        part_used = sem("part_used")
        coef_in = [sem(f"coef_in{i}") for i in range(4)]
        consts = sem("consts")
        hot_made, pool_hot = sem("hot_made"), sem("pool_hot")
        composed, zeroed = sem("composed"), sem("zeroed")
        running, upper_composed = sem("running"), sem("upper_composed")
        biased, bcs_ready = sem("biased"), sem("bcs_ready")
        xn_ready = sem("xn_ready")
        var_ready, rstd_ready = sem("var_ready"), sem("rstd_ready")
        ms_ready, rms_ready = sem("ms_ready"), sem("rms_ready")
        xT_turned, xT_ready = sem("xT_turned"), sem("xT_ready")
        tok_ready = [sem(f"tok_ready_{n}") for n in GNN]
        turned = [sem(f"turned_{n}") for n in GNN]
        fm_ready = [sem(f"fm_ready_{n}") for n in GNN]
        live_ready = sem("live_ready")
        counts_done, counts_read = sem("counts_done"), sem("counts_read")
        soft_ready = sem("soft_ready")
        scores_done, scores_read = sem("scores_done"), sem("scores_read")
        shifted, exped = sem("shifted"), sem("exped")
        probs_ready = sem("probs_ready")
        probs_turned, probsT_ready = sem("probs_turned"), sem("probsT_ready")
        attended, attended_read = sem("attended"), sem("attended_read")
        exp_tok = sem("exp_tok")
        exp_turned, exp_fm = sem("exp_turned"), sem("exp_fm")
        up1_done, up1_read = sem("up1_done"), sem("up1_read")
        up2_turned, up2_fm = sem("up2_turned"), sem("up2_fm")
        up2_done, up2_read0, up2_read1 = sem("up2_done"), sem("up2_read0"), sem("up2_read1")
        act_turned, act_biased, act_fm = sem("act_turned"), sem("act_biased"), sem("act_fm")
        dn1_done, dn1_read0, dn1_read1 = sem("dn1_done"), sem("dn1_read0"), sem("dn1_read1")
        dn2_turned, dn2_fm = sem("dn2_turned"), sem("dn2_fm")
        dn2_done, dn2_read0, dn2_read1 = sem("dn2_done"), sem("dn2_read0"), sem("dn2_read1")
        x2_ready = sem("x2_ready")
        idx_in, hot_ready = sem("idx_in"), sem("hot_ready")
        wd_done, wd_tok, wd_turned, wd_fm = sem("wd_done"), sem("wd_tok"), sem("wd_turned"), sem("wd_fm")
        lr_done, lr_ready = sem("lr_done"), sem("lr_ready")
        lr_split = sem("lr_split")
        z_done, z_scaled, msg_ready = sem("z_done"), sem("z_scaled"), sem("msg_ready")
        e_done, rhs_ready = sem("e_done"), sem("rhs_ready")
        pair_done, pair_shift, pair_exp, alpha_ready = (
            sem("pair_done"), sem("pair_shift"), sem("pair_exp"), sem("alpha_ready"))
        alpha_turned, alphaT_ready = sem("alpha_turned"), sem("alphaT_ready")
        agg_done, agg_ready = sem("agg_done"), sem("agg_ready")
        up_done = sem("up_done")
        fin_done, fin_ready = sem("fin_done"), sem("fin_ready")
        out_done = sem("out_done")
        dve_step, act_step, pool_step = sem("dve_step"), sem("act_step"), sem("pool_step")

        block = ctx.enter_context(nc.Block())

        def take_step(to, m, pair, j, copy):
            first = 8 * m + 4 * j
            return copy(to[0:T, first:first + 4, :, :],
                        bank[pair + j][0:T, :].rearrange("p (n x c) -> p n x c", n=4, x=2))

        SCORE = ((6, 7), (0, 1))
        UPT = (4, 5, 0, 1, 2, 3, 4, 5)

        @block.sync
        def _(sp):
            def load(i):
                sp.dma_start(ring[:, i % SLOTS, :], A["stream"][i]).then_inc(slab_in[i % SLOTS], 16)

            def load_round(r):
                for s in range(SLOTS):
                    yield s
                    sp.dma_start(ring[:, s, :],
                                 A["stream"][bass.ds(r * SLOTS + s, 1)].rearrange("o p n -> (o p) n")
                                 ).then_inc(slab_in[s], 16)

            sp.dma_start(x[:], A["x"]).then_inc(x_in, 16)
            for i in range(SLOTS):
                load(i)
            rounds = GNN_SLABS // SLOTS
            with sp.Fori(1, rounds + 1) as r:
                for s in load_round(r):
                    sp.wait_ge(part_used, (r * SLOTS + s - SLOTS + 1) * PARTS)
            for i in range((rounds + 1) * SLOTS, GNN_SLABS + SLOTS):
                sp.wait_ge(part_used, (i - SLOTS + 1) * PARTS)
                load(i)
            def split_round(r):
                for s in load_round(r):
                    sp.wait_ge(lo_ready, (r * SLOTS + s - SLOTS - GNN_SLABS + 1) * PARTS + split_no(GNN_SLABS, 0))

            start = GNN_SLABS + SLOTS
            for i in range(start, -(-start // SLOTS) * SLOTS):
                sp.wait_ge(lo_ready, split_no(i - SLOTS, PARTS - 1) + 1)
                load(i)
            with sp.Fori(-(-start // SLOTS), STAGED // SLOTS) as r:
                split_round(r)
            sp.wait_ge(composed, 4)
            load(STAGED)
            for i in range(STAGED + 1, STAGED + SLOTS):
                sp.wait_ge(lo_ready, split_no(i - SLOTS, PARTS - 1) + 1)
                load(i)
            with sp.Fori(STAGED // SLOTS + 1, STREAM // SLOTS) as r:
                split_round(r)
            sp.wait_ge(lo_ready, split_no(STREAM - SLOTS, PARTS - 1) + 1)
            sp.dma_start(ring[:, 0, 0:2048], A["w_down"]).then_inc(down_in, 16)
            sp.dma_start(ring[:, 0, 2048:3072].rearrange("p (k n) -> p k n", k=2)[:, :, 0:G1], A["w_l"]).then_inc(down_in, 16)
            sp.dma_start(ring[:, 0, 2048:3072].rearrange("p (k n) -> p k n", k=2)[:, :, G1:], A["w_r"]).then_inc(down_in, 16)
            sp.wait_ge(lo_ready, split_no(STREAM - SLOTS + 1, PARTS - 1) + 1)
            sp.dma_start(ring[:, 1, 0:2048], A["w_up"]).then_inc(up_in, 16)
            sp.dma_start(ring[0:64, 1, 2048:3072], A["disha"]).then_inc(up_in, 16)
            sp.dma_start(ring[64:128, 1, 2048:3072], A["disha"]).then_inc(up_in, 16)
            sp.wait_ge(lo_ready, split_no(STREAM - 1, PARTS - 1) + 1)
            sp.dma_start(ring[:, 2, :], A["stream"][STREAM]).then_inc(slab_in[2], 16)
            sp.wait_ge(lr_done, 1)
            sp.dma_start(ring[:, 0, :], A["stream"][STREAM + 1]).then_inc(slab_in[0], 16)
            for n in range(2):
                sp.wait_ge(fin_ready, n + 1)
                sp.dma_start(out[:, n * BANK:(n + 1) * BANK], xn[:, n * BANK:(n + 1) * BANK]).then_inc(out_done, 16)
            sp.wait_ge(out_done, 32)

        @block.gpsimd
        def _(pool):
            stages = [stage] * 3 + [ring[:, STAGED % SLOTS, :]]

            def coefs(k):
                src = A["coef"][k]
                stage = stages[k]
                for s in range(STAGES):
                    rows = 2 ** (STAGES + 1 - s)
                    width = NT * 2 ** (s + 1)
                    at = NT * (2 ** (s + 1) - 2)
                    row_src = src[s].rearrange("(r f) -> r f", r=rows)
                    pool.dma_start(stage[:, at:at + width],
                                   row_src[:, None, :].broadcast_to([rows, 2 ** s, width])
                                   ).then_inc(coef_in[k], 16)

            nc.gpsimd.memset(ident[:], 0.0).then_inc(pool_step, 1)
            nc.gpsimd.memset(ones[:], 1.0).then_inc(consts, 1)
            nc.gpsimd.memset(minus_half[:], -0.5).then_inc(pool_step, 1)
            pool.wait_ge(pool_step, 2)
            nc.gpsimd.affine_select(out=ident[:], in_=ident[:], compare_op=ALU.not_equal, fill=1.0, base=0,
                                    pattern=[[-1, P]], channel_multiplier=1).then_inc(consts, 1)
            def root(n):
                pool.wait_ge(var_ready, n)
                nc.gpsimd.tensor_tensor(rstd[:], mv[:, 1:2], minus_half[:], ALU.pow).then_inc(rstd_ready, 1)

            root(1)
            nc.gpsimd.iota(node_row[:], pattern=[[1, T]], base=0, channel_multiplier=0,
                           allow_small_or_imprecise_dtypes=True).then_inc(consts, 1)
            nc.gpsimd.iota(node_col[:], pattern=[[0, 1]], base=0, channel_multiplier=1,
                           allow_small_or_imprecise_dtypes=True).then_inc(consts, 1)
            nc.gpsimd.memset(after[:], 1.0).then_inc(pool_step, 1)
            pool.wait_ge(pool_step, 3)
            nc.gpsimd.affine_select(out=after[:], in_=after[:], compare_op=ALU.is_gt, fill=0.0, base=0,
                                    pattern=[[1, EP]], channel_multiplier=-1).then_inc(consts, 1)
            pool.wait_ge(slab_in[2], 16)
            pool.dma_start(ends[:, :, :].bitcast(I32), A["ends"][None, :, :].broadcast_to([P, 2, EP])).then_inc(ends_in, 16)
            pool.wait_ge(slab_in[0], 32)
            pool.dma_start(rows, A["rows"][None, :, :].broadcast_to([T, 3, D])).then_inc(rows_in, 16)
            pool.wait_ge(rows_in, 16)
            pool.wait_ge(xn_ready, 1)
            nc.gpsimd.tensor_tensor(x[:], x[:], rows[:, 0, :], ALU.add).then_inc(biased, 1)
            nc.gpsimd.tensor_tensor(bcs[:], rows[:, 1, :], rows[:, 2, :], ALU.add).then_inc(bcs_ready, 1)
            pool.wait_ge(biased, 1)
            pool.wait_ge(bcs_ready, 1)
            for m in (mix_low, mix_high):
                nc.gpsimd.memset(m[:, :, :].rearrange("p n c -> p (n c)"), 0.0).then_inc(zeroed, 1)
            pool.wait_ge(hot_made, 2)
            pool.wait_ge(live_ready, 1)
            nc.gpsimd.tensor_tensor(src_live[:], src_hot[:], stands[:, :, None].broadcast_to([P, ET, T]),
                                    ALU.mult).then_inc(pool_hot, 1)
            nc.gpsimd.tensor_tensor(dst_code[:], dst_hot[:], live_code[:, :, None].broadcast_to([P, ET, T]),
                                    ALU.mult).then_inc(pool_hot, 1)
            pool.wait_ge(slab_in[10 % SLOTS], 16 * (10 // SLOTS + 1))
            coefs(0)
            done = 3
            for k in range(4):
                mix = (mix_low, mix_high)[k % 2]
                pool.wait_ge(coef_in[k], 16 * STAGES)
                cur = stages[k][:, 0:NT * 2].rearrange("p (g n) -> p g n", g=NT)
                for s in range(1, STAGES):
                    n = 2 ** s
                    at = NT * (2 * n - 2)
                    coef = stages[k][:, at:at + NT * 2 * n].rearrange("p (g b n) -> p g b n", g=NT, b=2)
                    if s < STAGES - 1:
                        dst = (cur_even, cur_odd)[s % 2][:, 0:NT * 2 * n]
                        new = dst.rearrange("p (g b n) -> p g b n", g=NT, b=2)
                        ins = nc.gpsimd.tensor_tensor(new, cur[:, :, None, :].broadcast_to([P, NT, 2, n]), coef, ALU.mult)
                        if k == 2 and s == STAGES - 2:
                            ins.then_inc(running, 1)
                            pool.wait_ge(running, 1)
                        else:
                            ins.then_inc(pool_step, 1)
                            done += 1
                            pool.wait_ge(pool_step, done)
                        cur = dst.rearrange("p (g n) -> p g n", g=NT)
                        continue
                    if k < 2:
                        pool.wait_ge(zeroed, k + 1)
                    if k == 2:
                        pool.wait_ge(lo_ready, split_no(STAGED - SLOTS, PARTS - 1) + 1)
                        coefs(3)
                        pool.wait_ge(up1_done, 4)
                    if k == 3:
                        pool.wait_ge(up2_done, 4)
                    for h in range(1 if k == 2 else 2):
                        hs = slice(64 * h, 64 * h + 64)
                        new = mix[hs, :, 64 * h:64 * h + 64].rearrange("p g (b n) -> p g b n", b=2)
                        ins = nc.gpsimd.tensor_tensor(new, cur[hs, :, None, :].broadcast_to([64, NT, 2, n]),
                                                      coef[hs], ALU.mult)
                        if h == 0 and k != 2:
                            ins.then_inc(pool_step, 1)
                            done += 1
                            pool.wait_ge(pool_step, done)
                    ins.then_inc(composed, 1)
                    pool.wait_ge(composed, k + 1)
                if k < 2:
                    coefs(k + 1)
                if k == 0:
                    root(2)
                if k == 2:
                    pool.wait_ge(upper_composed, 1)
            root(3)
            pool.wait_ge(ms_ready, 2)
            nc.gpsimd.tensor_tensor(rms[:], ms[:], minus_half[:], ALU.pow).then_inc(rms_ready, 1)
            root(4)

        @block.scalar
        def _(act):
            act.dma_start(edge_cols[:], A["edge_cols"]).then_inc(edge_in, 16)
            act.dma_start(by_feature[:], A["by_feature"]).then_inc(small_in, 16)
            act.dma_start(etw[:], A["etw"].broadcast_to([T, 4])).then_inc(small_in, 16)
            act.wait_ge(small_in, 32)
            nc.scalar.activation(sp_t[:, 0, :], etw[:], ACT.Abs).then_inc(act_step, 1)
            act.wait_ge(act_step, 1)
            nc.scalar.activation(sp_t[:, 1, :], sp_t[:, 0, :], ACT.Exp, scale=-1.0).then_inc(act_step, 1)
            act.wait_ge(act_step, 2)
            nc.scalar.activation(sp_t[:, 2, :], sp_t[:, 1, :], ACT.Ln, bias=1.0).then_inc(soft_ready, 1)

            splits = [0]

            def split_until(slab, part):
                while splits[0] < split_no(slab, part):
                    n = splits[0]
                    i, c = part_of_split(n)
                    if c == 0:
                        act.wait_ge(slab_in[slot_of(i)], 16 * (i // SLOTS + 1))
                    if n >= NSPLIT:
                        j, d = part_of_split(n - NSPLIT)
                        act.wait_ge(part_used, PARTS * j + d + 1)
                    nc.scalar.copy(part_hi[:, n % NSPLIT, :], ring[:, slot_of(i), c * PART:(c + 1) * PART]
                                   ).then_inc(hi_ready, 1)
                    splits[0] += 1

            def copy_probs(c):
                act.wait_ge(probs_turned, c + 1)
                nc.scalar.copy(PT[:, 4 * c:4 * c + 4, :], bank[4 + c][0:T, 0:4 * T].rearrange("p (h t) -> p h t", t=T)
                               ).then_inc(probsT_ready, 1)

            for j in range(6):
                for n in range(2):
                    split_until(2 * j + n + 2, 0)
                    act.wait_ge(part_used, PARTS * (2 * j + n + 1))
                    if j >= 2:
                        act.wait_ge(turned[j - 2], 2)
                    nc.scalar.copy(tok[:, j % 2, n * BANK:(n + 1) * BANK],
                                   bank[2 * (j % 2) + n][0:T, :]).then_inc(tok_ready[j], 1)
                    if j == 5 and n == 0:
                        copy_probs(1)
                    if j == 4 and n == 1:
                        split_until(2 * j + 3, 0)
                        for g in range(2):
                            act.wait_ge(shifted, g + 1)
                            nc.scalar.activation(S[:, g * 768:(g + 1) * 768], S[:, g * 768:(g + 1) * 768],
                                                 ACT.Exp).then_inc(exped, 1)
            copy_probs(3)

            def evac_up1(m):
                act.wait_ge(up1_done, m + 1)
                for h in range(2):
                    take_step(by_group, m, 6, h, nc.scalar.copy).then_inc(up1_read, 1)

            for n in range(EXP_SLABS):
                split_until(GNN_SLABS + n, PARTS)
                if n >= 4 and n % 2 == 0:
                    evac_up1((n - 4) // 2)
                split_until(GNN_SLABS + n + 1, 2)
                act.wait_ge(part_used, PARTS * (GNN_SLABS + n + 1))
                if n >= 2:
                    act.wait_ge(exp_turned, n - 1)
                nc.scalar.copy(tok[:, n % 2, 0:BANK], bank[n % 4][0:T, :]).then_inc(exp_tok, 1)
            evac_up1(2)
            evac_up1(3)
            act.wait_ge(composed, 3)
            act.wait_ge(upper_composed, 1)
            for m in range(4):
                act.wait_ge(up2_done, m + 1)
                take_step(by_place, m, (6, 2)[m % 2], 0, nc.scalar.copy).then_inc(up2_read0, 1)

            def gelu(c):
                act.wait_ge(act_biased, c + 1)
                g = B1[:, 4 * c:4 * c + 4, :]
                nc.scalar.activation(g, g, ACT.Gelu).then_inc(act_fm, 1)

            def evac_dn1(m):
                act.wait_ge(dn1_done, m + 1)
                take_step(by_group, m, (6, 2)[m % 2], 0, nc.scalar.copy).then_inc(dn1_read0, 1)

            for c in range(8):
                gelu(c)
                if c >= 6:
                    evac_dn1(c - 6)
            evac_dn1(2)
            evac_dn1(3)
            act.dma_start(by_node[0:T, :, 0:EP].bitcast(I32), A["ends"][None, :, :].broadcast_to([T, 2, EP])).then_inc(idx_in, 16)
            for c in range(8):
                act.wait_ge(dn2_done, c + 1)
                nc.scalar.copy(z_hi[:, 4 * c:4 * c + 4, :],
                               bank[(6, 2)[c % 2]][:, 0:4 * T].rearrange("p (r t) -> p r t", t=T)).then_inc(dn2_read0, 1)
                if c >= 1:
                    split_until(GNN_SLABS + EXP_SLABS + c - 1, 3 if c == 1 else 2)
            split_until(STREAM, NSPLIT)
            act.wait_ge(lr_done, 1)
            nc.scalar.copy(lr_hi[:], bank[7][0:T, :]).then_inc(lr_split, 1)
            act.wait_ge(lr_split, 2)
            nc.scalar.copy(tok[:, 1, 0:BANK], bank[7][0:T, :]).then_inc(lr_ready, 1)
            for i in range(8):
                c, f = i // 2, i % 2
                w = min(BANK, EL - c * BANK)
                act.wait_ge(z_done, i + 1)
                if i >= 2:
                    act.wait_ge(msg_ready, i - 1)
                nc.scalar.mul(small_fm[:, i % 2, 0:w], bank[i % 4][:, 0:w], 0.2).then_inc(z_scaled, 1)
            act.wait_ge(pair_shift, 1)
            nc.scalar.activation(alpha[:, 0:H1, :], alpha[:, 0:H1, :], ACT.Exp).then_inc(pair_exp, 1)
            split_until(STREAM + 2, 0)

        @block.tensor
        def _(pe):
            def part(i, c, lhs, dst, first, last):
                n = split_no(i, c)
                split = c < split_parts(i)
                if split:
                    pe.wait_ge(lo_ready, n + 1)
                    hi, lo = part_hi[:, n % NSPLIT, :], part_lo[:, n % NSPLIT, :]
                else:
                    pe.wait_ge(slab_in[slot_of(i)], 16 * (i // SLOTS + 1))
                    raw = ring[:, slot_of(i), c * PART:(c + 1) * PART]
                for k in range(2):
                    cols = slice(k * BANK, (k + 1) * BANK)
                    tile = 2 * c + k if len(dst) == 1 else c
                    b = dst[k % len(dst)][0:T, :]
                    start = first and (k == 0 or len(dst) == 2)
                    stop = last and (k == 1 or len(dst) == 2)
                    if split:
                        nc.tensor.matmul(b, lhs[1][:, tile, :], hi[:, cols], start=start, stop=False)
                        nc.tensor.matmul(b, lhs[1][:, tile, :], lo[:, cols], start=False, stop=False)
                        mm = nc.tensor.matmul(b, lhs[2][:, tile, :], hi[:, cols], start=False, stop=stop)
                    else:
                        mm = nc.tensor.matmul(b, lhs[0][:, tile, :], raw[:, cols], start=start, stop=stop)
                mm.then_inc(part_used, 1)

            def keep_clock(n, free):
                for _ in range(n):
                    nc.tensor.matmul(bank[free][:, 0:P], ident[:], ident[:], start=True, stop=True)

            def turn8(src, done):
                for c in range(2):
                    for k in range(4):
                        mm = nc.tensor.transpose(bank[4 + c][:, k * T:(k + 1) * T],
                                                 src[:, (4 * c + k) * P:(4 * c + k + 1) * P], ident[0:T, 0:T])
                    mm.then_inc(done, 1)

            pe.wait_ge(consts, 2)
            keep_clock(18, 7)
            pe.wait_ge(xn_ready, 1)
            turn8(xn, xT_turned)

            def half(j, n, lhs, parts=range(PARTS)):
                for c in parts:
                    part(2 * j + n, c, lhs, [bank[2 * (j % 2) + n]], c == 0, c == PARTS - 1)

            def turn(j):
                pe.wait_ge(tok_ready[j], 2)
                if j >= 1:
                    pe.wait_ge(fm_ready[j - 1], 2)
                turn8(tok[:, j % 2, :], turned[j])

            def probs_turn(g):
                pe.wait_ge(probs_ready, g + 1)
                for c in (2 * g, 2 * g + 1):
                    for i in range(4):
                        mm = nc.tensor.transpose(bank[4 + c][0:T, i * T:(i + 1) * T], S3[:, 4 * c + i, :],
                                                 ident[0:T, 0:T])
                    mm.then_inc(probs_turned, 1)

            normed = (xT, xT_hi, xT_lo)
            inputs = [normed, normed, (fmv[0], fm_hiv[0], fm_lov[0]), (fmv[1], fm_hiv[1], fm_lov[1]), normed,
                      (fmv[1], fm_hiv[0], fm_lov[0]), (fmv[2], fm_hiv[1], fm_lov[1])]
            for j in range(6):
                if j >= 2:
                    pe.wait_ge(tok_ready[j - 2], 2)
                if j == 0:
                    pe.wait_ge(xT_ready, 2)
                if j in (2, 3):
                    pe.wait_ge(fm_ready[j - 2], 2)
                if j == 5:
                    keep_clock(11, 3)
                    pe.wait_ge(fm_ready[4], 1)
                half(j, 0, inputs[j], range(0, 2))
                if 1 <= j <= 4:
                    turn(j - 1)
                if j == 5:
                    pe.wait_ge(fm_ready[4], 2)
                half(j, 0, inputs[j], range(2, PARTS))
                if j == 0:
                    pe.wait_ge(xT_ready, 2 + 2)
                if j == 5:
                    pe.wait_ge(scores_read, 4)
                    probs_turn(0)
                half(j, 1, inputs[j], range(0, 2))
                if j == 5:
                    probs_turn(1)
                half(j, 1, inputs[j], range(2, PARTS))
                if j == 3:
                    pe.wait_ge(hot_made, 2)
                    pe.wait_ge(pool_hot, 2)
                    for t in range(ET):
                        nc.tensor.matmul(bank[6][0:T, 0:T], src_hot[:, t, :], dst_code[:, t, :],
                                         start=(t == 0), stop=(t == ET - 1))
                    for t in range(ET):
                        mm = nc.tensor.matmul(bank[7][0:T, 0:T], dst_hot[:, t, :], src_hot[:, t, :],
                                              start=(t == 0), stop=(t == ET - 1))
                    mm.then_inc(counts_done, 1)
                if j == 4:
                    pe.wait_ge(fm_ready[3], 2)
                    pe.wait_ge(counts_read, 1)
                    for c in range(2):
                        if c == 1:
                            turn(4)
                        for par in range(2):
                            for i in range(4):
                                k = 4 * c + i
                                mm = nc.tensor.matmul(bank[SCORE[c][par]][0:T, i * T:(i + 1) * T],
                                                      fmv[2][64 * par:64 * par + 64, k, :],
                                                      fmv[0][64 * par:64 * par + 64, k, :], start=True, stop=True)
                            mm.then_inc(scores_done, 1)
            for c in range(2):
                pe.wait_ge(tok_ready[5], c + 1)
                pe.wait_ge(probsT_ready, 4)
                for k in range(4 * c, 4 * c + 4):
                    for par in range(2):
                        h = 2 * k + par
                        mm = nc.tensor.matmul(bank[2 + c][64 * par:64 * par + 64, (k - 4 * c) * T:(k - 4 * c + 1) * T],
                                              tok[:, 1, h * HD:(h + 1) * HD], PT[:, par * 8 + k, :],
                                              start=True, stop=True)
                mm.then_inc(attended, 1)
            pe.wait_ge(attended_read, 1)
            half(6, 0, inputs[6], range(0, 2))
            pe.wait_ge(attended_read, 2)
            half(6, 0, inputs[6], range(2, PARTS))
            half(6, 1, inputs[6])

            keep_clock(14, 7)
            pe.wait_ge(xn_ready, 2)
            turn8(xn, xT_turned)

            def expand(n):
                if n >= 4:
                    pe.wait_ge(exp_tok, n - 3)
                for c in range(PARTS):
                    if n == 0 and c in (0, 2):
                        pe.wait_ge(xT_ready, 5 + c // 2)
                    part(GNN_SLABS + n, c, normed, [bank[n % 4]], c == 0, c == PARTS - 1)

            def exp_turn(n):
                pe.wait_ge(exp_tok, n + 1)
                if n >= 2:
                    pe.wait_ge(exp_fm, n - 1)
                for k in range(4):
                    mm = nc.tensor.transpose(bank[4 + n % 2][:, k * T:(k + 1) * T],
                                             tok[:, n % 2, k * P:(k + 1) * P], ident[0:T, 0:T])
                mm.then_inc(exp_turned, 1)

            def first_step(m, fm_in, mix, pair):
                for g in range(8):
                    mm = nc.tensor.matmul(bank[pair + g // 4][0:T, (g % 4) * P:(g % 4 + 1) * P],
                                          fm_in[:, 8 * m + g, :], mix[:, 8 * m + g, :], start=True, stop=True)
                return mm

            def up1(m):
                pe.wait_ge(exp_fm, 2 * m + 2)
                if m == 0:
                    pe.wait_ge(composed, 1)
                else:
                    pe.wait_ge(up1_read, 2 * m)
                first_step(m, B1, mix_low, 6).then_inc(up1_done, 1)

            for n in range(EXP_SLABS):
                expand(n)
                if n >= 1:
                    exp_turn(n - 1)
                if n >= 3 and n % 2:
                    up1((n - 3) // 2)
            exp_turn(7)
            up1(3)

            def turn4(c, src, b, done):
                for i in range(4 * c, 4 * c + 4):
                    mm = nc.tensor.transpose(b[:, (i - 4 * c) * T:(i - 4 * c + 1) * T], src[0:T, i * P:(i + 1) * P],
                                             ident[0:T, 0:T])
                mm.then_inc(done, 1)

            pe.wait_ge(up1_read, 8)
            pe.wait_ge(composed, 2)

            def step_pair(m):
                return (6, 2)[m % 2]

            def up2(m):
                pe.wait_ge(up2_fm, max(2 * m + 2, 6 * (m % 2)))
                if m >= 2:
                    pe.wait_ge(up2_read0, m - 1)
                    pe.wait_ge(up2_read1, m - 1)
                first_step(m, B0, mix_high, step_pair(m)).then_inc(up2_done, 1)

            for c in range(8):
                if c < 2:
                    pe.wait_ge(exp_fm, 8)
                if c >= 6:
                    pe.wait_ge(up2_fm, c - 5)
                turn4(c, U, bank[UPT[c]], up2_turned)
                if c == 5:
                    up2(0)
            for m in range(1, 4):
                up2(m)
            pe.wait_ge(up2_read0, 4)
            pe.wait_ge(up2_read1, 4)

            def dn1(m):
                pe.wait_ge(act_fm, 2 * m + 2)
                if m % 2:
                    pe.wait_ge(act_biased, 6)
                if m >= 2:
                    pe.wait_ge(dn1_read0, m - 1)
                    pe.wait_ge(dn1_read1, m - 1)
                first_step(m, B1, mix_low, step_pair(m)).then_inc(dn1_done, 1)

            pe.wait_ge(composed, 3)
            pe.wait_ge(upper_composed, 1)
            pe.wait_ge(up2_fm, 8)
            for c in range(8):
                if c >= 6:
                    pe.wait_ge(act_biased, c - 5)
                turn4(c, V, bank[UPT[c]], act_turned)
                if c == 5:
                    dn1(0)
            for m in range(1, 4):
                dn1(m)
            pe.wait_ge(dn1_read0, 4)
            pe.wait_ge(dn1_read1, 4)

            def dn2(c):
                if c == 0:
                    pe.wait_ge(composed, 4)
                pe.wait_ge(dn2_fm, c + 1)
                if c >= 2:
                    pe.wait_ge(dn2_read1, c - 1)
                for i in range(4):
                    mm = nc.tensor.matmul(bank[(6, 2)[c % 2]][:, i * T:(i + 1) * T],
                                          mix_high[:, 4 * c + i, :], B1[:, 4 * c + i, :], start=True, stop=True)
                mm.then_inc(dn2_done, 1)

            def contract(s):
                pe.wait_ge(dn2_read1, s + 1)
                for c in range(PARTS):
                    tile = 4 * s
                    part(GNN_SLABS + EXP_SLABS + s, c,
                         (None, z_hi[:, tile:tile + 4, :], z_lo[:, tile:tile + 4, :]),
                         [bank[0], bank[1]], s == 0 and c == 0, s == 7 and c == 3)

            for c in range(8):
                if c < 2:
                    pe.wait_ge(act_biased, 8)
                else:
                    pe.wait_ge(dn2_fm, c - 1)
                turn4(c, U, bank[4 + c % 2], dn2_turned)
                if c >= 1:
                    dn2(c - 1)
                if c >= 3:
                    contract(c - 3)
            dn2(7)
            for s in range(5, 8):
                contract(s)

            keep_clock(22, 7)
            pe.wait_ge(xn_ready, 3)
            turn8(xn, xT_turned)
            small, big = ring[:, 0, :], ring[:, 1, :]
            pe.wait_ge(down_in, 48)
            pe.wait_ge(xT_ready, 8)
            for k in range(KD):
                mm = nc.tensor.matmul(bank[6][0:T, 0:G1], xT[:, k, :], small[:, k * G1:(k + 1) * G1],
                                      start=(k == 0), stop=(k == KD - 1))
            mm.then_inc(wd_done, 1)
            pe.wait_ge(wd_tok, 1)
            for k in range(2):
                mm = nc.tensor.transpose(bank[4][:, k * T:(k + 1) * T], tok[:, 0, k * P:(k + 1) * P], ident[0:T, 0:T])
            mm.then_inc(wd_turned, 1)
            pe.wait_ge(wd_fm, 1)
            for k in range(2):
                mm = nc.tensor.matmul(bank[7][0:T, :], sfm[2][:, k, :], small[:, 2048 + k * 512:2048 + (k + 1) * 512],
                                      start=(k == 0), stop=(k == 1))
            mm.then_inc(lr_done, 1)
            pe.wait_ge(hot_ready, 4)
            pe.wait_ge(lr_split, 1)

            def messages(c):
                w = min(BANK, EL - c * BANK)
                for f in range(2):
                    i = 2 * c + f
                    if i >= 4:
                        pe.wait_ge(msg_ready, i - 3)
                    for half, rows in enumerate((lr_hi, lr_lo)):
                        if half == 1 and i == 0:
                            pe.wait_ge(lr_split, 2)
                        for side, hot in enumerate((src_by_node, dst_by_node)):
                            mm = nc.tensor.matmul(bank[i % 4][:, 0:w], rows[:, side * G1 + f * P:side * G1 + (f + 1) * P],
                                                  hot[:, c * BANK:c * BANK + w], start=(half + side == 0),
                                                  stop=(half + side == 2))
                    mm.then_inc(z_done, 1)

            def logits(c):
                pe.wait_ge(msg_ready, 2 * c + 2)
                if c >= 2:
                    pe.wait_ge(rhs_ready, c - 1)
                if c == 1:
                    pe.wait_ge(lr_ready, 1)
                for t in range(4 * c, min(4 * c + 4, LT)):
                    w = P if t < ET else T
                    for f in range(2):
                        mm = nc.tensor.matmul(bank[(5, 7)[c % 2]][0:w, t * H1:(t + 1) * H1],
                                              msg[:, f, t * P:t * P + w],
                                              att[:, f, :], start=(f == 0), stop=(f == 1))
                mm.then_inc(e_done, 1)

            def spread(c):
                pe.wait_ge(rhs_ready, c + 1 if c < 3 else 5)
                for t in range(4 * c, min(4 * c + 4, LT)):
                    w, dst = (P, dst_hot[:, t, :]) if t < ET else (T, ident[0:T, 0:T])
                    mm = nc.tensor.matmul(bank[6][0:T, 0:H1 * T], dst,
                                          edge_rhs[0:w, t, :, :].rearrange("p h t -> p (h t)"),
                                          start=(t == 0), stop=(t == LT - 1))
                return mm

            messages(0)
            messages(1)
            logits(0)
            messages(2)
            logits(1)
            spread(0)
            messages(3)
            logits(2)
            spread(1)
            logits(3)
            spread(2)
            spread(3).then_inc(pair_done, 1)
            keep_clock(19, 7)
            pe.wait_ge(alpha_ready, 1)
            for h in range(H1):
                mm = nc.tensor.transpose(bank[4][0:T, h * T:(h + 1) * T], alpha[:, h, :], ident[0:T, 0:T])
            mm.then_inc(alpha_turned, 1)
            pe.wait_ge(alphaT_ready, 1)
            for h in range(H1):
                p0 = 64 * (h % 2)
                mm = nc.tensor.matmul(bank[5][p0:p0 + 64, (h // 2) * T:(h // 2 + 1) * T],
                                      tok[:, 1, h * 64:(h + 1) * 64], alpha[:, H1 + h, :], start=True, stop=True)
            mm.then_inc(agg_done, 1)
            pe.wait_ge(agg_ready, 1)
            pe.wait_ge(up_in, 48)
            for n in range(2):
                for k in range(2):
                    mm = nc.tensor.matmul(bank[n][0:T, :], sfm[2][:, k, :], big[:, k * D + n * BANK:k * D + (n + 1) * BANK],
                                          start=(k == 0), stop=(k == 1))
                mm.then_inc(up_done, 1)

            keep_clock(16, 7)
            pe.wait_ge(xn_ready, 4)
            turn8(xn, xT_turned)
            pe.wait_ge(xT_ready, 10)
            for n in range(2):
                for c in range(PARTS):
                    part(STREAM + n, c, normed, [bank[2 + n]], c == 0, False)
                pe.wait_ge(xT_ready, 11)
                nc.tensor.matmul(bank[2 + n][0:T, :], pooled[:], big[:, 2048 + n * BANK:2048 + (n + 1) * BANK],
                                 start=False, stop=True).then_inc(fin_done, 1)

        @block.vector
        def _(dve):
            steps, norms = [0], [0]

            def step(ins):
                steps[0] += 1
                ins.then_inc(dve_step, 1)
                dve.wait_ge(dve_step, steps[0])

            def layer_norm():
                for n in range(2):
                    st = nc.vector.bn_stats(stats[:, n, :], x[:, n * BANK:(n + 1) * BANK])
                step(st)
                normalize()

            def normalize():
                step(nc.vector.bn_aggr(mv[:], stats[:]))
                nc.vector.tensor_scalar(mv[:, 1:2], mv[:, 1:2], LN_EPS, None, ALU.add).then_inc(var_ready, 1)
                norms[0] += 1
                dve.wait_ge(var_ready, norms[0])
                dve.wait_ge(rstd_ready, norms[0])
                nc.vector.tensor_scalar(xn[:], x[:], mv[:, 0:1], rstd[:], ALU.subtract, ALU.mult
                                        ).then_inc(xn_ready, 1)

            subs = [0]

            def sub_until(slab, part):
                while subs[0] < split_no(slab, part):
                    n = subs[0]
                    i, c = part_of_split(n)
                    dve.wait_ge(hi_ready, n + 1)
                    nc.vector.tensor_tensor(part_lo[:, n % NSPLIT, :], ring[:, slot_of(i), c * PART:(c + 1) * PART],
                                            part_hi[:, n % NSPLIT, :].bitcast(F32), ALU.subtract).then_inc(lo_ready, 1)
                    subs[0] += 1

            def split_to(hi, lo, src, done):
                step(nc.vector.tensor_copy(hi, src))
                nc.vector.tensor_tensor(lo, src, hi.bitcast(F32), ALU.subtract).then_inc(done, 1)

            def take_xT(t0, split, scale=None):
                for c in range(2):
                    dve.wait_ge(xT_turned, t0 + c + 1)
                    src = bank[4 + c][:, 0:4 * T].rearrange("p (k t) -> p k t", t=T)
                    ks = slice(4 * c, 4 * c + 4)
                    if split:
                        split_to(xT_hi[:, ks, :], xT_lo[:, ks, :], src, xT_ready)
                    elif scale is None:
                        nc.vector.tensor_copy(xT[:, ks, :], src).then_inc(xT_ready, 1)
                    else:
                        nc.vector.tensor_tensor(xT[:, ks, :], src, scale[:, ks, None].broadcast_to([P, 4, T]),
                                                ALU.mult).then_inc(xT_ready, 1)

            def take_turn(j, dst, split=None):
                for c in range(2):
                    dve.wait_ge(turned[j], c + 1)
                    src = bank[4 + c][:, 0:4 * T].rearrange("p (k t) -> p k t", t=T)
                    ks = slice(4 * c, 4 * c + 4)
                    b = bias_fm[:, BIAS[j], ks, None].broadcast_to([P, 4, T])
                    ins = nc.vector.tensor_tensor(dst[:, ks, :], src, b, ALU.add)
                    if split is None:
                        ins.then_inc(fm_ready[j], 1)
                    else:
                        step(ins)
                        split_to(fm_hiv[split][:, ks, :], fm_lov[split][:, ks, :], dst[:, ks, :], fm_ready[j])

            BIAS = [0, 1, 2, 3, 4, 5]
            dve.wait_ge(x_in, 16)
            layer_norm()
            take_xT(0, False)
            dve.wait_ge(xT_ready, 2)
            for c in range(2):
                ks = slice(4 * c, 4 * c + 4)
                split_to(xT_hi[:, ks, :], xT_lo[:, ks, :], xT[:, ks, :], xT_ready)
            sub_until(4, 0)
            dve.wait_ge(small_in, 32)
            take_turn(0, fmv[0], 0)
            dve.wait_ge(edge_in, 16)
            dve.wait_ge(ends_in, 16)
            dve.wait_ge(consts, 5)
            step(nc.vector.scalar_tensor_tensor(out=keys, in0=keys.bitcast(I32), scalar=float(T),
                                                in1=dst_bc.bitcast(I32), op0=ALU.mult, op1=ALU.add))
            step(nc.vector.scalar_tensor_tensor(out=key_col[:], in0=src_col, scalar=float(T), in1=dst_col,
                                                op0=ALU.mult, op1=ALU.add))
            nodes = node_row[:, None, :].broadcast_to([P, ET, T])
            nc.vector.tensor_tensor(dst_hot[:], dst_col[:, :, None].broadcast_to([P, ET, T]), nodes,
                                    ALU.is_equal).then_inc(hot_made, 1)
            parts_after = {0: (5, 0), 3: (6, 0), 6: (7, 0), 12: (8, 0)}
            for t in range(ET):
                w = EP - t * P
                step(nc.vector.scalar_tensor_tensor(out=junk[:, 0:w], in0=keys[:, t * P:EP], scalar=key_col[:, t:t + 1],
                                                    in1=after[:, 0:w], op0=ALU.is_equal, op1=ALU.mult,
                                                    accum_out=later[:, t:t + 1]))
                if t == 3:
                    take_turn(1, fmv[1], 1)
                if t in parts_after:
                    sub_until(*parts_after[t])
            take_turn(2, fmv[2])
            nc.vector.tensor_tensor(src_hot[:], src_col[:, :, None].broadcast_to([P, ET, T]), nodes,
                                    ALU.is_equal).then_inc(hot_made, 1)
            step(nc.vector.tensor_scalar(live[:], later[:], 0.0, None, ALU.is_equal))
            step(nc.vector.tensor_scalar(code[:], type_col, 0.0, 4.0, ALU.is_equal, ALU.mult))
            step(nc.vector.tensor_tensor(code[:], code[:], type_col, ALU.add))
            step(nc.vector.tensor_tensor(stands[:], src_col, dst_col, ALU.not_equal))
            step(nc.vector.tensor_tensor(stands[:], stands[:], live[:], ALU.mult))
            nc.vector.tensor_tensor(live_code[:], live[:], code[:], ALU.mult).then_inc(live_ready, 1)
            sub_until(9, 0)

            dve.wait_ge(counts_done, 1)
            dve.wait_ge(soft_ready, 1)
            step(nc.vector.scalar_tensor_tensor(out=sp_t[:, 3, :], in0=etw[:], scalar=0.0, in1=sp_t[:, 2, :],
                                                op0=ALU.max, op1=ALU.add))
            step(nc.vector.tensor_copy(mtmp[:, 0, :], bank[6][0:T, 0:T]))
            step(nc.vector.tensor_scalar(mtmp[:, 1, :], mtmp[:, 0, :], 0.0, 4.0, ALU.is_equal, ALU.mult))
            step(nc.vector.tensor_tensor(mtmp[:, 1, :], mtmp[:, 1, :], ident[0:T, 0:T], ALU.mult))
            step(nc.vector.tensor_tensor(mtmp[:, 0, :], mtmp[:, 0, :], mtmp[:, 1, :], ALU.add))
            step(nc.vector.tensor_scalar(mask[:], mtmp[:, 0, :], 0.0, -BIG, ALU.is_equal, ALU.mult))
            for c in range(4):
                step(nc.vector.tensor_scalar(mtmp[:, 1, :], mtmp[:, 0, :], float(c + 1), sp_t[:, 3, c:c + 1],
                                             ALU.is_equal, ALU.mult))
                step(nc.vector.tensor_tensor(mask[:], mask[:], mtmp[:, 1, :], ALU.add))
            step(nc.vector.tensor_tensor(count[:], ident[0:T, 0:T], bank[7][0:T, 0:T], ALU.add))
            nc.vector.tensor_scalar(absent[:], count[:], 0.0, -BIG, ALU.is_equal, ALU.mult).then_inc(counts_read, 1)
            sub_until(9, 1)
            dve.wait_ge(part_used, PARTS * 6)
            take_turn(3, fmv[0])
            sub_until(10, 2)
            sub_until(10, 2)

            def take_scores(c):
                for par in range(2):
                    dve.wait_ge(scores_done, 2 * c + par + 1)
                    at = (par * 8 + c * 4) * T
                    nc.vector.scalar_tensor_tensor(out=S[:, at:at + 4 * T].rearrange("p (h t) -> p h t", t=T),
                                                   in0=bank[SCORE[c][par]][0:T, 0:4 * T].rearrange("p (h t) -> p h t", t=T),
                                                   scalar=float(HD) ** -0.5,
                                                   in1=mask[:, None, :].broadcast_to([T, 4, T]),
                                                   op0=ALU.mult, op1=ALU.add).then_inc(scores_read, 1)

            take_scores(0)
            dve.wait_ge(part_used, PARTS * 8)
            take_turn(4, fmv[1], 0)
            take_scores(1)
            dve.wait_ge(scores_read, 4)
            for g in range(2):
                sl = S3[:, 8 * g:8 * g + 8, :]
                step(nc.vector.tensor_reduce(mx[:, 8 * g:8 * g + 8], sl, AX.X, ALU.max))
                nc.vector.tensor_tensor(sl, sl, mx[:, 8 * g:8 * g + 8, None].broadcast_to([T, 8, T]),
                                        ALU.subtract).then_inc(shifted, 1)
                sub_until(10, 3)
            for g in range(2):
                sl = S3[:, 8 * g:8 * g + 8, :]
                dve.wait_ge(exped, g + 1)
                step(nc.vector.tensor_reduce(den[:, 8 * g:8 * g + 8], sl, AX.X, ALU.add))
                step(nc.vector.reciprocal(den[:, 8 * g:8 * g + 8], den[:, 8 * g:8 * g + 8]))
                nc.vector.tensor_tensor(sl, sl, den[:, 8 * g:8 * g + 8, None].broadcast_to([T, 8, T]),
                                        ALU.mult).then_inc(probs_ready, 1)
                sub_until(11, 2 + g)
            for c in (0, 2):
                if c == 2:
                    sub_until(12, 2)
                dve.wait_ge(probs_turned, c + 1)
                nc.vector.tensor_copy(PT[:, 4 * c:4 * c + 4, :],
                                      bank[4 + c][0:T, 0:4 * T].rearrange("p (h t) -> p h t", t=T)).then_inc(probsT_ready, 1)
            for c in range(2):
                dve.wait_ge(attended, c + 1)
                ks = slice(4 * c, 4 * c + 4)
                step(nc.vector.tensor_tensor(fmv[2][:, ks, :], bank[2 + c][:, 0:4 * T].rearrange("p (k t) -> p k t", t=T),
                                             bias_fm[:, 5, ks, None].broadcast_to([P, 4, T]), ALU.add))
                split_to(fm_hiv[1][:, ks, :], fm_lov[1][:, ks, :], fmv[2][:, ks, :], attended_read)

            sub_until(14, 0)
            dve.wait_ge(biased, 1)
            for n in range(2):
                cols = slice(n * BANK, (n + 1) * BANK)
                dve.wait_ge(part_used, PARTS * (13 + n))
                step(nc.vector.tensor_tensor(x[:, cols], x[:, cols], bank[n][0:T, :], ALU.add))
                st = nc.vector.bn_stats(stats[:, n, :], x[:, cols])
                if n == 0:
                    sub_until(14, 2)
            step(st)
            normalize()
            take_xT(2, True)
            sub_until(15, 0)
            dve.wait_ge(bcs_ready, 1)
            step(nc.vector.tensor_tensor(x[:], x[:], bcs[:], ALU.add))
            for n in range(EXP_SLABS):
                sub_until(GNN_SLABS + min(n + 2, EXP_SLABS), 2)
                dve.wait_ge(exp_turned, n + 1)
                nc.vector.tensor_tensor(B1[:, 4 * n:4 * n + 4, :],
                                        bank[4 + n % 2][:, 0:4 * T].rearrange("p (k t) -> p k t", t=T),
                                        bexp[:, 4 * n:4 * n + 4, None].broadcast_to([P, 4, T]), ALU.add).then_inc(exp_fm, 1)


            def evac_up2(m):
                dve.wait_ge(up2_done, m + 1)
                take_step(by_place, m, (6, 2)[m % 2], 1, nc.vector.tensor_copy).then_inc(up2_read1, 1)

            dve.wait_ge(running, 1)
            dve.wait_ge(up1_done, 4)
            n = GRP // 2
            at = NT * (2 * n - 2)
            nc.vector.tensor_tensor(
                mix_low[64:128, :, 64:128].rearrange("p g (b n) -> p g b n", b=2),
                cur_even[64:128, :].rearrange("p (g n) -> p g n", g=NT)[:, :, None, :].broadcast_to([64, NT, 2, n]),
                stage[64:128, at:at + NT * 2 * n].rearrange("p (g b n) -> p g b n", g=NT, b=2), ALU.mult
            ).then_inc(upper_composed, 1)
            for c in range(8):
                dve.wait_ge(up2_turned, c + 1)
                nc.vector.tensor_copy(B0[:, 4 * c:4 * c + 4, :],
                                      bank[UPT[c]][:, 0:4 * T].rearrange("p (k t) -> p k t", t=T)).then_inc(up2_fm, 1)
                if c == 6:
                    dve.wait_ge(composed, 3)
                    dve.wait_ge(upper_composed, 1)
                if c >= 6:
                    evac_up2(c - 6)
            evac_up2(2)
            evac_up2(3)

            def evac_dn1(m):
                dve.wait_ge(dn1_done, m + 1)
                take_step(by_group, m, (6, 2)[m % 2], 1, nc.vector.tensor_copy).then_inc(dn1_read1, 1)

            for c in range(8):
                dve.wait_ge(act_turned, c + 1)
                nc.vector.tensor_tensor(B1[:, 4 * c:4 * c + 4, :],
                                        bank[UPT[c]][:, 0:4 * T].rearrange("p (k t) -> p k t", t=T),
                                        upb[:, 4 * c:4 * c + 4, None].broadcast_to([P, 4, T]), ALU.add).then_inc(act_biased, 1)
                if c >= 6:
                    evac_dn1(c - 6)
            evac_dn1(2)
            evac_dn1(3)
            CON = GNN_SLABS + EXP_SLABS

            def split_dn2(c):
                dve.wait_ge(dn2_read0, c + 1)
                nc.vector.tensor_tensor(z_lo[:, 4 * c:4 * c + 4, :],
                                        bank[(6, 2)[c % 2]][:, 0:4 * T].rearrange("p (r t) -> p r t", t=T),
                                        z_hi[:, 4 * c:4 * c + 4, :].bitcast(F32), ALU.subtract).then_inc(dn2_read1, 1)

            sub_until(CON, 2)
            for c in range(8):
                dve.wait_ge(dn2_turned, c + 1)
                if c == 0:
                    dve.wait_ge(dn1_done, 4)
                nc.vector.tensor_copy(B1[:, 4 * c:4 * c + 4, :],
                                      bank[4 + c % 2][:, 0:4 * T].rearrange("p (k t) -> p k t", t=T)).then_inc(dn2_fm, 1)
                if c >= 1:
                    split_dn2(c - 1)
                if c == 2:
                    sub_until(CON, 3)
                if c >= 3:
                    sub_until(CON + c - 2, 2)
            split_dn2(7)
            sub_until(CON + 7, 0)
            sub_until(STREAM, 0)
            dve.wait_ge(idx_in, 16)
            dve.wait_ge(dn2_done, 8)
            for i, view in enumerate((src_by_node, dst_by_node)):
                nc.vector.tensor_scalar(view[:, 0:EP], by_node[0:T, i, 0:EP].bitcast(I32), node_col[0:T, 0:1], None,
                                        ALU.is_equal).then_inc(hot_ready, 1)
                nc.vector.tensor_copy(view[:, EP:EL], ident[0:T, 0:T]).then_inc(hot_ready, 1)
            dve.wait_ge(part_used, PARTS * STREAM)
            for n in range(2):
                cols = slice(n * BANK, (n + 1) * BANK)
                nc.vector.tensor_tensor(x[:, cols], x[:, cols], bank[n][0:T, :], ALU.add).then_inc(x2_ready, 1)
            dve.wait_ge(x2_ready, 2)
            layer_norm()
            dve.wait_ge(xn_ready, 3)
            take_xT(4, False, rmsw)
            nc.vector.scalar_tensor_tensor(out=tok[:, 1, :], in0=xn[:], scalar=1.0 / D, in1=xn[:],
                                           op0=ALU.mult, op1=ALU.mult, accum_out=ms[:]).then_inc(ms_ready, 1)
            dve.wait_ge(ms_ready, 1)
            nc.vector.tensor_scalar(ms[:], ms[:], RMS_EPS, None, ALU.add).then_inc(ms_ready, 1)
            dve.wait_ge(rms_ready, 1)
            dve.wait_ge(wd_done, 1)
            nc.vector.tensor_scalar(tok[:, 0, 0:G1], bank[6][0:T, 0:G1], rms[:], None, ALU.mult).then_inc(wd_tok, 1)
            dve.wait_ge(wd_turned, 1)
            nc.vector.tensor_copy(sfm[2][:, 0:2, :], bank[4][:, 0:2 * T].rearrange("p (k t) -> p k t", t=T)
                                  ).then_inc(wd_fm, 1)
            dve.wait_ge(lr_split, 1)
            nc.vector.tensor_tensor(lr_lo[:], bank[7][0:T, :], lr_hi[:].bitcast(F32), ALU.subtract).then_inc(lr_split, 1)

            def leaky(c):
                w = min(BANK, EL - c * BANK)
                for f in range(2):
                    i = 2 * c + f
                    dve.wait_ge(z_scaled, i + 1)
                    nc.vector.tensor_tensor(msg[:, f, c * BANK:c * BANK + w], small_fm[:, i % 2, 0:w], bank[i % 4][:, 0:w],
                                            ALU.max).then_inc(msg_ready, 1)

            def weigh(c):
                dve.wait_ge(e_done, c + 1)
                for t0, n, w, hot in (((4 * c, 4, P, src_live[:, 4 * c:4 * c + 4, :]),) if c < 3 else
                                      ((ET - 1, 1, P, src_live[:, ET - 1:ET, :]), (ET, 1, T, ident[0:T, None, 0:T]))):
                    step(nc.vector.tensor_copy(e_sb[0:w, t0:t0 + n, :].rearrange("p t h -> p (t h)"),
                                               bank[(5, 7)[c % 2]][0:w, t0 * H1:(t0 + n) * H1]))
                    nc.vector.tensor_tensor(edge_rhs[0:w, t0:t0 + n, :, :],
                                            hot[:, :, None, :].broadcast_to([w, n, H1, T]),
                                            e_sb[0:w, t0:t0 + n, :, None].broadcast_to([w, n, H1, T]),
                                            ALU.mult).then_inc(rhs_ready, 1)

            leaky(0)
            leaky(1)
            weigh(0)
            leaky(2)
            weigh(1)
            leaky(3)
            weigh(2)
            weigh(3)
            sub_until(STREAM, 3)
            dve.wait_ge(pair_done, 1)
            pr = alpha[:, 0:H1, :]
            step(nc.vector.tensor_tensor(pr, bank[6][0:T, 0:H1 * T].rearrange("p (h t) -> p h t", t=T),
                                         absent[:, None, :].broadcast_to([T, H1, T]), ALU.add))
            step(nc.vector.tensor_reduce(mx[:, 0:H1], pr, AX.X, ALU.max))
            nc.vector.tensor_tensor(pr, pr, mx[:, 0:H1, None].broadcast_to([T, H1, T]), ALU.subtract).then_inc(pair_shift, 1)
            dve.wait_ge(pair_exp, 1)
            step(nc.vector.tensor_tensor(pr, pr, count[:, None, :].broadcast_to([T, H1, T]), ALU.mult))
            step(nc.vector.tensor_reduce(den[:, 0:H1], pr, AX.X, ALU.add))
            step(nc.vector.tensor_scalar(den[:, 0:H1], den[:, 0:H1], 1e-16, None, ALU.add))
            step(nc.vector.reciprocal(den[:, 0:H1], den[:, 0:H1]))
            nc.vector.tensor_tensor(pr, pr, den[:, 0:H1, None].broadcast_to([T, H1, T]), ALU.mult).then_inc(alpha_ready, 1)
            dve.wait_ge(alpha_turned, 1)
            nc.vector.tensor_copy(alpha[:, H1:2 * H1, :], bank[4][0:T, 0:H1 * T].rearrange("p (h t) -> p h t", t=T)
                                  ).then_inc(alphaT_ready, 1)
            dve.wait_ge(agg_done, 1)
            nc.vector.tensor_copy(sfm[2][:, 0:2, :], bank[5][:, 0:2 * T].rearrange("p (k t) -> p k t", t=T)
                                  ).then_inc(agg_ready, 1)
            for n in range(2):
                cols = slice(n * BANK, (n + 1) * BANK)
                dve.wait_ge(up_done, n + 1)
                nc.vector.tensor_tensor(x[:, cols], x[:, cols], bank[n][0:T, :], ALU.add).then_inc(x2_ready, 1)
            dve.wait_ge(x2_ready, 4)
            layer_norm()
            take_xT(6, True)
            for c in range(2):
                step(nc.vector.tensor_copy(xT[:, 4 * c:4 * c + 4, :],
                                           bank[4 + c][:, 0:4 * T].rearrange("p (k t) -> p k t", t=T)))
            nc.vector.tensor_reduce(pooled[:], xT[:, :, :].rearrange("p k t -> p t k"), AX.X, ALU.add).then_inc(xT_ready, 1)
            sub_until(STREAM + 2, 0)
            for n in range(2):
                cols = slice(n * BANK, (n + 1) * BANK)
                dve.wait_ge(fin_done, n + 1)
                nc.vector.tensor_tensor(xn[:, cols], x[:, cols], bank[2 + n][0:T, :], ALU.add).then_inc(fin_ready, 1)


def lay_out(i):
    import numpy as np

    a = {k: np.asarray(v) for k, v in i.items()}

    def tiles(w):
        return w.reshape(-1, P, w.shape[1]).transpose(1, 0, 2).reshape(P, -1)

    def halves(w):
        return [tiles(w[:, n * BANK:(n + 1) * BANK]) for n in range(w.shape[1] // BANK)]

    slabs = []
    for n in GNN:
        slabs += halves(a["L0_gnn_w" + n].T)
    slabs += halves(a["L0_ffn_W_exp"])
    con = a["L0_ffn_W_con"].reshape(GRP, NT, 2, D).transpose(2, 0, 1, 3).reshape(P, NT, D)
    slabs += [con[:, 4 * s:4 * s + 4].reshape(P, SLAB) for s in range(CON_SLABS)]
    slabs += halves(a["L1_ffn_weight"].T)

    def coefs(w):
        low, high = [], []
        for s in range(STAGES):
            v = w[s].reshape(NT, 2, 2 ** (5 - s), 2 ** s, 2, 2)
            low.append(v.transpose(1, 2, 5, 0, 4, 3).reshape(-1))
            v = w[s + 6].reshape(2 ** (5 - s), 2 ** s, NT, 2, 2, 2)
            high.append(v.transpose(3, 0, 5, 2, 4, 1).reshape(-1))
        return [np.stack(low), np.stack(high)]

    def by_feature(v, k):
        return v.reshape(k, P).T

    def edge_list(v):
        return np.concatenate([v, np.full(EP - E, -1, v.dtype)])

    att = np.zeros((P, 2, H1), np.float32)
    for h in range(H1):
        att[64 * (h % 2):64 * (h % 2) + 64, h // 2, h] = a["L1_gnn_att"].reshape(H1, 64)[h]
    r = {
        "x": a["x"],
        "stream": np.stack(slabs),
        "coef": np.stack(coefs(a["L0_ffn_up_weights"]) + coefs(a["L0_ffn_down_weights"])),
        "rows": np.stack([a["L0_gnn_bo"], a["L0_ffn_b_con"].reshape(D), a["L0_ffn_down_bias"].reshape(D)]),
        "by_feature": np.concatenate(
            [by_feature(a["L0_gnn_b" + n], KD) for n in ("q", "k", "iq", "ik", "v", "iv")]
            + [by_feature(a["L0_ffn_b_exp"], NT), by_feature(a["L0_ffn_up_bias"], NT),
               by_feature(a["L1_gnn_rms_w"], KD), att.reshape(P, 2 * H1)], axis=1),
        "etw": a["L0_gnn_edge_type_weights"].reshape(1, 4),
        "w_down": tiles(a["L1_gnn_W_down"]),
        "w_l": a["L1_gnn_Wl"].reshape(2, P, G1).transpose(1, 0, 2),
        "w_r": a["L1_gnn_Wr"].reshape(2, P, G1).transpose(1, 0, 2),
        "w_up": tiles(a["L1_gnn_W_up"]),
        "disha": a["L1_ffn_disha"],
        "ends": np.stack([edge_list(a["src"]), edge_list(a["dst"])]),
        "edge_cols": np.stack([edge_list(a[k]).reshape(ET, P).T for k in ("src", "dst", "edge_type_5")], axis=1),
    }
    return {k: np.ascontiguousarray(v) for k, v in r.items()}


def kernel(**inputs):
    import concourse.bacc as bacc
    from concourse.bass_utils import run_bass_kernel_spmd

    nc = bacc.Bacc("TRN2", target_bir_lowering=False, num_devices=1)
    arrays = lay_out(inputs)
    A = {k: nc.dram_tensor(f"in_{k}", v.shape, mybir.dt.from_np(v.dtype), kind="ExternalInput").ap()
         for k, v in arrays.items()}
    out = nc.dram_tensor("out", (T, D), F32, kind="ExternalOutput").ap()
    program(nc, A, out)
    r = run_bass_kernel_spmd(nc, [{f"in_{k}": v for k, v in arrays.items()}], core_ids=[0])
    return r.results[0]["out"]
```

```python
from contextlib import ExitStack

import concourse.bass as bass
from concourse import mybir

F32 = mybir.dt.float32
F32R = mybir.dt.float32r
I32 = mybir.dt.int32
BF16 = mybir.dt.bfloat16
ALU = mybir.AluOpType
ACT = mybir.ActivationFunctionType
AX = mybir.AxisListType

P = 128
BANK = 512
T = 96
D = 1024
KD = D // P
HID = 4096
HEADS, HD = 16, 64
E = 1632
ET = (E + P - 1) // P
EP = ET * P
EL = EP + T
LT = ET + 1
G1 = 256
H1 = 4
SLOTS = 3
SLAB = 4096
STAGES = 6
GRP = 64
NT = HID // P
BIG = 1.0e30
LN_EPS, RMS_EPS = 1e-5, 1e-6
GNN = ["q", "k", "iq", "ik", "v", "iv", "o"]
GNN_SLABS = 2 * len(GNN)
EXP_SLABS = 8
CON_SLABS = 8
STAGED = 24
FEATS = 7 * KD + 2 * NT + 2 * H1
PARTS = 4
PART = SLAB // PARTS
NSPLIT = 3
STREAM = GNN_SLABS + EXP_SLABS + CON_SLABS


def slot_of(slab):
    return slab % SLOTS if slab < STREAM else (2, 0)[slab - STREAM]


def split_parts(slab):
    if slab < GNN_SLABS:
        return (0, 0, 2, 1, 0, 0, 1, 1, 3, 3, 2, 1, 3, 3)[slab]
    return 3 if slab == STREAM else PARTS


def split_no(slab, part):
    return sum(split_parts(i) for i in range(slab)) + min(part, split_parts(slab) if slab < STREAM + 2 else 0)


def part_of_split(n):
    slab = 0
    while n >= split_parts(slab):
        n -= split_parts(slab)
        slab += 1
    return slab, n


def program(nc, A, out):
    with ExitStack() as ctx:
        def sb(name, shape, dt=F32):
            return ctx.enter_context(nc.sbuf_tensor(name, shape, dt))

        def sem(name):
            return ctx.enter_context(nc.semaphore(name))

        ring = sb("ring", [P, SLOTS, SLAB])
        part_hi = sb("part_hi", [P, NSPLIT, PART], F32R)
        part_lo = sb("part_lo", [P, NSPLIT, PART], F32R)
        x = sb("x", [T, D])
        bcs = sb("bcs", [T, D])
        xT = sb("xT", [P, KD, T])
        xT_hi = sb("xT_hi", [P, KD, T], F32R)
        xT_lo = sb("xT_lo", [P, KD, T], F32R)
        tok = sb("tok", [T, 2, D])
        xc = tok[:, 0, :]
        dst_hot = sb("dst_hot", [P, ET, T], F32R)
        loop_hot = sb("loop_hot", [T, T], F32R)
        src_live = sb("src_live", [P, ET, T])
        edge_cols = sb("edge_cols", [P, 3, ET], I32)
        src_col, dst_col, type_col = (edge_cols[:, i, :] for i in range(3))
        key_col = sb("key_col", [P, ET])
        code = sb("code", [P, ET])
        later = sb("later", [P, ET])
        live = sb("live", [P, ET])
        stands = sb("stands", [P, ET])
        live_code = sb("live_code", [P, ET])
        node_row = sb("node_row", [P, T])
        node_col = sb("node_col", [P, 1])
        ident = sb("ident", [P, P])
        by_feature = sb("by_feature", [P, FEATS])
        bias_fm = by_feature[:, 0:6 * KD].rearrange("p (i k) -> p i k", i=6)
        bexp = by_feature[:, 6 * KD:6 * KD + NT]
        upb = by_feature[:, 6 * KD + NT:6 * KD + 2 * NT]
        rmsw = by_feature[:, 6 * KD + 2 * NT:7 * KD + 2 * NT]
        att = by_feature[:, 7 * KD + 2 * NT:FEATS].rearrange("p (f h) -> p f h", f=2)
        etw = sb("etw", [T, 4])
        sp_t = sb("sp_t", [T, 4, 4])
        mask = sb("mask", [T, T])
        mtmp = sb("mtmp", [T, 3, T])
        count = sb("count", [T, T])
        absent = sb("absent", [T, T])
        stats = sb("stats", [T, 2, 6])
        mv = sb("mv", [T, 2])
        rstd = sb("rstd", [T, 1])
        minus_half = sb("minus_half", [T, 1])
        ms = sb("ms", [T, 1])
        rms = sb("rms", [T, 1])
        mx = sb("mx", [T, HEADS])
        den = sb("den", [T, HEADS])
        e_hi = sb("e_hi", [P, LT, H1], F32R)
        e_lo = sb("e_lo", [P, LT, H1])
        pooled = sb("pooled", [P, T])

        def phase(*tensors):
            with ExitStack() as space:
                return [space.enter_context(nc.sbuf_tensor(name, shape, dt)) for name, shape, dt in tensors]

        MIX = (("low{}", [P, NT, P], F32), ("high{}", [P, NT, P], F32))

        def mixes(n):
            return [(name.format(n), shape, dt) for name, shape, dt in MIX]

        mix_low, mix_high, stage, ends, after, fm, fm_hi, fm_lo = phase(
            *mixes(1),
            ("stage", [P, HID], F32),
            ("ends", [P, 2, EP], F32),
            ("after", [P, EP], BF16),
            ("fm", [P, 3, KD * T], F32),
            ("fm_hi", [P, 2, KD * T], F32R),
            ("fm_lo", [P, 2, KD * T], F32R))
        keys, dst_bc = ends[:, 0, :], ends[:, 1, :]
        junk = dst_bc.bitcast(BF16)[:, 0:EP]
        _, _, _, src_hot, dst_code, S3 = phase(
            *mixes("_1b"),
            ("stage_1b", [P, HID], F32),
            ("src_hot", [P, ET, T], F32),
            ("dst_code", [P, ET, T], F32),
            ("scores", [T, HEADS, T], F32))
        _, _, _, PT = phase(
            *mixes("_1c"),
            ("stage_1c", [P, HID], F32),
            ("probs_by_source", [T, HEADS, T], F32))
        _, _, V, B0, B1, U, cur_even, cur_odd = phase(
            *mixes("_2"),
            ("V", [P, HID], F32),
            ("B0", [P, NT, T], F32),
            ("B1", [P, NT, T], F32),
            ("U", [P, HID], F32),
            ("cur_even", [P, NT * 32], F32),
            ("cur_odd", [P, NT * 16], F32))
        by_node, _, z_lo, z_hi = phase(
            ("by_node", [P, 2, NT * GRP], F32),
            ("high_2b", [P, NT, P], F32),
            ("z_lo", [P, HID], F32R),
            ("z_hi", [P, NT, T], F32R))
        z_lo = z_lo[:, 0:NT * T].rearrange("p (n t) -> p n t", t=T)
        _, hot_by_node, edge_rhs, edge_rhs_lo, lr_hi, lr_lo, alpha, small_fm, msg = phase(
            ("by_node_3", [P, 2, NT * GRP], F32),
            ("hot_by_node", [P, 2, NT * GRP], F32R),
            ("edge_rhs", [P, LT, H1, T], F32R),
            ("edge_rhs_lo", [P, 2, 4 * H1, T], F32R),
            ("lr_hi", [T, 2 * G1], F32R),
            ("lr_lo", [T, 2 * G1], F32R),
            ("alpha", [T, 2 * H1, T], F32),
            ("small_fm", [P, 3, KD * T], F32),
            ("msg", [P, 2, EL], F32))

        bank = [ctx.enter_context(nc.psum_tensor(f"bank{i}", [P, BANK], F32)) for i in range(8)]

        rows = mix_high[0:T, :, :].rearrange("p a n -> p (a n)")[:, 0:3 * D].rearrange("p (a n) -> p a n", a=3)
        by_group = U[:, :].rearrange("p (c g x) -> p g x c", g=NT, x=2)
        by_place = V[:, :].rearrange("p (g r x) -> p r x g", r=NT, x=2)
        S = S3[:, :, :].rearrange("p h t -> p (h t)")
        fmv, fm_hiv, fm_lov = ([f[:, i, :].rearrange("p (k t) -> p k t", t=T) for i in range(n)]
                               for f, n in ((fm, 3), (fm_hi, 2), (fm_lo, 2)))
        sfm = [small_fm[:, i, :].rearrange("p (k t) -> p k t", t=T) for i in range(3)]
        src_by_node = hot_by_node[0:T, 0, 0:EL]
        dst_by_node = hot_by_node[0:T, 1, 0:EL]

        x_in = sem("x_in")
        rows_in = sem("rows_in")
        edge_in, ends_in = sem("edge_in"), sem("ends_in")
        small_in = sem("small_in")
        slab_in = [sem(f"slab_in{i}") for i in range(SLOTS)]
        down_in, up_in = sem("down_in"), sem("up_in")
        hi_ready, lo_ready = sem("hi_ready"), sem("lo_ready")
        part_used = sem("part_used")
        coef_in = [sem(f"coef_in{i}") for i in range(4)]
        consts = sem("consts")
        loops_ready = sem("loops_ready")
        hot_made, pool_hot = sem("hot_made"), sem("pool_hot")
        composed, zeroed = sem("composed"), sem("zeroed")
        running, upper_composed = sem("running"), sem("upper_composed")
        biased, bcs_ready = sem("biased"), sem("bcs_ready")
        centered = sem("centered")
        var_ready, rstd_ready = sem("var_ready"), sem("rstd_ready")
        ms_ready, rms_ready = sem("ms_ready"), sem("rms_ready")
        xT_turned, xT_ready = sem("xT_turned"), sem("xT_ready")
        tok_ready = [sem(f"tok_ready_{n}") for n in GNN]
        turned = [sem(f"turned_{n}") for n in GNN]
        fm_ready = [sem(f"fm_ready_{n}") for n in GNN]
        live_ready = sem("live_ready")
        counts_done, counts_read = sem("counts_done"), sem("counts_read")
        soft_ready = sem("soft_ready")
        scores_done, scores_read = sem("scores_done"), sem("scores_read")
        shifted, exped = sem("shifted"), sem("exped")
        probs_ready = sem("probs_ready")
        probs_turned, probsT_ready = sem("probs_turned"), sem("probsT_ready")
        attended, attended_read = sem("attended"), sem("attended_read")
        exp_tok = sem("exp_tok")
        exp_turned, exp_fm = sem("exp_turned"), sem("exp_fm")
        up1_done, up1_read = sem("up1_done"), sem("up1_read")
        up2_turned, up2_fm = sem("up2_turned"), sem("up2_fm")
        up2_done, up2_read0, up2_read1 = sem("up2_done"), sem("up2_read0"), sem("up2_read1")
        act_turned, act_biased, act_fm = sem("act_turned"), sem("act_biased"), sem("act_fm")
        dn1_done, dn1_read0, dn1_read1 = sem("dn1_done"), sem("dn1_read0"), sem("dn1_read1")
        dn2_turned, dn2_fm = sem("dn2_turned"), sem("dn2_fm")
        dn2_done, dn2_read0, dn2_read1 = sem("dn2_done"), sem("dn2_read0"), sem("dn2_read1")
        con_half = sem("con_half")
        idx_in, hot_ready = sem("idx_in"), sem("hot_ready")
        wd_done, wd_fm = sem("wd_done"), sem("wd_fm")
        lr_done, lr_ready = sem("lr_done"), sem("lr_ready")
        lr_split = sem("lr_split")
        z_done, z_scaled, msg_ready = sem("z_done"), sem("z_scaled"), sem("msg_ready")
        e_done, e_lo_ready = sem("e_done"), sem("e_lo_ready")
        rhs_ready, rhs_lo_ready = sem("rhs_ready"), sem("rhs_lo_ready")
        pair_done, pair_shift, pair_exp, alpha_ready = (
            sem("pair_done"), sem("pair_shift"), sem("pair_exp"), sem("alpha_ready"))
        alpha_turned, alphaT_ready = sem("alpha_turned"), sem("alphaT_ready")
        agg_done, agg_ready = sem("agg_done"), sem("agg_ready")
        up_done = sem("up_done")
        fin_done, fin_ready = sem("fin_done"), sem("fin_ready")
        out_done = sem("out_done")
        dve_step, act_step, pool_step = sem("dve_step"), sem("act_step"), sem("pool_step")

        block = ctx.enter_context(nc.Block())

        def take_step(to, m, pair, j, copy):
            first = 8 * m + 4 * j
            return copy(to[0:T, first:first + 4, :, :],
                        bank[pair + j][0:T, :].rearrange("p (n x c) -> p n x c", n=4, x=2))

        def groups(c):
            if c < 3:
                return ((4 * c, 4, P, src_live[:, 4 * c:4 * c + 4, :]),)
            return (ET - 1, 1, P, src_live[:, ET - 1:ET, :]), (ET, 1, T, ident[0:T, None, 0:T])

        def spread_low(engine, c, t0, n, w, hot):
            k = (t0 - 4 * c) * H1
            return engine.tensor_tensor(
                edge_rhs_lo[0:w, c % 2, k:k + n * H1, :].rearrange("p (n h) t -> p n h t", h=H1),
                hot[:, :, None, :].broadcast_to([w, n, H1, T]),
                e_lo[0:w, t0:t0 + n, :, None].broadcast_to([w, n, H1, T]), ALU.mult)

        SCORE = ((6, 7), (0, 1))
        STEP = (6, 2, 6, 2)
        UPT = (4, 5, 0, 1, 2, 3, 4, 5)

        @block.sync
        def _(sp):
            def load(i):
                sp.dma_start(ring[:, i % SLOTS, :], A["stream"][i]).then_inc(slab_in[i % SLOTS], 16)

            def load_round(r):
                for s in range(SLOTS):
                    yield s
                    sp.dma_start(ring[:, s, :],
                                 A["stream"][bass.ds(r * SLOTS + s, 1)].rearrange("o p n -> (o p) n")
                                 ).then_inc(slab_in[s], 16)

            sp.dma_start(x[:], A["x"]).then_inc(x_in, 16)
            for i in range(SLOTS):
                load(i)
            rounds = GNN_SLABS // SLOTS
            with sp.Fori(1, rounds + 1) as r:
                for s in load_round(r):
                    sp.wait_ge(part_used, (r * SLOTS + s - SLOTS + 1) * PARTS)
            for i in range((rounds + 1) * SLOTS, GNN_SLABS + SLOTS):
                sp.wait_ge(part_used, (i - SLOTS + 1) * PARTS)
                load(i)
            def split_round(r):
                for s in load_round(r):
                    sp.wait_ge(lo_ready, (r * SLOTS + s - SLOTS - GNN_SLABS + 1) * PARTS + split_no(GNN_SLABS, 0))

            start = GNN_SLABS + SLOTS
            for i in range(start, -(-start // SLOTS) * SLOTS):
                sp.wait_ge(lo_ready, split_no(i - SLOTS, PARTS - 1) + 1)
                load(i)
            with sp.Fori(-(-start // SLOTS), STAGED // SLOTS) as r:
                split_round(r)
            sp.wait_ge(composed, 4)
            load(STAGED)
            for i in range(STAGED + 1, STAGED + SLOTS):
                sp.wait_ge(lo_ready, split_no(i - SLOTS, PARTS - 1) + 1)
                load(i)
            with sp.Fori(STAGED // SLOTS + 1, STREAM // SLOTS) as r:
                split_round(r)
            sp.wait_ge(lo_ready, split_no(STREAM - SLOTS, PARTS - 1) + 1)
            sp.dma_start(ring[:, 0, 0:2048], A["w_down"]).then_inc(down_in, 16)
            sp.dma_start(ring[:, 0, 2048:3072].rearrange("p (k n) -> p k n", k=2)[:, :, 0:G1], A["w_l"]).then_inc(down_in, 16)
            sp.dma_start(ring[:, 0, 2048:3072].rearrange("p (k n) -> p k n", k=2)[:, :, G1:], A["w_r"]).then_inc(down_in, 16)
            sp.wait_ge(lo_ready, split_no(STREAM - SLOTS + 1, PARTS - 1) + 1)
            sp.dma_start(ring[:, 1, 0:2048], A["w_up"]).then_inc(up_in, 16)
            sp.dma_start(ring[0:64, 1, 2048:3072], A["disha"]).then_inc(up_in, 16)
            sp.dma_start(ring[64:128, 1, 2048:3072], A["disha"]).then_inc(up_in, 16)
            sp.wait_ge(lo_ready, split_no(STREAM - 1, PARTS - 1) + 1)
            sp.dma_start(ring[:, 2, :], A["stream"][STREAM]).then_inc(slab_in[2], 16)
            sp.wait_ge(lr_done, 1)
            sp.dma_start(ring[:, 0, :], A["stream"][STREAM + 1]).then_inc(slab_in[0], 16)
            for n in range(2):
                sp.wait_ge(fin_ready, n + 1)
                sp.dma_start(out[:, n * BANK:(n + 1) * BANK], xc[:, n * BANK:(n + 1) * BANK]).then_inc(out_done, 16)
            sp.wait_ge(out_done, 32)

        @block.gpsimd
        def _(pool):
            stages = [stage] * 3 + [ring[:, STAGED % SLOTS, :]]

            def coefs(k):
                src = A["coef"][k]
                stage = stages[k]
                for s in range(STAGES):
                    rows = 2 ** (STAGES + 1 - s)
                    width = NT * 2 ** (s + 1)
                    at = NT * (2 ** (s + 1) - 2)
                    row_src = src[s].rearrange("(r f) -> r f", r=rows)
                    pool.dma_start(stage[:, at:at + width],
                                   row_src[:, None, :].broadcast_to([rows, 2 ** s, width])
                                   ).then_inc(coef_in[k], 16)

            nc.gpsimd.memset(ident[:], 0.0).then_inc(pool_step, 1)
            nc.gpsimd.memset(minus_half[:], -0.5).then_inc(pool_step, 1)
            pool.wait_ge(pool_step, 2)
            nc.gpsimd.affine_select(out=ident[:], in_=ident[:], compare_op=ALU.not_equal, fill=1.0, base=0,
                                    pattern=[[-1, P]], channel_multiplier=1).then_inc(consts, 1)

            def root(n):
                pool.wait_ge(var_ready, n)
                nc.gpsimd.tensor_tensor(rstd[:], mv[:, 1:2], minus_half[:], ALU.pow).then_inc(rstd_ready, 1)

            root(1)
            nc.gpsimd.iota(node_row[:], pattern=[[1, T]], base=0, channel_multiplier=0,
                           allow_small_or_imprecise_dtypes=True).then_inc(consts, 1)
            nc.gpsimd.iota(node_col[:], pattern=[[0, 1]], base=0, channel_multiplier=1,
                           allow_small_or_imprecise_dtypes=True).then_inc(consts, 1)
            nc.gpsimd.memset(after[:], 1.0).then_inc(pool_step, 1)
            pool.wait_ge(pool_step, 3)
            nc.gpsimd.affine_select(out=after[:], in_=after[:], compare_op=ALU.is_gt, fill=0.0, base=0,
                                    pattern=[[1, EP]], channel_multiplier=-1).then_inc(consts, 1)
            pool.wait_ge(slab_in[2], 16)
            pool.dma_start(ends[:, :, :].bitcast(I32), A["ends"][None, :, :].broadcast_to([P, 2, EP])).then_inc(ends_in, 16)
            pool.wait_ge(slab_in[7 % SLOTS], 16 * (7 // SLOTS + 1))
            pool.dma_start(rows, A["rows"][None, :, :].broadcast_to([T, 3, D])).then_inc(rows_in, 16)
            nc.gpsimd.memset(mix_low[:, :, :].rearrange("p n c -> p (n c)"), 0.0).then_inc(zeroed, 1)
            pool.wait_ge(hot_made, 2)
            pool.wait_ge(live_ready, 1)
            nc.gpsimd.tensor_tensor(src_live[:], src_hot[:], stands[:, :, None].broadcast_to([P, ET, T]),
                                    ALU.mult).then_inc(pool_hot, 1)
            nc.gpsimd.tensor_tensor(dst_code[:], dst_hot[:].bitcast(F32), live_code[:, :, None].broadcast_to([P, ET, T]),
                                    ALU.mult).then_inc(pool_hot, 1)
            pool.wait_ge(rows_in, 16)
            pool.wait_ge(centered, 2)
            nc.gpsimd.tensor_tensor(x[:], x[:], rows[:, 0, :], ALU.add).then_inc(biased, 1)
            nc.gpsimd.tensor_tensor(bcs[:], rows[:, 1, :], rows[:, 2, :], ALU.add).then_inc(bcs_ready, 1)
            pool.wait_ge(biased, 1)
            pool.wait_ge(bcs_ready, 1)
            nc.gpsimd.memset(mix_high[:, :, :].rearrange("p n c -> p (n c)"), 0.0).then_inc(zeroed, 1)
            pool.wait_ge(slab_in[9 % SLOTS], 16 * (9 // SLOTS + 1))
            coefs(0)
            done = 3
            for k in range(4):
                mix = (mix_low, mix_high)[k % 2]
                pool.wait_ge(coef_in[k], 16 * STAGES)
                cur = stages[k][:, 0:NT * 2].rearrange("p (g n) -> p g n", g=NT)
                for s in range(1, STAGES):
                    n = 2 ** s
                    at = NT * (2 * n - 2)
                    coef = stages[k][:, at:at + NT * 2 * n].rearrange("p (g b n) -> p g b n", g=NT, b=2)
                    if s < STAGES - 1:
                        dst = (cur_even, cur_odd)[s % 2][:, 0:NT * 2 * n]
                        new = dst.rearrange("p (g b n) -> p g b n", g=NT, b=2)
                        ins = nc.gpsimd.tensor_tensor(new, cur[:, :, None, :].broadcast_to([P, NT, 2, n]), coef, ALU.mult)
                        if k == 2 and s == STAGES - 2:
                            ins.then_inc(running, 1)
                            pool.wait_ge(running, 1)
                        else:
                            ins.then_inc(pool_step, 1)
                            done += 1
                            pool.wait_ge(pool_step, done)
                        cur = dst.rearrange("p (g n) -> p g n", g=NT)
                        continue
                    if k < 2:
                        pool.wait_ge(zeroed, k + 1)
                    if k == 2:
                        pool.wait_ge(lo_ready, split_no(STAGED - SLOTS, PARTS - 1) + 1)
                        coefs(3)
                        pool.wait_ge(up1_done, 4)
                    if k == 3:
                        pool.wait_ge(up2_done, 4)
                    for h in range(1 if k == 2 else 2):
                        hs = slice(64 * h, 64 * h + 64)
                        new = mix[hs, :, 64 * h:64 * h + 64].rearrange("p g (b n) -> p g b n", b=2)
                        ins = nc.gpsimd.tensor_tensor(new, cur[hs, :, None, :].broadcast_to([64, NT, 2, n]),
                                                      coef[hs], ALU.mult)
                        if h == 0 and k != 2:
                            ins.then_inc(pool_step, 1)
                            done += 1
                            pool.wait_ge(pool_step, done)
                    ins.then_inc(composed, 1)
                    pool.wait_ge(composed, k + 1)
                if k < 2:
                    coefs(k + 1)
                if k == 0:
                    root(2)
                if k == 2:
                    pool.wait_ge(upper_composed, 1)
            root(3)
            pool.wait_ge(ms_ready, 1)
            nc.gpsimd.tensor_tensor(rms[:], ms[:], minus_half[:], ALU.pow).then_inc(rms_ready, 1)
            pool.wait_ge(rms_ready, 1)
            nc.gpsimd.tensor_tensor(rms[:], rms[:], rstd[:], ALU.mult).then_inc(rms_ready, 1)
            for c in range(3):
                pool.wait_ge(e_lo_ready, c + 1)
                if c == 2:
                    pool.wait_ge(pair_done, 1)
                spread_low(nc.gpsimd, c, *groups(c)[0]).then_inc(rhs_lo_ready, 1)
            root(4)

        @block.scalar
        def _(act):
            act.dma_start(edge_cols[:], A["edge_cols"]).then_inc(edge_in, 16)
            act.dma_start(by_feature[:], A["by_feature"]).then_inc(small_in, 16)
            act.dma_start(etw[:], A["etw"].broadcast_to([T, 4])).then_inc(small_in, 16)
            act.wait_ge(small_in, 32)
            nc.scalar.activation(sp_t[:, 0, :], etw[:], ACT.Abs).then_inc(act_step, 1)
            act.wait_ge(act_step, 1)
            nc.scalar.activation(sp_t[:, 1, :], sp_t[:, 0, :], ACT.Exp, scale=-1.0).then_inc(act_step, 1)
            act.wait_ge(act_step, 2)
            nc.scalar.activation(sp_t[:, 2, :], sp_t[:, 1, :], ACT.Ln, bias=1.0).then_inc(soft_ready, 1)

            splits = [0]

            def split_until(slab, part):
                while splits[0] < split_no(slab, part):
                    n = splits[0]
                    i, c = part_of_split(n)
                    if c == 0:
                        act.wait_ge(slab_in[slot_of(i)], 16 * (i // SLOTS + 1))
                    if n >= NSPLIT:
                        j, d = part_of_split(n - NSPLIT)
                        act.wait_ge(part_used, PARTS * j + d + 1)
                    nc.scalar.copy(part_hi[:, n % NSPLIT, :], ring[:, slot_of(i), c * PART:(c + 1) * PART]
                                   ).then_inc(hi_ready, 1)
                    splits[0] += 1

            def copy_probs(c):
                act.wait_ge(probs_turned, c + 1)
                nc.scalar.copy(PT[:, 4 * c:4 * c + 4, :], bank[4 + c][0:T, 0:4 * T].rearrange("p (h t) -> p h t", t=T)
                               ).then_inc(probsT_ready, 1)

            for j in range(6):
                for n in range(2):
                    split_until(2 * j + n + 2, 0)
                    if j == 5 and n == 1:
                        split_until(12, 2)
                        copy_probs(1)
                        copy_probs(3)
                        split_until(12, 3)
                    act.wait_ge(part_used, PARTS * (2 * j + n + 1))
                    if j >= 2:
                        act.wait_ge(turned[j - 2], 2)
                    to, result = tok[:, j % 2, n * BANK:(n + 1) * BANK], bank[2 * (j % 2) + n][0:T, :]
                    if j in (0, 1, 4):
                        act.wait_ge(rstd_ready, 1)
                        nc.scalar.mul(to, result, rstd[:]).then_inc(tok_ready[j], 1)
                    else:
                        nc.scalar.copy(to, result).then_inc(tok_ready[j], 1)
                    if j == 4 and n == 1:
                        split_until(2 * j + 3, 0)
                        for g in range(2):
                            act.wait_ge(shifted, g + 1)
                            nc.scalar.activation(S[:, g * 768:(g + 1) * 768], S[:, g * 768:(g + 1) * 768],
                                                 ACT.Exp).then_inc(exped, 1)
                            split_until(2 * j + 3, 1 + g)

            def evac_up1(m):
                act.wait_ge(up1_done, m + 1)
                for h in range(2):
                    take_step(by_group, m, 6, h, nc.scalar.copy).then_inc(up1_read, 1)

            for n in range(EXP_SLABS):
                split_until(GNN_SLABS + n, PARTS)
                if n >= 4 and n % 2 == 0:
                    evac_up1((n - 4) // 2)
                split_until(GNN_SLABS + n + 1, 2)
                act.wait_ge(part_used, PARTS * (GNN_SLABS + n + 1))
                if n >= 2:
                    act.wait_ge(exp_turned, n - 1)
                if n == 0:
                    act.wait_ge(rstd_ready, 2)
                nc.scalar.mul(tok[:, n % 2, 0:BANK], bank[n % 4][0:T, :], rstd[:]).then_inc(exp_tok, 1)
            evac_up1(2)
            evac_up1(3)
            act.wait_ge(composed, 3)
            act.wait_ge(upper_composed, 1)
            for m in range(4):
                act.wait_ge(up2_done, m + 1)
                take_step(by_place, m, STEP[m], 0, nc.scalar.copy).then_inc(up2_read0, 1)

            def gelu(c):
                act.wait_ge(act_biased, c + 1)
                g = B1[:, 4 * c:4 * c + 4, :]
                nc.scalar.activation(g, g, ACT.Gelu).then_inc(act_fm, 1)

            def evac_dn1(m):
                act.wait_ge(dn1_done, m + 1)
                take_step(by_group, m, STEP[m], 0, nc.scalar.copy).then_inc(dn1_read0, 1)

            for c in range(8):
                gelu(c)
                if c >= 6:
                    evac_dn1(c - 6)
            evac_dn1(2)
            evac_dn1(3)
            act.dma_start(by_node[0:T, :, 0:EP].bitcast(I32), A["ends"][None, :, :].broadcast_to([T, 2, EP])).then_inc(idx_in, 16)
            for c in range(8):
                if c >= 2:
                    split_until(GNN_SLABS + EXP_SLABS + c - 2, 3)
                act.wait_ge(dn2_done, c + 1)
                nc.scalar.copy(z_hi[:, 4 * c:4 * c + 4, :],
                               bank[(6, 2)[c % 2]][:, 0:4 * T].rearrange("p (r t) -> p r t", t=T)).then_inc(dn2_read0, 1)
                if c >= 1:
                    split_until(GNN_SLABS + EXP_SLABS + c - 1, 3 if c == 1 else 2)
            split_until(STREAM, NSPLIT)
            act.wait_ge(lr_done, 1)
            act.wait_ge(rms_ready, 2)
            nc.scalar.mul(lr_hi[:], bank[7][0:T, :], rms[:]).then_inc(lr_split, 1)
            act.wait_ge(lr_split, 2)
            nc.scalar.mul(tok[:, 1, 0:BANK], bank[7][0:T, :], rms[:]).then_inc(lr_ready, 1)
            for i in range(8):
                c, f = i // 2, i % 2
                w = min(BANK, EL - c * BANK)
                act.wait_ge(z_done, i + 1)
                if i >= 2:
                    act.wait_ge(msg_ready, i - 1)
                nc.scalar.mul(small_fm[:, i % 2, 0:w], bank[i % 4][:, 0:w], 0.2).then_inc(z_scaled, 1)
            act.wait_ge(pair_shift, 1)
            nc.scalar.activation(alpha[:, 0:H1, :], alpha[:, 0:H1, :], ACT.Exp).then_inc(pair_exp, 1)
            split_until(STREAM + 2, 0)

        @block.tensor
        def _(pe):
            def part(i, c, lhs, dst, first, last):
                n = split_no(i, c)
                split = c < split_parts(i)
                if split:
                    pe.wait_ge(lo_ready, n + 1)
                    hi, lo = part_hi[:, n % NSPLIT, :], part_lo[:, n % NSPLIT, :]
                else:
                    pe.wait_ge(slab_in[slot_of(i)], 16 * (i // SLOTS + 1))
                    raw = ring[:, slot_of(i), c * PART:(c + 1) * PART]
                for k in range(2):
                    cols = slice(k * BANK, (k + 1) * BANK)
                    tile = 2 * c + k if len(dst) == 1 else c
                    b = dst[k % len(dst)][0:T, :]
                    start = first and (k == 0 or len(dst) == 2)
                    stop = last and (k == 1 or len(dst) == 2)
                    if split:
                        nc.tensor.matmul(b, lhs[1][:, tile, :], hi[:, cols], start=start, stop=False)
                        nc.tensor.matmul(b, lhs[1][:, tile, :], lo[:, cols], start=False, stop=False)
                        mm = nc.tensor.matmul(b, lhs[2][:, tile, :], hi[:, cols], start=False, stop=stop)
                    else:
                        mm = nc.tensor.matmul(b, lhs[0][:, tile, :], raw[:, cols], start=start, stop=stop)
                mm.then_inc(part_used, 1)

            def keep_clock(n, free):
                for _ in range(n):
                    nc.tensor.matmul(bank[free][:, 0:P], ident[:], ident[:], start=True, stop=True)

            def turn8(src, done, half_ready=None, before=0):
                for c in range(2):
                    if half_ready is not None:
                        pe.wait_ge(half_ready, before + c + 1)
                    for k in range(4):
                        mm = nc.tensor.transpose(bank[4 + c][:, k * T:(k + 1) * T],
                                                 src[:, (4 * c + k) * P:(4 * c + k + 1) * P], ident[0:T, 0:T])
                    mm.then_inc(done, 1)

            pe.wait_ge(consts, 1)
            keep_clock(14, 7)
            turn8(xc, xT_turned, centered, 0)

            def half(j, n, lhs, parts=range(PARTS)):
                for c in parts:
                    part(2 * j + n, c, lhs, [bank[2 * (j % 2) + n]], c == 0, c == PARTS - 1)

            def turn(j):
                pe.wait_ge(tok_ready[j], 2)
                if j >= 1:
                    pe.wait_ge(fm_ready[j - 1], 2)
                turn8(tok[:, j % 2, :], turned[j])

            def probs_turn(g):
                pe.wait_ge(probs_ready, g + 1)
                for c in (2 * g, 2 * g + 1):
                    for i in range(4):
                        mm = nc.tensor.transpose(bank[4 + c][0:T, i * T:(i + 1) * T], S3[:, 4 * c + i, :],
                                                 ident[0:T, 0:T])
                    mm.then_inc(probs_turned, 1)

            rows_T = (xT, xT_hi, xT_lo)
            inputs = [rows_T, rows_T, (fmv[0], fm_hiv[0], fm_lov[0]), (fmv[1], fm_hiv[1], fm_lov[1]), rows_T,
                      (fmv[1], fm_hiv[0], fm_lov[0]), (fmv[2], fm_hiv[1], fm_lov[1])]
            for j in range(6):
                if j >= 2:
                    pe.wait_ge(tok_ready[j - 2], 2)
                if j == 0:
                    pe.wait_ge(xT_ready, 2)
                if j in (2, 3):
                    pe.wait_ge(fm_ready[j - 2], 2)
                if j == 5:
                    keep_clock(11, 3)
                    pe.wait_ge(fm_ready[4], 1)
                half(j, 0, inputs[j], range(0, 2))
                if 1 <= j <= 4:
                    turn(j - 1)
                if j == 5:
                    pe.wait_ge(fm_ready[4], 2)
                half(j, 0, inputs[j], range(2, PARTS))
                if j == 0:
                    pe.wait_ge(xT_ready, 2 + 2)
                half(j, 1, inputs[j], range(0, 2))
                if j == 5:
                    pe.wait_ge(scores_read, 4)
                    probs_turn(0)
                half(j, 1, inputs[j], range(2, 3))
                if j == 5:
                    probs_turn(1)
                half(j, 1, inputs[j], range(3, PARTS))
                if j == 3:
                    pe.wait_ge(hot_made, 2)
                    pe.wait_ge(pool_hot, 2)
                    for t in range(ET):
                        nc.tensor.matmul(bank[6][0:T, 0:T], src_hot[:, t, :], dst_code[:, t, :],
                                         start=(t == 0), stop=(t == ET - 1))
                    for t in range(ET):
                        mm = nc.tensor.matmul(bank[7][0:T, 0:T], dst_hot[:, t, :].bitcast(F32), src_hot[:, t, :],
                                              start=(t == 0), stop=(t == ET - 1))
                    mm.then_inc(counts_done, 1)
                if j == 4:
                    pe.wait_ge(fm_ready[3], 2)
                    pe.wait_ge(counts_read, 1)
                    for c in range(2):
                        if c == 1:
                            turn(4)
                        for par in range(2):
                            for i in range(4):
                                k = 4 * c + i
                                mm = nc.tensor.matmul(bank[SCORE[c][par]][0:T, i * T:(i + 1) * T],
                                                      fmv[2][64 * par:64 * par + 64, k, :],
                                                      fmv[0][64 * par:64 * par + 64, k, :], start=True, stop=True)
                            mm.then_inc(scores_done, 1)
            for c in range(2):
                pe.wait_ge(tok_ready[5], c + 1)
                pe.wait_ge(probsT_ready, 4)
                for k in range(4 * c, 4 * c + 4):
                    for par in range(2):
                        h = 2 * k + par
                        mm = nc.tensor.matmul(bank[2 + c][64 * par:64 * par + 64, (k - 4 * c) * T:(k - 4 * c + 1) * T],
                                              tok[:, 1, h * HD:(h + 1) * HD], PT[:, par * 8 + k, :],
                                              start=True, stop=True)
                mm.then_inc(attended, 1)
            pe.wait_ge(attended_read, 1)
            half(6, 0, inputs[6], range(0, 2))
            pe.wait_ge(attended_read, 2)
            half(6, 0, inputs[6], range(2, PARTS))
            half(6, 1, inputs[6])

            keep_clock(10, 7)
            turn8(xc, xT_turned, centered, 2)

            def expand(n):
                if n >= 4:
                    pe.wait_ge(exp_tok, n - 3)
                for c in range(PARTS):
                    if n == 0 and c in (0, 2):
                        pe.wait_ge(xT_ready, 5 + c // 2)
                    part(GNN_SLABS + n, c, rows_T, [bank[n % 4]], c == 0, c == PARTS - 1)

            def exp_turn(n):
                pe.wait_ge(exp_tok, n + 1)
                if n >= 2:
                    pe.wait_ge(exp_fm, n - 1)
                for k in range(4):
                    mm = nc.tensor.transpose(bank[4 + n % 2][:, k * T:(k + 1) * T],
                                             tok[:, n % 2, k * P:(k + 1) * P], ident[0:T, 0:T])
                mm.then_inc(exp_turned, 1)

            def first_step(m, fm_in, mix, pair):
                for g in range(8):
                    mm = nc.tensor.matmul(bank[pair + g // 4][0:T, (g % 4) * P:(g % 4 + 1) * P],
                                          fm_in[:, 8 * m + g, :], mix[:, 8 * m + g, :], start=True, stop=True)
                return mm

            def up1(m):
                pe.wait_ge(exp_fm, 2 * m + 2)
                if m == 0:
                    pe.wait_ge(composed, 1)
                else:
                    pe.wait_ge(up1_read, 2 * m)
                first_step(m, B1, mix_low, 6).then_inc(up1_done, 1)

            for n in range(EXP_SLABS):
                expand(n)
                if n >= 1:
                    exp_turn(n - 1)
                if n >= 3 and n % 2:
                    up1((n - 3) // 2)
            exp_turn(7)
            up1(3)

            def turn4(c, src, b, done):
                for i in range(4 * c, 4 * c + 4):
                    mm = nc.tensor.transpose(b[:, (i - 4 * c) * T:(i - 4 * c + 1) * T], src[0:T, i * P:(i + 1) * P],
                                             ident[0:T, 0:T])
                mm.then_inc(done, 1)

            pe.wait_ge(up1_read, 8)
            pe.wait_ge(composed, 2)

            def up2(m):
                pe.wait_ge(up2_fm, max(2 * m + 2, 6 * (m % 2)))
                if m >= 2:
                    pe.wait_ge(up2_read0, m - 1)
                    pe.wait_ge(up2_read1, m - 1)
                first_step(m, B0, mix_high, STEP[m]).then_inc(up2_done, 1)

            for c in range(8):
                if c < 2:
                    pe.wait_ge(exp_fm, 8)
                if c >= 6:
                    pe.wait_ge(up2_fm, c - 5)
                turn4(c, U, bank[UPT[c]], up2_turned)
                if c == 5:
                    up2(0)
            for m in range(1, 4):
                up2(m)
            pe.wait_ge(up2_read0, 4)
            pe.wait_ge(up2_read1, 4)

            def dn1(m):
                pe.wait_ge(act_fm, 2 * m + 2)
                if STEP[m] == 2:
                    pe.wait_ge(act_biased, 6)
                if m >= 2:
                    pe.wait_ge(dn1_read0, m - 1)
                    pe.wait_ge(dn1_read1, m - 1)
                first_step(m, B1, mix_low, STEP[m]).then_inc(dn1_done, 1)

            pe.wait_ge(composed, 3)
            pe.wait_ge(upper_composed, 1)
            pe.wait_ge(up2_fm, 8)
            for c in range(8):
                if c >= 6:
                    pe.wait_ge(act_biased, c - 5)
                turn4(c, V, bank[UPT[c]], act_turned)
                if c == 5:
                    dn1(0)
            for m in range(1, 4):
                dn1(m)
            pe.wait_ge(dn1_read0, 4)
            pe.wait_ge(dn1_read1, 4)

            def dn2(c):
                if c == 0:
                    pe.wait_ge(composed, 4)
                pe.wait_ge(dn2_fm, c + 1)
                if c >= 2:
                    pe.wait_ge(dn2_read1, c - 1)
                for i in range(4):
                    mm = nc.tensor.matmul(bank[(6, 2)[c % 2]][:, i * T:(i + 1) * T],
                                          mix_high[:, 4 * c + i, :], B1[:, 4 * c + i, :], start=True, stop=True)
                mm.then_inc(dn2_done, 1)

            def contract_last(s):
                pe.wait_ge(dn2_read1, s + 1)
                slab = GNN_SLABS + EXP_SLABS + s
                for parts in (range(0, 1), range(1, 2), range(2, 4)):
                    for k in range(2):
                        for c in parts:
                            n = split_no(slab, c)
                            pe.wait_ge(lo_ready, n + 1)
                            cols, b = slice(k * BANK, (k + 1) * BANK), bank[k][0:T, :]
                            hi, lo = part_hi[:, n % NSPLIT, cols], part_lo[:, n % NSPLIT, cols]
                            nc.tensor.matmul(b, z_hi[:, 4 * s + c, :], hi, start=False, stop=False)
                            nc.tensor.matmul(b, z_hi[:, 4 * s + c, :], lo, start=False, stop=False)
                            mm = nc.tensor.matmul(b, z_lo[:, 4 * s + c, :], hi, start=False, stop=(c == 3))
                            if k == 1:
                                mm.then_inc(part_used, 1)
                            elif c == 3:
                                mm.then_inc(con_half, 1)

            def contract(s):
                pe.wait_ge(dn2_read1, s + 1)
                for c in range(PARTS):
                    tile = 4 * s
                    part(GNN_SLABS + EXP_SLABS + s, c,
                         (None, z_hi[:, tile:tile + 4, :], z_lo[:, tile:tile + 4, :]),
                         [bank[0], bank[1]], s == 0 and c == 0, s == 7 and c == 3)

            for c in range(8):
                if c < 2:
                    pe.wait_ge(act_biased, 8)
                else:
                    pe.wait_ge(dn2_fm, c - 1)
                turn4(c, U, bank[4 + c % 2], dn2_turned)
                if c >= 1:
                    dn2(c - 1)
                if c >= 3:
                    contract(c - 3)
            dn2(7)
            contract(5)
            contract(6)
            contract_last(7)

            keep_clock(10, 7)
            turn8(xc, xT_turned, centered, 4)
            small, big = ring[:, 0, :], ring[:, 1, :]
            pe.wait_ge(down_in, 48)
            pe.wait_ge(xT_ready, 8)
            for m in range(2):
                for k in range(KD):
                    mm = nc.tensor.matmul(bank[6][:, m * T:(m + 1) * T], small[:, k * G1 + m * P:k * G1 + (m + 1) * P],
                                          xT[:, k, :], start=(k == 0), stop=(k == KD - 1))
            mm.then_inc(wd_done, 1)
            pe.wait_ge(wd_fm, 1)
            for k in range(2):
                mm = nc.tensor.matmul(bank[7][0:T, :], sfm[2][:, k, :], small[:, 2048 + k * 512:2048 + (k + 1) * 512],
                                      start=(k == 0), stop=(k == 1))
            mm.then_inc(lr_done, 1)
            pe.wait_ge(hot_ready, 4)
            pe.wait_ge(lr_split, 1)

            def messages(c):
                w = min(BANK, EL - c * BANK)
                for f in range(2):
                    i = 2 * c + f
                    if i >= 4:
                        pe.wait_ge(msg_ready, i - 3)
                    for half, rows in enumerate((lr_hi, lr_lo)):
                        if half == 1 and i == 0:
                            pe.wait_ge(lr_split, 2)
                        for side, hot in enumerate((src_by_node, dst_by_node)):
                            mm = nc.tensor.matmul(bank[i % 4][:, 0:w], rows[:, side * G1 + f * P:side * G1 + (f + 1) * P],
                                                  hot[:, c * BANK:c * BANK + w], start=(half + side == 0),
                                                  stop=(half + side == 2))
                    mm.then_inc(z_done, 1)

            def logits(c):
                pe.wait_ge(msg_ready, 2 * c + 2)
                if c >= 2:
                    pe.wait_ge(rhs_ready, c - 1)
                if c == 1:
                    pe.wait_ge(lr_ready, 1)
                for t in range(4 * c, min(4 * c + 4, LT)):
                    w = P if t < ET else T
                    for f in range(2):
                        mm = nc.tensor.matmul(bank[(5, 7)[c % 2]][0:w, t * H1:(t + 1) * H1],
                                              msg[:, f, t * P:t * P + w],
                                              att[:, f, :], start=(f == 0), stop=(f == 1))
                mm.then_inc(e_done, 1)

            def spread(c):
                pe.wait_ge(rhs_ready, c + 1 if c < 3 else 7)
                if c < 3:
                    pe.wait_ge(rhs_lo_ready, c + 1)
                for t in range(4 * c, min(4 * c + 4, LT)):
                    w, dst = (P, dst_hot[:, t, :]) if t < ET else (T, loop_hot[:])
                    k = (t - 4 * c) * H1
                    nc.tensor.matmul(bank[6][0:T, 0:H1 * T], dst,
                                     edge_rhs[0:w, t, :, :].rearrange("p h t -> p (h t)"), start=(t == 0), stop=False)
                    mm = nc.tensor.matmul(bank[6][0:T, 0:H1 * T], dst,
                                          edge_rhs_lo[0:w, c % 2, k:k + H1, :].rearrange("p h t -> p (h t)"),
                                          start=False, stop=(t == LT - 1))
                mm.then_inc(pair_done, 1)

            pe.wait_ge(loops_ready, 1)
            messages(0)
            messages(1)
            logits(0)
            messages(2)
            logits(1)
            spread(0)
            messages(3)
            logits(2)
            spread(1)
            logits(3)
            keep_clock(5, 4)
            spread(2)
            spread(3)
            keep_clock(20, 7)
            pe.wait_ge(alpha_ready, 1)
            for h in range(H1):
                mm = nc.tensor.transpose(bank[4][0:T, h * T:(h + 1) * T], alpha[:, h, :], ident[0:T, 0:T])
            mm.then_inc(alpha_turned, 1)
            keep_clock(3, 7)
            pe.wait_ge(alphaT_ready, 1)
            for h in range(H1):
                p0 = 64 * (h % 2)
                mm = nc.tensor.matmul(bank[5][p0:p0 + 64, (h // 2) * T:(h // 2 + 1) * T],
                                      tok[:, 1, h * 64:(h + 1) * 64], alpha[:, H1 + h, :], start=True, stop=True)
            mm.then_inc(agg_done, 1)
            keep_clock(3, 7)
            pe.wait_ge(agg_ready, 1)
            pe.wait_ge(up_in, 48)
            for n in range(2):
                for k in range(2):
                    mm = nc.tensor.matmul(bank[n][0:T, :], sfm[2][:, k, :], big[:, k * D + n * BANK:k * D + (n + 1) * BANK],
                                          start=(k == 0), stop=(k == 1))
                mm.then_inc(up_done, 1)

            keep_clock(9, 7)
            turn8(xc, xT_turned, centered, 6)
            for n in range(2):
                for c in range(PARTS):
                    if n == 0 and c in (0, 2):
                        pe.wait_ge(xT_ready, 9 + c // 2)
                    if n == 0 and c == 3:
                        pe.wait_ge(xT_ready, 12)
                    part(STREAM + n, c, rows_T, [bank[2 + n]], c == 0, False)
                pe.wait_ge(xT_ready, 13)
                nc.tensor.matmul(bank[2 + n][0:T, :], pooled[:], big[:, 2048 + n * BANK:2048 + (n + 1) * BANK],
                                 start=False, stop=True).then_inc(fin_done, 1)

        @block.vector
        def _(dve):
            steps = [0]

            def step(ins):
                steps[0] += 1
                ins.then_inc(dve_step, 1)
                dve.wait_ge(dve_step, steps[0])

            def layer_norm():
                for n in range(2):
                    st = nc.vector.bn_stats(stats[:, n, :], x[:, n * BANK:(n + 1) * BANK])
                step(st)
                center()

            def center():
                step(nc.vector.bn_aggr(mv[:], stats[:]))
                for n in range(2):
                    cols = slice(n * BANK, (n + 1) * BANK)
                    nc.vector.tensor_scalar(xc[:, cols], x[:, cols], mv[:, 0:1], None, ALU.subtract
                                            ).then_inc(centered, 1)
                nc.vector.tensor_scalar(mv[:, 1:2], mv[:, 1:2], LN_EPS, None, ALU.add).then_inc(var_ready, 1)

            subs = [0]

            def sub_until(slab, part):
                while subs[0] < split_no(slab, part):
                    n = subs[0]
                    i, c = part_of_split(n)
                    dve.wait_ge(hi_ready, n + 1)
                    nc.vector.tensor_tensor(part_lo[:, n % NSPLIT, :], ring[:, slot_of(i), c * PART:(c + 1) * PART],
                                            part_hi[:, n % NSPLIT, :].bitcast(F32), ALU.subtract).then_inc(lo_ready, 1)
                    subs[0] += 1

            def split_to(hi, lo, src, done):
                step(nc.vector.tensor_copy(hi, src))
                nc.vector.tensor_tensor(lo, src, hi.bitcast(F32), ALU.subtract).then_inc(done, 1)

            def take_xT(t0, split, scale=None):
                for c in range(2):
                    dve.wait_ge(xT_turned, t0 + c + 1)
                    src = bank[4 + c][:, 0:4 * T].rearrange("p (k t) -> p k t", t=T)
                    ks = slice(4 * c, 4 * c + 4)
                    if split:
                        split_to(xT_hi[:, ks, :], xT_lo[:, ks, :], src, xT_ready)
                    elif scale is None:
                        nc.vector.tensor_copy(xT[:, ks, :], src).then_inc(xT_ready, 1)
                    else:
                        nc.vector.tensor_tensor(xT[:, ks, :], src, scale[:, ks, None].broadcast_to([P, 4, T]),
                                                ALU.mult).then_inc(xT_ready, 1)

            def take_turn(j, dst, split=None):
                for c in range(2):
                    dve.wait_ge(turned[j], c + 1)
                    src = bank[4 + c][:, 0:4 * T].rearrange("p (k t) -> p k t", t=T)
                    ks = slice(4 * c, 4 * c + 4)
                    b = bias_fm[:, BIAS[j], ks, None].broadcast_to([P, 4, T])
                    ins = nc.vector.tensor_tensor(dst[:, ks, :], src, b, ALU.add)
                    if split is None:
                        ins.then_inc(fm_ready[j], 1)
                    else:
                        step(ins)
                        split_to(fm_hiv[split][:, ks, :], fm_lov[split][:, ks, :], dst[:, ks, :], fm_ready[j])

            BIAS = [0, 1, 2, 3, 4, 5]
            dve.wait_ge(x_in, 16)
            layer_norm()
            take_xT(0, False)
            dve.wait_ge(xT_ready, 2)
            for c in range(2):
                ks = slice(4 * c, 4 * c + 4)
                split_to(xT_hi[:, ks, :], xT_lo[:, ks, :], xT[:, ks, :], xT_ready)
            sub_until(4, 0)
            dve.wait_ge(small_in, 32)
            take_turn(0, fmv[0], 0)
            dve.wait_ge(edge_in, 16)
            dve.wait_ge(ends_in, 16)
            dve.wait_ge(consts, 4)
            step(nc.vector.scalar_tensor_tensor(out=keys, in0=keys.bitcast(I32), scalar=float(T),
                                                in1=dst_bc.bitcast(I32), op0=ALU.mult, op1=ALU.add))
            step(nc.vector.scalar_tensor_tensor(out=key_col[:], in0=src_col, scalar=float(T), in1=dst_col,
                                                op0=ALU.mult, op1=ALU.add))
            nodes = node_row[:, None, :].broadcast_to([P, ET, T])
            nc.vector.tensor_tensor(dst_hot[:], dst_col[:, :, None].broadcast_to([P, ET, T]), nodes,
                                    ALU.is_equal).then_inc(hot_made, 1)
            nc.vector.tensor_copy(loop_hot[:], ident[0:T, 0:T]).then_inc(loops_ready, 1)
            parts_after = {3: (6, 0), 6: (7, 0), 12: (8, 0)}
            for t in range(ET):
                w = EP - t * P
                step(nc.vector.scalar_tensor_tensor(out=junk[:, 0:w], in0=keys[:, t * P:EP], scalar=key_col[:, t:t + 1],
                                                    in1=after[:, 0:w], op0=ALU.is_equal, op1=ALU.mult,
                                                    accum_out=later[:, t:t + 1]))
                if t == 3:
                    take_turn(1, fmv[1], 1)
                if t in parts_after:
                    sub_until(*parts_after[t])
            take_turn(2, fmv[2])
            nc.vector.tensor_tensor(src_hot[:], src_col[:, :, None].broadcast_to([P, ET, T]), nodes,
                                    ALU.is_equal).then_inc(hot_made, 1)
            step(nc.vector.tensor_scalar(live[:], later[:], 0.0, None, ALU.is_equal))
            step(nc.vector.tensor_scalar(code[:], type_col, 0.0, 4.0, ALU.is_equal, ALU.mult))
            step(nc.vector.tensor_tensor(code[:], code[:], type_col, ALU.add))
            step(nc.vector.tensor_tensor(stands[:], src_col, dst_col, ALU.not_equal))
            step(nc.vector.tensor_tensor(stands[:], stands[:], live[:], ALU.mult))
            nc.vector.tensor_tensor(live_code[:], live[:], code[:], ALU.mult).then_inc(live_ready, 1)
            sub_until(9, 0)

            dve.wait_ge(counts_done, 1)
            dve.wait_ge(soft_ready, 1)
            step(nc.vector.scalar_tensor_tensor(out=sp_t[:, 3, :], in0=etw[:], scalar=0.0, in1=sp_t[:, 2, :],
                                                op0=ALU.max, op1=ALU.add))
            step(nc.vector.tensor_copy(mtmp[:, 0, :], bank[6][0:T, 0:T]))
            step(nc.vector.tensor_scalar(mtmp[:, 1, :], mtmp[:, 0, :], 0.0, 4.0, ALU.is_equal, ALU.mult))
            step(nc.vector.tensor_tensor(mtmp[:, 1, :], mtmp[:, 1, :], ident[0:T, 0:T], ALU.mult))
            step(nc.vector.tensor_tensor(mtmp[:, 0, :], mtmp[:, 0, :], mtmp[:, 1, :], ALU.add))
            step(nc.vector.tensor_scalar(mask[:], mtmp[:, 0, :], 0.0, -BIG, ALU.is_equal, ALU.mult))
            for c in range(4):
                step(nc.vector.tensor_scalar(mtmp[:, 1, :], mtmp[:, 0, :], float(c + 1), sp_t[:, 3, c:c + 1],
                                             ALU.is_equal, ALU.mult))
                step(nc.vector.tensor_tensor(mask[:], mask[:], mtmp[:, 1, :], ALU.add))
            step(nc.vector.tensor_tensor(count[:], ident[0:T, 0:T], bank[7][0:T, 0:T], ALU.add))
            nc.vector.tensor_scalar(absent[:], count[:], 0.0, -BIG, ALU.is_equal, ALU.mult).then_inc(counts_read, 1)
            sub_until(9, 1)
            dve.wait_ge(part_used, PARTS * 6)
            take_turn(3, fmv[0])
            sub_until(10, 2)

            def take_scores(c):
                for par in range(2):
                    dve.wait_ge(scores_done, 2 * c + par + 1)
                    at = (par * 8 + c * 4) * T
                    nc.vector.scalar_tensor_tensor(out=S[:, at:at + 4 * T].rearrange("p (h t) -> p h t", t=T),
                                                   in0=bank[SCORE[c][par]][0:T, 0:4 * T].rearrange("p (h t) -> p h t", t=T),
                                                   scalar=float(HD) ** -0.5,
                                                   in1=mask[:, None, :].broadcast_to([T, 4, T]),
                                                   op0=ALU.mult, op1=ALU.add).then_inc(scores_read, 1)

            take_scores(0)
            dve.wait_ge(part_used, PARTS * 8)
            take_turn(4, fmv[1], 0)
            take_scores(1)
            sub_until(10, 3)
            dve.wait_ge(scores_read, 4)
            for g in range(2):
                sl = S3[:, 8 * g:8 * g + 8, :]
                step(nc.vector.tensor_reduce(mx[:, 8 * g:8 * g + 8], sl, AX.X, ALU.max))
                nc.vector.tensor_tensor(sl, sl, mx[:, 8 * g:8 * g + 8, None].broadcast_to([T, 8, T]),
                                        ALU.subtract).then_inc(shifted, 1)
            sub_until(11, 1)
            for g in range(2):
                sl = S3[:, 8 * g:8 * g + 8, :]
                dve.wait_ge(exped, g + 1)
                step(nc.vector.tensor_reduce(den[:, 8 * g:8 * g + 8], sl, AX.X, ALU.add))
                step(nc.vector.reciprocal(den[:, 8 * g:8 * g + 8], den[:, 8 * g:8 * g + 8]))
                nc.vector.tensor_tensor(sl, sl, den[:, 8 * g:8 * g + 8, None].broadcast_to([T, 8, T]),
                                        ALU.mult).then_inc(probs_ready, 1)
                sub_until(11, 2 + g)
            sub_until(12, 2)
            for c in (0, 2):
                dve.wait_ge(probs_turned, c + 1)
                nc.vector.tensor_copy(PT[:, 4 * c:4 * c + 4, :],
                                      bank[4 + c][0:T, 0:4 * T].rearrange("p (h t) -> p h t", t=T)).then_inc(probsT_ready, 1)
            sub_until(12, 3)
            for c in range(2):
                dve.wait_ge(attended, c + 1)
                ks = slice(4 * c, 4 * c + 4)
                step(nc.vector.tensor_tensor(fmv[2][:, ks, :], bank[2 + c][:, 0:4 * T].rearrange("p (k t) -> p k t", t=T),
                                             bias_fm[:, 5, ks, None].broadcast_to([P, 4, T]), ALU.add))
                split_to(fm_hiv[1][:, ks, :], fm_lov[1][:, ks, :], fmv[2][:, ks, :], attended_read)

            sub_until(14, 0)
            dve.wait_ge(biased, 1)
            for n in range(2):
                cols = slice(n * BANK, (n + 1) * BANK)
                dve.wait_ge(part_used, PARTS * (13 + n))
                step(nc.vector.tensor_tensor(x[:, cols], x[:, cols], bank[n][0:T, :], ALU.add))
                st = nc.vector.bn_stats(stats[:, n, :], x[:, cols])
                if n == 0:
                    sub_until(14, 2)
            step(st)
            center()
            take_xT(2, True)
            sub_until(15, 0)
            dve.wait_ge(bcs_ready, 1)
            step(nc.vector.tensor_tensor(x[:], x[:], bcs[:], ALU.add))
            for n in range(EXP_SLABS):
                sub_until(GNN_SLABS + min(n + 2, EXP_SLABS), 2)
                dve.wait_ge(exp_turned, n + 1)
                nc.vector.tensor_tensor(B1[:, 4 * n:4 * n + 4, :],
                                        bank[4 + n % 2][:, 0:4 * T].rearrange("p (k t) -> p k t", t=T),
                                        bexp[:, 4 * n:4 * n + 4, None].broadcast_to([P, 4, T]), ALU.add).then_inc(exp_fm, 1)

            def evac_up2(m):
                dve.wait_ge(up2_done, m + 1)
                take_step(by_place, m, STEP[m], 1, nc.vector.tensor_copy).then_inc(up2_read1, 1)

            dve.wait_ge(running, 1)
            dve.wait_ge(up1_done, 4)
            n = GRP // 2
            at = NT * (2 * n - 2)
            nc.vector.tensor_tensor(
                mix_low[64:128, :, 64:128].rearrange("p g (b n) -> p g b n", b=2),
                cur_even[64:128, :].rearrange("p (g n) -> p g n", g=NT)[:, :, None, :].broadcast_to([64, NT, 2, n]),
                stage[64:128, at:at + NT * 2 * n].rearrange("p (g b n) -> p g b n", g=NT, b=2), ALU.mult
            ).then_inc(upper_composed, 1)
            for c in range(8):
                dve.wait_ge(up2_turned, c + 1)
                nc.vector.tensor_copy(B0[:, 4 * c:4 * c + 4, :],
                                      bank[UPT[c]][:, 0:4 * T].rearrange("p (k t) -> p k t", t=T)).then_inc(up2_fm, 1)
                if c == 6:
                    dve.wait_ge(composed, 3)
                    dve.wait_ge(upper_composed, 1)
                if c >= 6:
                    evac_up2(c - 6)
            evac_up2(2)
            evac_up2(3)

            def evac_dn1(m):
                dve.wait_ge(dn1_done, m + 1)
                take_step(by_group, m, STEP[m], 1, nc.vector.tensor_copy).then_inc(dn1_read1, 1)

            for c in range(8):
                dve.wait_ge(act_turned, c + 1)
                nc.vector.tensor_tensor(B1[:, 4 * c:4 * c + 4, :],
                                        bank[UPT[c]][:, 0:4 * T].rearrange("p (k t) -> p k t", t=T),
                                        upb[:, 4 * c:4 * c + 4, None].broadcast_to([P, 4, T]), ALU.add).then_inc(act_biased, 1)
                if c >= 6:
                    evac_dn1(c - 6)
            evac_dn1(2)
            evac_dn1(3)
            CON = GNN_SLABS + EXP_SLABS

            def split_dn2(c):
                dve.wait_ge(dn2_read0, c + 1)
                nc.vector.tensor_tensor(z_lo[:, 4 * c:4 * c + 4, :],
                                        bank[(6, 2)[c % 2]][:, 0:4 * T].rearrange("p (r t) -> p r t", t=T),
                                        z_hi[:, 4 * c:4 * c + 4, :].bitcast(F32), ALU.subtract).then_inc(dn2_read1, 1)

            sub_until(CON, 2)
            for c in range(8):
                dve.wait_ge(dn2_turned, c + 1)
                if c == 0:
                    dve.wait_ge(dn1_done, 4)
                nc.vector.tensor_copy(B1[:, 4 * c:4 * c + 4, :],
                                      bank[4 + c % 2][:, 0:4 * T].rearrange("p (k t) -> p k t", t=T)).then_inc(dn2_fm, 1)
                if c >= 3:
                    sub_until(CON + c - 3, 3)
                if c >= 1:
                    split_dn2(c - 1)
                if c == 2:
                    sub_until(CON, 3)
                if c >= 3:
                    sub_until(CON + c - 2, 2)
            split_dn2(7)
            sub_until(CON + 7, 0)
            sub_until(STREAM, 0)
            for n in range(2):
                cols = slice(n * BANK, (n + 1) * BANK)
                if n == 0:
                    dve.wait_ge(con_half, 1)
                else:
                    dve.wait_ge(part_used, PARTS * STREAM)
                step(nc.vector.tensor_tensor(x[:, cols], x[:, cols], bank[n][0:T, :], ALU.add))
                st = nc.vector.bn_stats(stats[:, n, :], x[:, cols])
            step(st)
            center()
            dve.wait_ge(centered, 6)
            take_xT(4, False, rmsw)
            step(nc.vector.scalar_tensor_tensor(out=tok[:, 1, :], in0=xc[:], scalar=1.0 / D, in1=xc[:],
                                                op0=ALU.mult, op1=ALU.mult, accum_out=ms[:]))
            dve.wait_ge(rstd_ready, 3)
            step(nc.vector.tensor_scalar(ms[:], ms[:], rstd[:], rstd[:], ALU.mult, ALU.mult))
            nc.vector.tensor_scalar(ms[:], ms[:], RMS_EPS, None, ALU.add).then_inc(ms_ready, 1)
            dve.wait_ge(idx_in, 16)
            dve.wait_ge(dn2_done, 8)
            for i, view in enumerate((src_by_node, dst_by_node)):
                nc.vector.tensor_scalar(view[:, 0:EP], by_node[0:T, i, 0:EP].bitcast(I32), node_col[0:T, 0:1], None,
                                        ALU.is_equal).then_inc(hot_ready, 1)
                nc.vector.tensor_copy(view[:, EP:EL], ident[0:T, 0:T]).then_inc(hot_ready, 1)
            dve.wait_ge(wd_done, 1)
            nc.vector.tensor_copy(sfm[2][:, 0:2, :], bank[6][:, 0:2 * T].rearrange("p (k t) -> p k t", t=T)
                                  ).then_inc(wd_fm, 1)
            sub_until(STREAM, 2)
            dve.wait_ge(rms_ready, 2)
            dve.wait_ge(lr_split, 1)
            nc.vector.scalar_tensor_tensor(out=lr_lo[:], in0=bank[7][0:T, :], scalar=rms[:], in1=lr_hi[:].bitcast(F32),
                                           op0=ALU.mult, op1=ALU.subtract).then_inc(lr_split, 1)

            def leaky(c):
                w = min(BANK, EL - c * BANK)
                for f in range(2):
                    i = 2 * c + f
                    dve.wait_ge(z_scaled, i + 1)
                    nc.vector.tensor_tensor(msg[:, f, c * BANK:c * BANK + w], small_fm[:, i % 2, 0:w], bank[i % 4][:, 0:w],
                                            ALU.max).then_inc(msg_ready, 1)

            def weigh(c):
                dve.wait_ge(e_done, c + 1)
                for t0, n, w, hot in groups(c):
                    logits = bank[(5, 7)[c % 2]][0:w, t0 * H1:(t0 + n) * H1]
                    high, low = (e[0:w, t0:t0 + n, :].rearrange("p t h -> p (t h)") for e in (e_hi, e_lo))
                    step(nc.vector.tensor_copy(high, logits))
                    nc.vector.tensor_tensor(low, logits, high.bitcast(F32), ALU.subtract).then_inc(e_lo_ready, 1)
                    nc.vector.tensor_tensor(edge_rhs[0:w, t0:t0 + n, :, :],
                                            hot[:, :, None, :].broadcast_to([w, n, H1, T]),
                                            e_hi[0:w, t0:t0 + n, :, None].bitcast(F32).broadcast_to([w, n, H1, T]),
                                            ALU.mult).then_inc(rhs_ready, 1)

            leaky(0)
            leaky(1)
            weigh(0)
            leaky(2)
            weigh(1)
            leaky(3)
            weigh(2)
            weigh(3)
            dve.wait_ge(e_lo_ready, 5)
            dve.wait_ge(pair_done, 2)
            for group in groups(3):
                spread_low(nc.vector, 3, *group).then_inc(rhs_ready, 1)
            sub_until(STREAM, 3)
            dve.wait_ge(pair_done, 4)
            pr = alpha[:, 0:H1, :]
            step(nc.vector.tensor_tensor(pr, bank[6][0:T, 0:H1 * T].rearrange("p (h t) -> p h t", t=T),
                                         absent[:, None, :].broadcast_to([T, H1, T]), ALU.add))
            step(nc.vector.tensor_reduce(mx[:, 0:H1], pr, AX.X, ALU.max))
            nc.vector.tensor_tensor(pr, pr, mx[:, 0:H1, None].broadcast_to([T, H1, T]), ALU.subtract).then_inc(pair_shift, 1)
            dve.wait_ge(pair_exp, 1)
            step(nc.vector.tensor_tensor(pr, pr, count[:, None, :].broadcast_to([T, H1, T]), ALU.mult))
            step(nc.vector.tensor_reduce(den[:, 0:H1], pr, AX.X, ALU.add))
            step(nc.vector.tensor_scalar(den[:, 0:H1], den[:, 0:H1], 1e-16, None, ALU.add))
            step(nc.vector.reciprocal(den[:, 0:H1], den[:, 0:H1]))
            nc.vector.tensor_tensor(pr, pr, den[:, 0:H1, None].broadcast_to([T, H1, T]), ALU.mult).then_inc(alpha_ready, 1)
            dve.wait_ge(alpha_turned, 1)
            nc.vector.tensor_copy(alpha[:, H1:2 * H1, :], bank[4][0:T, 0:H1 * T].rearrange("p (h t) -> p h t", t=T)
                                  ).then_inc(alphaT_ready, 1)
            dve.wait_ge(agg_done, 1)
            nc.vector.tensor_copy(sfm[2][:, 0:2, :], bank[5][:, 0:2 * T].rearrange("p (k t) -> p k t", t=T)
                                  ).then_inc(agg_ready, 1)
            for n in range(2):
                cols = slice(n * BANK, (n + 1) * BANK)
                dve.wait_ge(up_done, n + 1)
                step(nc.vector.tensor_tensor(x[:, cols], x[:, cols], bank[n][0:T, :], ALU.add))
                st = nc.vector.bn_stats(stats[:, n, :], x[:, cols])
            step(st)
            center()
            take_xT(6, True)
            for c in range(2):
                nc.vector.tensor_copy(xT[:, 4 * c:4 * c + 4, :],
                                      bank[4 + c][:, 0:4 * T].rearrange("p (k t) -> p k t", t=T)).then_inc(xT_ready, 1)
            dve.wait_ge(xT_ready, 12)
            nc.vector.tensor_reduce(pooled[:], xT[:, :, :].rearrange("p k t -> p t k"), AX.X, ALU.add).then_inc(xT_ready, 1)
            sub_until(STREAM + 2, 0)
            for n in range(2):
                cols = slice(n * BANK, (n + 1) * BANK)
                dve.wait_ge(fin_done, n + 1)
                if n == 0:
                    dve.wait_ge(rstd_ready, 4)
                nc.vector.scalar_tensor_tensor(out=xc[:, cols], in0=bank[2 + n][0:T, :], scalar=rstd[:],
                                               in1=x[:, cols], op0=ALU.mult, op1=ALU.add).then_inc(fin_ready, 1)


def lay_out(i):
    import numpy as np

    a = {k: np.asarray(v) for k, v in i.items()}

    def tiles(w):
        return w.reshape(-1, P, w.shape[1]).transpose(1, 0, 2).reshape(P, -1)

    def halves(w):
        return [tiles(w[:, n * BANK:(n + 1) * BANK]) for n in range(w.shape[1] // BANK)]

    slabs = []
    for n in GNN:
        slabs += halves(a["L0_gnn_w" + n].T)
    slabs += halves(a["L0_ffn_W_exp"])
    con = a["L0_ffn_W_con"].reshape(GRP, NT, 2, D).transpose(2, 0, 1, 3).reshape(P, NT, D)
    slabs += [con[:, 4 * s:4 * s + 4].reshape(P, SLAB) for s in range(CON_SLABS)]
    slabs += halves(a["L1_ffn_weight"].T)

    def coefs(w):
        low, high = [], []
        for s in range(STAGES):
            v = w[s].reshape(NT, 2, 2 ** (5 - s), 2 ** s, 2, 2)
            low.append(v.transpose(1, 2, 5, 0, 4, 3).reshape(-1))
            v = w[s + 6].reshape(2 ** (5 - s), 2 ** s, NT, 2, 2, 2)
            high.append(v.transpose(3, 0, 5, 2, 4, 1).reshape(-1))
        return [np.stack(low), np.stack(high)]

    def by_feature(v, k):
        return v.reshape(k, P).T

    def edge_list(v):
        return np.concatenate([v, np.full(EP - E, -1, v.dtype)])

    att = np.zeros((P, 2, H1), np.float32)
    for h in range(H1):
        att[64 * (h % 2):64 * (h % 2) + 64, h // 2, h] = a["L1_gnn_att"].reshape(H1, 64)[h]
    r = {
        "x": a["x"],
        "stream": np.stack(slabs),
        "coef": np.stack(coefs(a["L0_ffn_up_weights"]) + coefs(a["L0_ffn_down_weights"])),
        "rows": np.stack([a["L0_gnn_bo"], a["L0_ffn_b_con"].reshape(D), a["L0_ffn_down_bias"].reshape(D)]),
        "by_feature": np.concatenate(
            [by_feature(a["L0_gnn_b" + n], KD) for n in ("q", "k", "iq", "ik", "v", "iv")]
            + [by_feature(a["L0_ffn_b_exp"], NT), by_feature(a["L0_ffn_up_bias"], NT),
               by_feature(a["L1_gnn_rms_w"], KD), att.reshape(P, 2 * H1)], axis=1),
        "etw": a["L0_gnn_edge_type_weights"].reshape(1, 4),
        "w_down": tiles(a["L1_gnn_W_down"]),
        "w_l": a["L1_gnn_Wl"].reshape(2, P, G1).transpose(1, 0, 2),
        "w_r": a["L1_gnn_Wr"].reshape(2, P, G1).transpose(1, 0, 2),
        "w_up": tiles(a["L1_gnn_W_up"]),
        "disha": a["L1_ffn_disha"],
        "ends": np.stack([edge_list(a["src"]), edge_list(a["dst"])]),
        "edge_cols": np.stack([edge_list(a[k]).reshape(ET, P).T for k in ("src", "dst", "edge_type_5")], axis=1),
    }
    return {k: np.ascontiguousarray(v) for k, v in r.items()}


def kernel(**inputs):
    import concourse.bacc as bacc
    from concourse.bass_utils import run_bass_kernel_spmd

    nc = bacc.Bacc("TRN2", target_bir_lowering=False, num_devices=1)
    arrays = lay_out(inputs)
    A = {k: nc.dram_tensor(f"in_{k}", v.shape, mybir.dt.from_np(v.dtype), kind="ExternalInput").ap()
         for k, v in arrays.items()}
    out = nc.dram_tensor("out", (T, D), F32, kind="ExternalOutput").ap()
    program(nc, A, out)
    r = run_bass_kernel_spmd(nc, [{f"in_{k}": v for k, v in arrays.items()}], core_ids=[0])
    return r.results[0]["out"]
```
